# Optimizing a Trainium2 kernel written in Bass

```python
import numpy as np
import jax
import jax.numpy as jnp

def _softmax(x, axis=-1):
    return jax.nn.softmax(x, axis=axis)

def _gelu(x):
    return jax.nn.gelu(x, approximate=True)

def _silu(x):
    return jax.nn.silu(x)

def _sigmoid(x):
    return jax.nn.sigmoid(x)

def _layernorm(x, axis=-1, eps=1e-05):
    m = jnp.mean(x, axis=axis, keepdims=True)
    v = jnp.var(x, axis=axis, keepdims=True)
    return (x - m) / jnp.sqrt(v + eps)

def _scatter_add(tgt, idx, src, axis=0):
    return tgt.at[idx].add(src)

def _segment_sum(src, seg, n):
    return jax.ops.segment_sum(src, seg, n)
kernel_name = 'mk_gnn_ffn_d2_gnn_r32_e3c783'

def setup_inputs(seed: int=0):
    np.random.seed(seed)
    _w = jnp.asarray

    def _rec_inputs():
        import jax
        import jax.numpy as jnp
        _gk = jax.random.key(seed)
        x = -0.0002117 + 1 * jax.random.normal(jax.random.fold_in(_gk, 1), (3125, 256), jnp.float32)
        src = jax.random.randint(jax.random.fold_in(_gk, 2), (50000,), 0, 3125, jnp.int32)
        dst = jax.random.randint(jax.random.fold_in(_gk, 3), (50000,), 0, 3125, jnp.int32)
        _o = jnp.argsort(dst, stable=True)
        src = src[_o]
        dst = dst[_o]
        return (x, src, dst)
    x, src, dst = _rec_inputs()

    def _L0_gnn_setup():
        import jax, jax.numpy as jnp
        import numpy as np
        N = 3125
        E = 25000
        EMB = 256
        HID = 256
        EPS = 1e-05

        def _pool_max(h, edge_src, edge_dst):
            pooled = jax.ops.segment_max(h[edge_src], edge_dst, num_segments=N)
            cnt = jax.ops.segment_sum(jnp.ones((edge_dst.shape[0],), h.dtype), edge_dst, num_segments=N)
            return jnp.where((cnt > 0)[:, None], pooled, jnp.zeros((), h.dtype))

        def _layernorm(x, g, b):
            mu = jnp.mean(x, axis=-1, keepdims=True)
            var = jnp.mean(jnp.square(x - mu), axis=-1, keepdims=True)
            return (x - mu) * jax.lax.rsqrt(var + EPS) * g + b
        key = jax.random.key(seed)
        ks = jax.random.split(key, 12)
        s = 0.05
        return {'embeddings': jax.random.normal(ks[0], (N, EMB), jnp.float32), 'edge_src': jax.random.randint(ks[1], (E,), 0, N, jnp.int32), 'edge_dst': jax.random.randint(ks[2], (E,), 0, N, jnp.int32), 'Wp1': jax.random.normal(ks[3], (HID, EMB), jnp.float32) * s, 'bp1': jnp.zeros((HID,), jnp.float32), 'Wm1': jax.random.normal(ks[4], (HID, EMB + HID), jnp.float32) * s, 'bm1': jnp.zeros((HID,), jnp.float32), 'Wm2': jax.random.normal(ks[5], (HID, 2 * HID), jnp.float32) * s, 'bm2': jnp.zeros((HID,), jnp.float32), 'Wm3': jax.random.normal(ks[6], (HID, 2 * HID), jnp.float32) * s, 'bm3': jnp.zeros((HID,), jnp.float32), 'ln2_g': jnp.ones((HID,), jnp.float32), 'ln2_b': jnp.zeros((HID,), jnp.float32), 'ln3_g': jnp.ones((HID,), jnp.float32), 'ln3_b': jnp.zeros((HID,), jnp.float32)}
    _L0_gnn_all = _L0_gnn_setup()
    _L0_gnn_in = {k: v for k, v in _L0_gnn_all.items() if k in ('Wp1', 'bp1', 'Wm1', 'bm1', 'Wm2', 'bm2', 'Wm3', 'bm3', 'ln2_g', 'ln2_b', 'ln3_g', 'ln3_b')}
    del _L0_gnn_all

    def _L0_ffn_setup():
        import jax, jax.numpy as jnp
        import numpy as np
        B, N, D = (16, 128, 256)
        NUM_EXPERTS, TOP_K, HEADS = (4, 2, 4)
        N_EDGES = 32768
        LN_EPS = 1e-05

        def _layernorm(x, g, b):
            mu = x.mean(-1, keepdims=True)
            var = ((x - mu) ** 2).mean(-1, keepdims=True)
            return (x - mu) * jax.lax.rsqrt(var + LN_EPS) * g + b

        def _forward(x, edge_index, W_gat, att_src, att_dst, b_gat, ln_gamma, ln_beta, W1, b1, W2, b2):
            Bc, Nc, Dc = x.shape
            M = Bc * Nc
            x_flat = x.reshape(M, Dc)
            h = (x_flat @ W_gat).reshape(M, HEADS, NUM_EXPERTS)
            loops = jnp.arange(M, dtype=edge_index.dtype)
            src = jnp.concatenate([edge_index[0], loops])
            dst = jnp.concatenate([edge_index[1], loops])
            a_src = (h * att_src).sum(-1)
            a_dst = (h * att_dst).sum(-1)
            e = jax.nn.leaky_relu(a_src[src] + a_dst[dst], negative_slope=0.2)
            e_max = jax.ops.segment_max(e, dst, num_segments=M)
            ee = jnp.exp(e - e_max[dst])
            denom = jax.ops.segment_sum(ee, dst, num_segments=M)
            alpha = ee / (denom[dst] + 1e-16)
            msg = h[src] * alpha[:, :, None]
            agg = jax.ops.segment_sum(msg, dst, num_segments=M).reshape(M, HEADS * NUM_EXPERTS) + b_gat
            scores = _layernorm(agg, ln_gamma, ln_beta).reshape(M, HEADS, NUM_EXPERTS).mean(1)
            scores = scores.reshape(Bc, Nc, NUM_EXPERTS)
            topk_s, topk_i = jax.lax.top_k(scores, TOP_K)
            w = jax.nn.softmax(topk_s, axis=-1)
            out = jnp.zeros_like(x)
            for ei in range(NUM_EXPERTS):
                g = jnp.where(topk_i == ei, w, 0.0).sum(-1)
                hh = jax.nn.gelu(x @ W1[ei] + b1[ei], approximate=False)
                out = out + g[..., None] * (hh @ W2[ei] + b2[ei])
            return out
        key = jax.random.key(seed)
        ks = jax.random.split(key, 8)
        s = 0.05
        return {'x': jax.random.normal(ks[0], (B, N, D), jnp.float32), 'W_gat': jax.random.normal(ks[1], (D, HEADS * NUM_EXPERTS), jnp.float32) * s, 'att_src': jax.random.normal(ks[2], (HEADS, NUM_EXPERTS), jnp.float32) * s, 'att_dst': jax.random.normal(ks[3], (HEADS, NUM_EXPERTS), jnp.float32) * s, 'b_gat': jnp.zeros((HEADS * NUM_EXPERTS,), jnp.float32), 'ln_gamma': jnp.ones((HEADS * NUM_EXPERTS,), jnp.float32), 'ln_beta': jnp.zeros((HEADS * NUM_EXPERTS,), jnp.float32), 'W1': jax.random.normal(ks[4], (NUM_EXPERTS, D, 2 * D), jnp.float32) * s, 'b1': jnp.zeros((NUM_EXPERTS, 2 * D), jnp.float32), 'W2': jax.random.normal(ks[5], (NUM_EXPERTS, 2 * D, D), jnp.float32) * s, 'b2': jnp.zeros((NUM_EXPERTS, D), jnp.float32), 'edge_index': jax.random.randint(ks[6], (2, N_EDGES), 0, B * N, jnp.int32)}
    _L0_ffn_all = _L0_ffn_setup()
    _L0_ffn_in = {k: v for k, v in _L0_ffn_all.items() if k in ('W_gat', 'att_src', 'att_dst', 'b_gat', 'ln_gamma', 'ln_beta', 'W1', 'b1', 'W2', 'b2', 'edge_index')}
    del _L0_ffn_all

    def _L1_gnn_setup():
        import jax, jax.numpy as jnp
        import numpy as np
        N_NODES = 3125
        CHANNELS = 256
        N_EDGES = 100000
        key = jax.random.key(seed)
        ks = jax.random.split(key, 7)
        C = CHANNELS
        x = jax.random.normal(ks[0], (N_NODES, C), dtype=jnp.float32)
        edge_index = jax.random.randint(ks[1], (2, N_EDGES), 0, N_NODES, dtype=jnp.int64)
        s = 1.0 / np.sqrt(C)
        W_l = jax.random.uniform(ks[2], (C, C), jnp.float32, -s, s)
        b_l = jax.random.uniform(ks[3], (C,), jnp.float32, -s, s)
        W_r = jax.random.uniform(ks[4], (C, C), jnp.float32, -s, s)
        gamma = jnp.ones((C,), jnp.float32)
        beta = jnp.zeros((C,), jnp.float32)
        return {'x': x, 'edge_index': edge_index, 'W_l': W_l, 'b_l': b_l, 'W_r': W_r, 'gamma': gamma, 'beta': beta}
    _L1_gnn_all = _L1_gnn_setup()
    _L1_gnn_in = {k: v for k, v in _L1_gnn_all.items() if k in ('W_l', 'b_l', 'W_r', 'gamma', 'beta')}
    del _L1_gnn_all

    def _L1_ffn_setup():
        import jax, jax.numpy as jnp
        import numpy as np
        B, S, H, F, E, K = (8, 128, 256, 512, 16, 2)
        EPS = 1e-05
        key = jax.random.key(seed)
        ks = jax.random.split(key, 9)
        sc = 0.02
        return {'x': jax.random.normal(ks[0], (B, S, H), dtype=jnp.float32), 'gate_w': jax.random.normal(ks[1], (H, E), dtype=jnp.float32) * sc, 'gate_b': jnp.zeros((E,), dtype=jnp.float32), 'w1': jax.random.normal(ks[2], (E, H, F), dtype=jnp.float32) * sc, 'b1': jnp.zeros((E, F), dtype=jnp.float32), 'w2': jax.random.normal(ks[3], (E, F, H), dtype=jnp.float32) * sc, 'b2': jnp.zeros((E, H), dtype=jnp.float32), 'gamma': jnp.ones((H,), dtype=jnp.float32), 'beta': jnp.zeros((H,), dtype=jnp.float32)}
    _L1_ffn_all = _L1_ffn_setup()
    _L1_ffn_in = {k: v for k, v in _L1_ffn_all.items() if k in ('gate_w', 'gate_b', 'w1', 'b1', 'w2', 'b2', 'gamma', 'beta')}
    del _L1_ffn_all
    return {'x': x, 'src': src, 'dst': dst, 'L0_gnn_Wp1': _L0_gnn_in['Wp1'], 'L0_gnn_bp1': _L0_gnn_in['bp1'], 'L0_gnn_Wm1': _L0_gnn_in['Wm1'], 'L0_gnn_bm1': _L0_gnn_in['bm1'], 'L0_gnn_Wm2': _L0_gnn_in['Wm2'], 'L0_gnn_bm2': _L0_gnn_in['bm2'], 'L0_gnn_Wm3': _L0_gnn_in['Wm3'], 'L0_gnn_bm3': _L0_gnn_in['bm3'], 'L0_gnn_ln2_g': _L0_gnn_in['ln2_g'], 'L0_gnn_ln2_b': _L0_gnn_in['ln2_b'], 'L0_gnn_ln3_g': _L0_gnn_in['ln3_g'], 'L0_gnn_ln3_b': _L0_gnn_in['ln3_b'], 'L0_ffn_W_gat': _L0_ffn_in['W_gat'], 'L0_ffn_att_src': _L0_ffn_in['att_src'], 'L0_ffn_att_dst': _L0_ffn_in['att_dst'], 'L0_ffn_b_gat': _L0_ffn_in['b_gat'], 'L0_ffn_ln_gamma': _L0_ffn_in['ln_gamma'], 'L0_ffn_ln_beta': _L0_ffn_in['ln_beta'], 'L0_ffn_W1': _L0_ffn_in['W1'], 'L0_ffn_b1': _L0_ffn_in['b1'], 'L0_ffn_W2': _L0_ffn_in['W2'], 'L0_ffn_b2': _L0_ffn_in['b2'], 'L0_ffn_edge_index': _L0_ffn_in['edge_index'], 'L1_gnn_W_l': _L1_gnn_in['W_l'], 'L1_gnn_b_l': _L1_gnn_in['b_l'], 'L1_gnn_W_r': _L1_gnn_in['W_r'], 'L1_gnn_gamma': _L1_gnn_in['gamma'], 'L1_gnn_beta': _L1_gnn_in['beta'], 'L1_ffn_gate_w': _L1_ffn_in['gate_w'], 'L1_ffn_gate_b': _L1_ffn_in['gate_b'], 'L1_ffn_w1': _L1_ffn_in['w1'], 'L1_ffn_b1': _L1_ffn_in['b1'], 'L1_ffn_w2': _L1_ffn_in['w2'], 'L1_ffn_b2': _L1_ffn_in['b2'], 'L1_ffn_gamma': _L1_ffn_in['gamma'], 'L1_ffn_beta': _L1_ffn_in['beta']}

def reference(x, src, dst, L0_gnn_Wp1, L0_gnn_bp1, L0_gnn_Wm1, L0_gnn_bm1, L0_gnn_Wm2, L0_gnn_bm2, L0_gnn_Wm3, L0_gnn_bm3, L0_gnn_ln2_g, L0_gnn_ln2_b, L0_gnn_ln3_g, L0_gnn_ln3_b, L0_ffn_W_gat, L0_ffn_att_src, L0_ffn_att_dst, L0_ffn_b_gat, L0_ffn_ln_gamma, L0_ffn_ln_beta, L0_ffn_W1, L0_ffn_b1, L0_ffn_W2, L0_ffn_b2, L0_ffn_edge_index, L1_gnn_W_l, L1_gnn_b_l, L1_gnn_W_r, L1_gnn_gamma, L1_gnn_beta, L1_ffn_gate_w, L1_ffn_gate_b, L1_ffn_w1, L1_ffn_b1, L1_ffn_w2, L1_ffn_b2, L1_ffn_gamma, L1_ffn_beta):
    import jax
    import jax.numpy as jnp

    def _L0_gnn_ref(embeddings, edge_src, edge_dst, Wp1, bp1, Wm1, bm1, Wm2, bm2, Wm3, bm3, ln2_g, ln2_b, ln3_g, ln3_b):
        import jax, jax.numpy as jnp
        import numpy as np
        N = 3125
        E = 25000
        EMB = 256
        HID = 256
        EPS = 1e-05

        def _pool_max(h, edge_src, edge_dst):
            pooled = jax.ops.segment_max(h[edge_src], edge_dst, num_segments=N)
            cnt = jax.ops.segment_sum(jnp.ones((edge_dst.shape[0],), h.dtype), edge_dst, num_segments=N)
            return jnp.where((cnt > 0)[:, None], pooled, jnp.zeros((), h.dtype))

        def _layernorm(x, g, b):
            mu = jnp.mean(x, axis=-1, keepdims=True)
            var = jnp.mean(jnp.square(x - mu), axis=-1, keepdims=True)
            return (x - mu) * jax.lax.rsqrt(var + EPS) * g + b
        h1 = jax.nn.relu(embeddings @ Wp1.T + bp1)
        p1 = _pool_max(h1, edge_src, edge_dst)
        x = jax.nn.relu(jnp.concatenate([embeddings, p1], axis=1) @ Wm1.T + bm1)
        p2 = _pool_max(x, edge_src, edge_dst)
        y2 = jax.nn.relu(jnp.concatenate([x, p2], axis=1) @ Wm2.T + bm2)
        x = _layernorm(y2 + x, ln2_g, ln2_b)
        p3 = _pool_max(x, edge_src, edge_dst)
        y3 = jax.nn.relu(jnp.concatenate([x, p3], axis=1) @ Wm3.T + bm3)
        x = _layernorm(y3 + x, ln3_g, ln3_b)
        return x

    def _L0_ffn_ref(x, W_gat, att_src, att_dst, b_gat, ln_gamma, ln_beta, W1, b1, W2, b2, edge_index):
        import jax, jax.numpy as jnp
        import numpy as np
        B, N, D = (16, 128, 256)
        NUM_EXPERTS, TOP_K, HEADS = (4, 2, 4)
        N_EDGES = 32768
        LN_EPS = 1e-05

        def _layernorm(x, g, b):
            mu = x.mean(-1, keepdims=True)
            var = ((x - mu) ** 2).mean(-1, keepdims=True)
            return (x - mu) * jax.lax.rsqrt(var + LN_EPS) * g + b

        def _forward(x, edge_index, W_gat, att_src, att_dst, b_gat, ln_gamma, ln_beta, W1, b1, W2, b2):
            Bc, Nc, Dc = x.shape
            M = Bc * Nc
            x_flat = x.reshape(M, Dc)
            h = (x_flat @ W_gat).reshape(M, HEADS, NUM_EXPERTS)
            loops = jnp.arange(M, dtype=edge_index.dtype)
            src = jnp.concatenate([edge_index[0], loops])
            dst = jnp.concatenate([edge_index[1], loops])
            a_src = (h * att_src).sum(-1)
            a_dst = (h * att_dst).sum(-1)
            e = jax.nn.leaky_relu(a_src[src] + a_dst[dst], negative_slope=0.2)
            e_max = jax.ops.segment_max(e, dst, num_segments=M)
            ee = jnp.exp(e - e_max[dst])
            denom = jax.ops.segment_sum(ee, dst, num_segments=M)
            alpha = ee / (denom[dst] + 1e-16)
            msg = h[src] * alpha[:, :, None]
            agg = jax.ops.segment_sum(msg, dst, num_segments=M).reshape(M, HEADS * NUM_EXPERTS) + b_gat
            scores = _layernorm(agg, ln_gamma, ln_beta).reshape(M, HEADS, NUM_EXPERTS).mean(1)
            scores = scores.reshape(Bc, Nc, NUM_EXPERTS)
            topk_s, topk_i = jax.lax.top_k(scores, TOP_K)
            w = jax.nn.softmax(topk_s, axis=-1)
            out = jnp.zeros_like(x)
            for ei in range(NUM_EXPERTS):
                g = jnp.where(topk_i == ei, w, 0.0).sum(-1)
                hh = jax.nn.gelu(x @ W1[ei] + b1[ei], approximate=False)
                out = out + g[..., None] * (hh @ W2[ei] + b2[ei])
            return out
        return _forward(x, edge_index, W_gat, att_src, att_dst, b_gat, ln_gamma, ln_beta, W1, b1, W2, b2)

    def _L1_gnn_ref(x, edge_index, W_l, b_l, W_r, gamma, beta):
        import jax, jax.numpy as jnp
        import numpy as np
        N_NODES = 3125
        CHANNELS = 256
        N_EDGES = 100000
        src, dst = (edge_index[0], edge_index[1])
        agg = jax.ops.segment_sum(x[src], dst, num_segments=x.shape[0])
        cnt = jax.ops.segment_sum(jnp.ones((edge_index.shape[1],), x.dtype), dst, num_segments=x.shape[0])
        agg = agg / jnp.maximum(cnt, 1.0)[:, None]
        h = agg @ W_l.T + b_l + x @ W_r.T
        mu = h.mean(axis=-1, keepdims=True)
        var = h.var(axis=-1, keepdims=True)
        hn = (h - mu) * jax.lax.rsqrt(var + 1e-05) * gamma + beta
        return x + jax.nn.relu(hn)

    def _L1_ffn_ref(x, gate_w, gate_b, w1, b1, w2, b2, gamma, beta):
        import jax, jax.numpy as jnp
        import numpy as np
        B, S, H, F, E, K = (8, 128, 256, 512, 16, 2)
        EPS = 1e-05
        gate_logits = x @ gate_w + gate_b
        topk_vals, topk_idx = jax.lax.top_k(gate_logits, K)
        topk_w = jax.nn.softmax(topk_vals, axis=-1)
        h = jax.nn.relu(jnp.einsum('bsh,ehf->bsef', x, w1) + b1)
        expert_out = jnp.einsum('bsef,efh->bseh', h, w2) + b2
        sel = jnp.take_along_axis(expert_out, topk_idx[:, :, :, None], axis=2)
        moe = jnp.sum(topk_w[..., None] * sel, axis=2)
        y = x + moe
        mu = jnp.mean(y, axis=-1, keepdims=True)
        var = jnp.var(y, axis=-1, keepdims=True)
        return (y - mu) / jnp.sqrt(var + EPS) * gamma + beta
    edge_index = jnp.stack([src, dst])
    x = x + _L0_gnn_ref(_layernorm(x, axis=-1), src, dst, L0_gnn_Wp1, L0_gnn_bp1, L0_gnn_Wm1, L0_gnn_bm1, L0_gnn_Wm2, L0_gnn_bm2, L0_gnn_Wm3, L0_gnn_bm3, L0_gnn_ln2_g, L0_gnn_ln2_b, L0_gnn_ln3_g, L0_gnn_ln3_b)
    x = x + _L0_ffn_ref(_layernorm(x, axis=-1)[None], L0_ffn_W_gat, L0_ffn_att_src, L0_ffn_att_dst, L0_ffn_b_gat, L0_ffn_ln_gamma, L0_ffn_ln_beta, L0_ffn_W1, L0_ffn_b1, L0_ffn_W2, L0_ffn_b2, L0_ffn_edge_index)[0]
    x = x + _L1_gnn_ref(_layernorm(x, axis=-1), edge_index, L1_gnn_W_l, L1_gnn_b_l, L1_gnn_W_r, L1_gnn_gamma, L1_gnn_beta)
    x = x + _L1_ffn_ref(_layernorm(x, axis=-1)[None], L1_ffn_gate_w, L1_ffn_gate_b, L1_ffn_w1, L1_ffn_b1, L1_ffn_w2, L1_ffn_b2, L1_ffn_gamma, L1_ffn_beta)[0]
    return x

_drawn_inputs = setup_inputs


def setup_inputs(seed=0):
    import zlib

    import numpy as np

    out = dict(_drawn_inputs(seed))
    spreads = {'L0_gnn_bp1': (0.0, 0.1),
     'L0_gnn_bm1': (0.0, 0.1),
     'L0_gnn_bm2': (0.0, 0.1),
     'L0_gnn_bm3': (0.0, 0.1),
     'L0_gnn_ln2_g': (1.0, 0.2),
     'L0_gnn_ln2_b': (0.0, 0.1),
     'L0_gnn_ln3_g': (1.0, 0.2),
     'L0_gnn_ln3_b': (0.0, 0.1),
     'L0_ffn_b_gat': (0.0, 0.1),
     'L0_ffn_ln_gamma': (1.0, 0.2),
     'L0_ffn_ln_beta': (0.0, 0.1),
     'L0_ffn_b1': (0.0, 0.1),
     'L0_ffn_b2': (0.0, 0.1),
     'L1_gnn_gamma': (1.0, 0.2),
     'L1_gnn_beta': (0.0, 0.1),
     'L1_ffn_gate_b': (0.0, 0.404),
     'L1_ffn_b1': (0.0, 0.8),
     'L1_ffn_b2': (0.0, 0.399),
     'L1_ffn_gamma': (1.0, 0.2),
     'L1_ffn_beta': (0.0, 0.302)}
    factors = {'L1_gnn_b_l': 4.094, 'L1_ffn_w1': 3.328}
    for name, (base, spread) in spreads.items():
        noise = np.random.default_rng([zlib.crc32(name.encode()), seed]).standard_normal(out[name].shape)
        drawn = base * np.exp(spread * noise) if base else spread * noise
        out[name] = jnp.asarray(drawn.astype(out[name].dtype))
    for name, factor in factors.items():
        out[name] = (out[name] * factor).astype(out[name].dtype)
    return out
```

```python
import concourse.bass as bass
from concourse import mybir
from contextlib import ExitStack

ALU = mybir.AluOpType
ACT = mybir.ActivationFunctionType
AX_X = mybir.AxisListType.X
F32 = mybir.dt.float32
I32 = mybir.dt.int32
BF16 = mybir.dt.bfloat16

P = 128
N = 3125
C = 256
NT = (N + P - 1) // P
NP = NT * P
LAST = N - (NT - 1) * P
NL = NT + 1
PAD_ROW = NL * P
SLOTS = 4
BLOCK = P * SLOTS
QUAD = 4
EPS = 1e-5
LOWEST = -3.0e38


class Chain:

    def __init__(self, eng, sem):
        self.eng, self.sem, self.n = eng, sem, 0

    def mark(self, ins):
        self.n += 1
        return ins.then_inc(self.sem, 1)

    def wait(self):
        self.eng.wait_ge(self.sem, self.n)

    def link(self, ins):
        self.mark(ins)
        self.wait()

    def restart(self):
        self.wait()
        self.eng.sem_clear(self.sem)
        self.n = 0


def hold(eng, sem, value, passed):
    eng.wait_ge(sem, value)
    eng.sem_inc(passed, 1)


class Kit:

    def __init__(self, nc, ctx, stage):
        self.nc, self.ctx, self.stage = nc, ctx, stage
        self.sems = []
        ctx.callback(self.clear)

    def clear(self):
        if self.sems:
            self.nc.clear_and_free_semaphores(self.sems)
            self.nc.all_engine_barrier(sem_only=True)

    def sb(self, name, shape, dt=F32):
        return self.ctx.enter_context(self.nc.sbuf_tensor(f"{self.stage}_{name}", shape, dt))

    def ps(self, name, shape, dt=F32):
        return self.ctx.enter_context(self.nc.psum_tensor(f"{self.stage}_{name}", shape, dt))

    def sem(self, name):
        self.sems.append(self.nc.alloc_semaphore(f"{self.stage}_{name}"))
        return self.sems[-1]

    def pool_dma_sem(self, name):
        return self.nc.alloc_semaphore(f"{self.stage}_{name}")


def slot_capacity(edges):
    most = (edges + edges // P) // SLOTS + 2 * NT
    return (most + QUAD * 40) // (QUAD * 40) * (QUAD * 40)


def build_constants(nc, const, sorted_x, pooled, cleared):
    with ExitStack() as ctx:
        k = Kit(nc, ctx, "const")
        s_set, s_pad, s_zero = k.sem("set"), k.sem("pad"), k.sem("zero")
        zeros = const["zeros"]
        block = ctx.enter_context(nc.Block())
        per = sorted_x.shape[0] // CLEARS // P

        @block.sync
        def _(sp):
            sp.wait_ge(s_zero, 1)
            for t in pooled:
                sp.dma_start(t[NP:NL * P, :], zeros[:, 0:C]).then_inc(s_pad, 16)
            for c in range(CLEARS):
                sp.dma_start(sorted_x[c * per * P:(c + 1) * per * P, :].rearrange("(p r) c -> p r c", p=P),
                             zeros[:, 0:C].rearrange("p (o c) -> p o c", o=1).to_broadcast([P, per, C])).then_inc(cleared, 16)
            sp.wait_ge(s_pad, 32)

        @block.gpsimd
        def _(pool):
            pool.memset(zeros[:, :], 0.0).then_inc(s_zero, 1)
            pool.memset(const["ident"][:, :], 0.0).then_inc(s_set, 1)
            pool.memset(const["before"][:, :], 1.0).then_inc(s_set, 1)
            pool.memset(const["after"][:, :], 1.0).then_inc(s_set, 1)
            pool.memset(const["ones"][:, :], 1.0).then_inc(s_set, 1)
            pool.memset(const["zero16"][:, :], 0.0).then_inc(s_set, 1)
            pool.memset(const["eps"][:, :], EPS).then_inc(s_set, 1)
            pool.wait_ge(s_set, 6)
            pool.affine_select(out=const["ident"][:, :], in_=const["ident"][:, :], compare_op=ALU.not_equal,
                               fill=1.0, base=0, pattern=[[-1, P]], channel_multiplier=1).then_inc(s_set, 1)
            pool.affine_select(out=const["before"][:, :], in_=const["before"][:, :], compare_op=ALU.is_gt,
                               fill=0.0, base=0, pattern=[[-1, P]], channel_multiplier=1).then_inc(s_set, 1)
            pool.affine_select(out=const["after"][:, :], in_=const["after"][:, :], compare_op=ALU.is_gt,
                               fill=0.0, base=0, pattern=[[1, P]], channel_multiplier=-1).then_inc(s_set, 1)
            pool.iota(const["ramp"][:, :], pattern=[[1, P]], base=0, channel_multiplier=0,
                      allow_small_or_imprecise_dtypes=True).then_inc(s_set, 1)
            pool.iota(const["row"][:, :], pattern=[[0, 1]], base=0, channel_multiplier=1,
                      allow_small_or_imprecise_dtypes=True).then_inc(s_set, 1)
            pool.wait_ge(s_set, 11)


def build_slots(nc, const, name, dst, src, edges, rows, slot_table, tile_of_block, ranked, perm, degree, turns):
    T = edges // rows
    CH = 20 if T % 20 == 0 else 16
    HALF = CH // 2
    NCH = T // CH
    assert T * rows == edges and NCH * CH == T
    STRIPE = 100 if T % 100 == 0 else P
    NS = T // STRIPE
    cap = slot_capacity(edges)
    TURN0 = 40 * QUAD
    ident, before, ramp, row, ones, zero16 = (const[k] for k in ("ident", "before", "ramp", "row", "ones", "zero16"))
    dst_rows = dst.rearrange("(t e) -> t e", e=rows)
    src_rows = src.rearrange("(t e) -> t e", e=rows)

    with ExitStack() as outer:
        k0 = Kit(nc, outer, name)
        dst_col = k0.sb("dst_col", [P, T])
        src_col = k0.sb("src_col", [P, T], I32)
        hi_col = k0.sb("hi_col", [P, T])
        lo_col = k0.sb("lo_col", [P, T])
        base = k0.sb("base", [P, NT])

        with ExitStack() as ctx:
            k = Kit(nc, ctx, name + "c")
            raw = k.sb("raw", [P, 2, NS, rows], I32)
            rawf = k.sb("rawf", [P, 2, NS, rows])
            hi_i = k.sb("hi_i", [P, T], I32)
            dst_i = k.sb("dst_i", [P, T], I32)
            turned = k.ps("turned", [P, 2, 512])
            s_raw, s_f, s_t, s_c, s_v = (k.sem(n) for n in ("raw", "f", "t", "c", "v"))
            block = ctx.enter_context(nc.Block())

            @block.sync
            def _(sp):
                for w, list_rows in enumerate((dst_rows, src_rows)):
                    sp.dma_start(raw[0:STRIPE, w, :, :], list_rows.rearrange("(s t) e -> t s e", t=STRIPE)).then_inc(s_raw, 16)
                sp.wait_ge(s_raw, 32)

            @block.tensor
            def _(pe):
                pe.wait_ge(s_f, 1)
                for w in range(2):
                    for s in range(NS):
                        nc.tensor.transpose(turned[0:rows, w, STRIPE * s:STRIPE * s + STRIPE], rawf[0:STRIPE, w, s, :],
                                            ident[0:STRIPE, 0:STRIPE]).then_inc(s_t, 1)

            @block.vector
            def _(dve):
                chain = Chain(dve, s_v)
                dve.wait_ge(s_raw, 32)
                dve.tensor_copy(rawf[0:STRIPE, :, :, :], raw[0:STRIPE, :, :, :]).then_inc(s_f, 1)
                dve.wait_ge(s_t, 2 * NS)
                chain.mark(dve.tensor_copy(dst_col[0:rows, :], turned[0:rows, 0, 0:T]))
                chain.mark(dve.tensor_copy(dst_i[0:rows, :], turned[0:rows, 0, 0:T]))
                chain.link(dve.tensor_copy(src_col[0:rows, :], turned[0:rows, 1, 0:T]))
                chain.link(dve.tensor_scalar(hi_i[0:rows, :], dst_i[0:rows, :], 7, None, ALU.logical_shift_right))
                chain.link(dve.tensor_copy(hi_col[0:rows, :], hi_i[0:rows, :]))
                chain.link(dve.scalar_tensor_tensor(out=lo_col[0:rows, :], in0=hi_col[0:rows, :], scalar=-float(P),
                                                    in1=dst_col[0:rows, :], op0=ALU.mult, op1=ALU.add))

        with ExitStack() as ctx:
            k = Kit(nc, ctx, name + "h")
            oh_lo = k.sb("oh_lo", [P, 2, HALF, P], BF16)
            oh_hi = k.sb("oh_hi", [P, 2, HALF, NT], BF16)
            counts = k.ps("counts", [P, NT])
            s_oh, s_used, s_done, s_pass = (k.sem(n) for n in ("oh", "used", "done", "pass"))
            block = ctx.enter_context(nc.Block())

            @block.vector
            def _(dve):
                with dve.Fori(0, NCH) as c:
                    for h in range(2):
                        hold(dve, s_used, 2 * c + h + 1, s_pass)
                        at = bass.ds(c * CH + h * HALF, HALF)
                        dve.tensor_tensor(oh_lo[0:rows, h, :, :],
                                          lo_col[0:rows, at].rearrange("p (t o) -> p t o", o=1).to_broadcast([rows, HALF, P]),
                                          ramp[0:rows, :].rearrange("p (o n) -> p o n", o=1).to_broadcast([rows, HALF, P]),
                                          ALU.is_equal).then_inc(s_oh, 1)
                        dve.tensor_tensor(oh_hi[0:rows, h, :, :],
                                          hi_col[0:rows, at].rearrange("p (t o) -> p t o", o=1).to_broadcast([rows, HALF, NT]),
                                          ramp[0:rows, 0:NT].rearrange("p (o n) -> p o n", o=1).to_broadcast([rows, HALF, NT]),
                                          ALU.is_equal).then_inc(s_oh, 1)
                dve.wait_ge(s_done, 1)
                dve.tensor_copy(degree[:, :], counts[:, :]).then_inc(s_done, 1)

            @block.tensor
            def _(pe):
                pe.sem_inc(s_used, 2)
                nc.tensor.matmul(counts[:, :], zero16[:, 0:P], zero16[:, 0:NT], start=True, stop=False,
                                 skip_group_check=True)
                with pe.Fori(0, NCH) as c:
                    for h in range(2):
                        pe.wait_ge(s_oh, 4 * c + 2 * h + 2)
                        for j in range(HALF):
                            last = nc.tensor.matmul(counts[:, :], oh_lo[0:rows, h, j, :], oh_hi[0:rows, h, j, :],
                                                    start=False, stop=False, skip_group_check=True)
                        last.then_inc(s_used, 1)
                nc.tensor.matmul(counts[:, :], zero16[:, 0:P], zero16[:, 0:NT], start=False, stop=True,
                                 skip_group_check=True).then_inc(s_done, 1)

        with ExitStack() as ctx:
            k = Kit(nc, ctx, name + "r")
            key = k.sb("key", [P, NT])
            node = k.sb("node", [P, NT])
            key_rows = k.sb("key_rows", [NT, P])
            all_keys = k.sb("all_keys", [P, NP])
            larger = k.sb("larger", [P, NP])
            rank = k.sb("rank", [P, NT])
            rank_i = k.sb("rank_i", [P, NT], I32)
            meta = k.sb("meta", [P, NT, 2], I32)
            ranked_in = k.sb("ranked_in", [P, NT, 2], I32)
            deg_rows = k.sb("deg_rows", [NT, P, 2], I32)
            deg_rows_f = k.sb("deg_rows_f", [NT, P])
            most = k.sb("most", [NT, 1])
            most_i = k.sb("most_i", [NT, 1], I32)
            blocks = k.sb("blocks", [NT, 1])
            diag = k.sb("diag", [NT, NT])
            tile_blocks = k.sb("tile_blocks", [P, NT])
            ends = k.sb("ends", [P, NT + 1])
            turn_i = k.sb("turn_i", [P, 2], I32)
            limits = k.sb("limits", [P, NT])
            past = k.sb("past", [P, NT, NT])
            tile_i = k.sb("tile_i", [P, NT], I32)
            tile_f = k.sb("tile_f", [P, NT])
            CB = cap // P
            block_no = k.sb("block_no", [P, CB])
            block_past = k.sb("block_past", [P, CB])
            block_i = k.sb("block_i", [P, CB], I32)
            empty = k.sb("empty", [P, TURN0 * SLOTS], I32)
            keys_t = k.ps("keys_t", [NT, P])
            blocks_t = k.ps("blocks_t", [P, NT])
            (s_v, s_iota, s_kt, s_kr, s_kd, s_ka, s_rk, s_rd, s_bt, s_bo, s_em, s_tn, s_pass) = (
                k.sem(n) for n in ("v", "iota", "kt", "kr", "kd", "ka", "rk", "rd", "bt", "bo", "em", "tn", "pass"))
            s_scat = k.pool_dma_sem("scat")
            key_dram = nc.dram_tensor(f"{name}_keys", [NP], F32, kind="Internal").ap()
            block = ctx.enter_context(nc.Block())

            @block.gpsimd
            def _(pool):
                pool.iota(node[:, :], pattern=[[P, NT]], base=0, channel_multiplier=1,
                          allow_small_or_imprecise_dtypes=True).then_inc(s_iota, 1)
                pool.iota(block_no[:, :], pattern=[[1, CB]], base=0, channel_multiplier=CB,
                          allow_small_or_imprecise_dtypes=True).then_inc(s_iota, 1)
                pool.iota(limits[:, :], pattern=[[P, NT]], base=P, channel_multiplier=0,
                          allow_small_or_imprecise_dtypes=True).then_inc(s_iota, 1)
                pool.memset(empty[:, :], PAD_ROW).then_inc(s_iota, 1)
                pool.wait_ge(s_rk, 1)
                for t in range(NT):
                    pool.indirect_dma_start(ranked[:, :], bass.IndirectOffsetOnAxis(ap=rank_i[:, t:t + 1], axis=0),
                                            meta[:, t, :], None).then_inc(s_scat, 16)

            @block.tensor
            def _(pe):
                pe.wait_ge(s_v, 3)
                nc.tensor.transpose(keys_t[:, :], key[:, :], ident[:, :]).then_inc(s_kt, 1)
                pe.wait_ge(s_bt, 1)
                nc.tensor.matmul(blocks_t[:, :], ones[0:NT, :], diag[:, :], start=True, stop=True).then_inc(s_bt, 1)

            @block.sync
            def _(sp):
                sp.wait_ge(s_kr, 1)
                sp.dma_start(key_dram.rearrange("(t p) -> t p", p=P), key_rows[:, :]).then_inc(s_kd, 16)
                sp.wait_ge(s_kd, 16)
                sp.dma_start(all_keys[:, :], key_dram.rearrange("(o n) -> o n", o=1).to_broadcast([P, NP])).then_inc(s_ka, 16)
                sp.wait_ge(s_scat, 16 * NT)
                sp.dma_start(deg_rows[:, :, :], ranked.rearrange("(t p) w -> t p w", p=P)).then_inc(s_rd, 16)
                sp.dma_start(ranked_in[:, :, :], ranked.rearrange("(t p) w -> p t w", p=P)).then_inc(s_rd, 16)
                sp.wait_ge(s_tn, 1)
                sp.wait_ge(s_iota, 4)
                n_clear = sp.value_load(turn_i[0:1, 1:2], min_val=1, max_val=cap // TURN0)
                with sp.Fori(0, n_clear) as c:
                    sp.dma_start(slot_table[bass.ds(c * (TURN0 * BLOCK), TURN0 * BLOCK)].rearrange("(p n) -> p n", p=P),
                                 empty[:, :]).then_inc(s_em, 16)
                    hold(sp, s_em, c * 16 + 16, s_pass)
                sp.wait_ge(s_bo, 1)
                sp.dma_start(tile_of_block.rearrange("(p n) -> p n", p=P), block_i[:, :]).then_inc(s_bo, 16)
                sp.wait_ge(s_bo, 17)
                sp.wait_ge(s_rd, 32)

            @block.vector
            def _(dve):
                chain = Chain(dve, s_v)
                dve.wait_ge(s_iota, 3)
                chain.link(dve.tensor_scalar(key[:, :], degree[:, :], 4095.0, 4096.0, ALU.min, ALU.mult))
                chain.link(dve.tensor_tensor(key[:, :], key[:, :], node[:, :], ALU.subtract))
                chain.link(dve.tensor_scalar(key[:, :], key[:, :], 4095.0, None, ALU.add))
                chain.mark(dve.tensor_copy(meta[:, :, 0], degree[:, :]))
                chain.mark(dve.tensor_copy(meta[:, :, 1], node[:, :]))
                dve.wait_ge(s_kt, 1)
                dve.tensor_copy(key_rows[:, :], keys_t[:, :]).then_inc(s_kr, 1)
                dve.wait_ge(s_ka, 16)
                for t in range(NT):
                    chain.mark(dve.tensor_scalar(larger[:, :], all_keys[:, :], key[:, t:t + 1], 0.0, ALU.is_gt, ALU.add,
                                                 accum_out=rank[:, t:t + 1]))
                    chain.wait()
                dve.tensor_copy(rank_i[:, :], rank[:, :]).then_inc(s_rk, 1)
                dve.wait_ge(s_rk, 1)
                chain.link(dve.tensor_scalar(tile_i[:, :], rank_i[:, :], 7, None, ALU.logical_shift_right))
                chain.link(dve.tensor_copy(tile_f[:, :], tile_i[:, :]))
                dve.wait_ge(s_rd, 32)
                chain.mark(dve.tensor_copy(perm[:, :], ranked_in[:, :, 1]))
                chain.mark(dve.tensor_copy(degree[:, :], ranked_in[:, :, 0]))
                chain.link(dve.tensor_copy(deg_rows_f[:, :], deg_rows[:, :, 0]))
                chain.link(dve.tensor_reduce(most[:, :], deg_rows_f[:, :], AX_X, ALU.max))
                chain.link(dve.tensor_scalar(most[:, :], most[:, :], SLOTS - 1.0, None, ALU.add))
                chain.link(dve.tensor_copy(most_i[:, :], most[:, :]))
                chain.link(dve.tensor_scalar(most_i[:, :], most_i[:, :], 2, None, ALU.logical_shift_right))
                chain.link(dve.tensor_copy(blocks[:, :], most_i[:, :]))
                chain.mark(dve.tensor_scalar(diag[:, :], ident[0:NT, 0:NT], blocks[:, 0:1], None, ALU.mult))
                chain.wait()
                dve.sem_inc(s_bt, 1)
                dve.wait_ge(s_bt, 2)
                chain.link(dve.tensor_copy(tile_blocks[:, :], blocks_t[:, :]))
                chain.link(dve.tensor_tensor_scan(ends[:, 0:NT], ones[:, 0:NT], tile_blocks[:, :], 0.0, ALU.mult, ALU.add))
                chain.link(dve.tensor_scalar(ends[:, NT:NT + 1], ends[:, NT - 1:NT], QUAD - 1.0, float(QUAD), ALU.add, ALU.max))
                chain.link(dve.tensor_copy(turn_i[:, 0:1], ends[:, NT:NT + 1]))
                chain.mark(dve.tensor_scalar(turns[0:1, 0:1], turn_i[0:1, 0:1], 2, None, ALU.logical_shift_right))
                chain.link(dve.tensor_scalar(ends[:, NT:NT + 1], ends[:, NT - 1:NT], TURN0 + QUAD - 1.0, 1.0 / TURN0, ALU.add, ALU.mult))
                chain.link(dve.tensor_scalar(ends[:, NT:NT + 1], ends[:, NT:NT + 1], 1.0, float(cap // TURN0), ALU.max, ALU.min))
                chain.link(dve.tensor_copy(turn_i[:, 1:2], ends[:, NT:NT + 1]))
                dve.sem_inc(s_tn, 1)
                chain.link(dve.tensor_tensor(
                    past[:, :, :], rank[:, :].rearrange("p (t o) -> p t o", o=1).to_broadcast([P, NT, NT]),
                    limits[:, :].rearrange("p (o j) -> p o j", o=1).to_broadcast([P, NT, NT]), ALU.is_ge))
                chain.link(dve.tensor_tensor(
                    past[:, :, :], past[:, :, :],
                    tile_blocks[:, :].rearrange("p (o j) -> p o j", o=1).to_broadcast([P, NT, NT]), ALU.mult))
                chain.link(dve.tensor_reduce(base[:, :], past[:, :, :], AX_X, ALU.add))
                chain.link(dve.tensor_scalar(base[:, :], base[:, :], float(P), None, ALU.mult))
                chain.link(dve.tensor_tensor(base[:, :], base[:, :], rank[:, :], ALU.add))
                chain.link(dve.scalar_tensor_tensor(out=base[:, :], in0=tile_f[:, :], scalar=-float(P), in1=base[:, :],
                                                    op0=ALU.mult, op1=ALU.add))
                chain.link(dve.tensor_scalar(base[:, :], base[:, :], float(SLOTS), None, ALU.mult))
                chain.link(dve.tensor_scalar(block_past[:, :], block_no[:, :], ends[:, 0:1], None, ALU.is_ge))
                for t in range(1, NT):
                    chain.link(dve.scalar_tensor_tensor(out=block_past[:, :], in0=block_no[:, :], scalar=ends[:, t:t + 1],
                                                        in1=block_past[:, :], op0=ALU.is_ge, op1=ALU.add))
                chain.link(dve.tensor_copy(block_i[:, :], block_past[:, :]))
                dve.sem_inc(s_bo, 1)

        with ExitStack() as ctx:
            k = Kit(nc, ctx, name + "s")
            dst_bc = k.sb("dst_bc", [P, 2, HALF * rows], I32)
            dst_lo = k.sb("dst_lo", [P, 2, HALF * rows], I32)
            oh_lo = k.sb("oh_lo", [P, 2, HALF, P], BF16)
            oh_hi = k.sb("oh_hi", [P, 2, HALF, NT], BF16)
            ohf_hi = k.sb("ohf_hi", [P, HALF, NT])
            oh_lo_t = k.sb("oh_lo_t", [P, 2, HALF * rows])
            same = k.sb("same", [P, P])
            in_tile = k.sb("in_tile", [P, 2, HALF])
            lookup = k.sb("lookup", [P, 2, 2, NT])
            picked = k.sb("picked", [P, HALF, 2, NT])
            found = k.sb("found", [P, HALF, 2])
            nth = k.sb("nth", [P, HALF])
            nth_i = k.sb("nth_i", [P, HALF], I32)
            quad = k.sb("quad", [P, HALF])
            place = k.sb("place", [P, HALF])
            slot_i = k.sb("slot_i", [P, 2, HALF], I32)
            src_i = k.sb("src_i", [P, 2, HALF], I32)
            primed = k.sb("primed", [1, 2], I32)
            counts = k.ps("counts", [P, NT])
            got = k.ps("got", [P, 2, 512])
            (s_bc, s_oh, s_lt, s_cnt, s_snap, s_got, s_slot, s_looked, s_ch, s_pass, s_pass2, s_pass3,
             s_pass4, s_free, s_base) = (
                k.sem(n) for n in ("bc", "oh", "lt", "cnt", "snap", "got", "slot", "looked", "ch", "pass", "pass2",
                                   "pass3", "pass4", "free", "base"))
            s_st = (k.pool_dma_sem("st0"), k.pool_dma_sem("st1"))
            block = ctx.enter_context(nc.Block())

            @block.sync
            def _(sp):
                with sp.Fori(0, NCH) as c:
                    for h in range(2):
                        hold(sp, s_free, 2 * c + h + 1, s_pass4)
                        sp.dma_start(dst_bc[:, h, :],
                                     dst[bass.ds((c * CH + h * HALF) * rows, HALF * rows)]
                                     .rearrange("(o n) -> o n", o=1).to_broadcast([P, HALF * rows])).then_inc(s_bc, 16)
                        hold(sp, s_bc, (2 * c + h + 1) * 16, s_pass4)

            @block.vector
            def _(dve):
                chain = Chain(dve, s_ch)
                dve.sem_inc(s_free, 2)
                dve.tensor_copy(lookup[:, 0, 0, :], base[:, :]).then_inc(s_base, 1)
                dve.tensor_copy(lookup[:, 1, 0, :], base[:, :]).then_inc(s_base, 1)
                with dve.Fori(0, NCH) as c:
                    for h in range(2):
                        at = bass.ds(c * CH + h * HALF, HALF)
                        hold(dve, s_got, 2 * c + h + 1, s_pass)
                        dve.tensor_tensor(oh_lo[0:rows, h, :, :],
                                          lo_col[0:rows, at].rearrange("p (t o) -> p t o", o=1).to_broadcast([rows, HALF, P]),
                                          ramp[0:rows, :].rearrange("p (o n) -> p o n", o=1).to_broadcast([rows, HALF, P]),
                                          ALU.is_equal).then_inc(s_oh, 1)
                        dve.tensor_tensor(oh_hi[0:rows, h, :, :],
                                          hi_col[0:rows, at].rearrange("p (t o) -> p t o", o=1).to_broadcast([rows, HALF, NT]),
                                          ramp[0:rows, 0:NT].rearrange("p (o n) -> p o n", o=1).to_broadcast([rows, HALF, NT]),
                                          ALU.is_equal).then_inc(s_oh, 1)
                        hold(dve, s_bc, (2 * c + h + 1) * 16, s_pass)
                        chain.link(dve.tensor_scalar(dst_lo[:, h, :], dst_bc[:, h, :], P - 1, None, ALU.bitwise_and))
                        dve.tensor_scalar(oh_lo_t[:, h, :], dst_lo[:, h, :], row[:, 0:1], None, ALU.is_equal).then_inc(s_lt, 1)
                        for j in range(HALF):
                            col = dst_col[0:rows, bass.ds(c * CH + h * HALF + j, 1)]
                            chain.link(dve.scalar_tensor_tensor(
                                out=same[0:rows, 0:rows], in0=dst_bc[0:rows, h, j * rows:(j + 1) * rows], scalar=col,
                                in1=before[0:rows, 0:rows], op0=ALU.is_equal, op1=ALU.mult,
                                accum_out=in_tile[0:rows, h, j:j + 1]))
                        dve.sem_inc(s_free, 1)
                        chain.link(dve.tensor_copy(ohf_hi[0:rows, :, :], oh_hi[0:rows, h, :, :]))
                        hold(dve, s_got, 2 * c + h + 3, s_pass)
                        chain.link(dve.tensor_tensor(
                            picked[0:rows, :, :, :].rearrange("p t w n -> p w t n"),
                            got[0:rows, h, 0:HALF * 2 * NT].rearrange("p (t w n) -> p w t n", w=2, n=NT),
                            ohf_hi[0:rows, :, :].rearrange("p (o t) n -> p o t n", o=1).to_broadcast([rows, 2, HALF, NT]), ALU.mult))
                        chain.link(dve.tensor_reduce(found[0:rows, :, :], picked[0:rows, :, :, :], AX_X, ALU.add))
                        chain.link(dve.tensor_tensor(nth[0:rows, :], found[0:rows, :, 1], in_tile[0:rows, h, :], ALU.add))
                        chain.link(dve.tensor_copy(nth_i[0:rows, :], nth[0:rows, :]))
                        chain.link(dve.tensor_scalar(nth_i[0:rows, :], nth_i[0:rows, :], 2, None, ALU.logical_shift_right))
                        chain.link(dve.tensor_copy(quad[0:rows, :], nth_i[0:rows, :]))
                        chain.link(dve.tensor_tensor(place[0:rows, :], found[0:rows, :, 0], nth[0:rows, :], ALU.add))
                        hold(dve, s_st[h], 16 * HALF * c + 16, s_pass)
                        chain.mark(dve.scalar_tensor_tensor(out=slot_i[0:rows, h, :], in0=quad[0:rows, :],
                                                            scalar=float(BLOCK - SLOTS), in1=place[0:rows, :],
                                                            op0=ALU.mult, op1=ALU.add))
                        chain.link(dve.tensor_copy(src_i[0:rows, h, :], src_col[0:rows, at]))
                        dve.sem_inc(s_slot, 1)
                    chain.restart()

            @block.tensor
            def _(pe):
                pe.sem_inc(s_got, 2)
                nc.tensor.matmul(counts[:, :], zero16[:, 0:P], zero16[:, 0:NT], start=True, stop=False,
                                 skip_group_check=True).then_inc(s_cnt, 1)
                pe.wait_ge(s_base, 2)
                with pe.Fori(0, NCH) as c:
                    for h in range(2):
                        hold(pe, s_oh, 4 * c + 2 * h + 2, s_pass2)
                        hold(pe, s_lt, 2 * c + h + 1, s_pass2)
                        for j in range(HALF):
                            n = c * CH + h * HALF + j
                            pe.wait_ge(s_snap, n + 1)
                            nc.tensor.matmul(counts[:, :], oh_lo[0:rows, h, j, :], oh_hi[0:rows, h, j, :],
                                             start=False, stop=False, skip_group_check=True).then_inc(s_cnt, 1)
                            last = nc.tensor.matmul(got[0:rows, h, j * 2 * NT:(j + 1) * 2 * NT],
                                                    oh_lo_t[:, h, j * rows:(j + 1) * rows],
                                                    lookup[:, j % 2, :, :].rearrange("p w n -> p (w n)"),
                                                    start=True, stop=True, skip_group_check=True)
                            if j == HALF - 1:
                                last.then_inc(s_got, 1)
                            else:
                                last.then_inc(s_looked, 1)

            @block.scalar
            def _(act):
                with act.Fori(0, NCH) as c:
                    for h in range(2):
                        for j in range(HALF):
                            n = c * CH + h * HALF + j
                            act.wait_ge(s_cnt, n + 1)
                            act.activation(lookup[:, j % 2, 1, :], counts[:, :], ACT.Copy).then_inc(s_snap, 1)

            @block.gpsimd
            def _(pool):
                for h in range(2):
                    pool.dma_start(primed[0:1, h:h + 1], dst[0:1].rearrange("(o n) -> o n", o=1)).then_inc(s_st[h], 16)
                with pool.Fori(0, NCH) as c:
                    for h in range(2):
                        hold(pool, s_slot, 2 * c + h + 1, s_pass3)
                        for j in range(HALF):
                            pool.indirect_dma_start(
                                slot_table.rearrange("(n o) -> n o", o=1),
                                bass.IndirectOffsetOnAxis(ap=slot_i[0:rows, h, j:j + 1], axis=0),
                                src_i[0:rows, h, j:j + 1], None).then_inc(s_st[h], 16)
                for h in range(2):
                    pool.wait_ge(s_st[h], 16 + 16 * HALF * NCH)


def gather_pass(nc, const, name, table, slot_table, tile_of_block, turns, perm, weight, pooled, op, init):
    RING = 2 * SLOTS
    with ExitStack() as ctx:
        k = Kit(nc, ctx, name)
        acc = k.sb("acc", [P, NT + 1, C])
        rows = k.sb("rows", [P, RING, C])
        slots = k.sb("slots", [P, 2, 2, SLOTS], I32)
        tiles = k.sb("tiles", [1, 2, 2], I32)
        s_row = [k.pool_dma_sem(f"row{r}") for r in range(RING)]
        s_slots, s_used, s_acc, s_init, s_fin, s_pass = (
            k.sem(n) for n in ("slots", "used", "acc", "init", "fin", "pass"))
        s_out = k.pool_dma_sem("out")
        table_of_blocks = slot_table.rearrange("(b p s) -> b p s", p=P, s=SLOTS)
        block = ctx.enter_context(nc.Block())

        @block.sync
        def _(sp):
            n = sp.value_load(turns[0:1, 0:1], min_val=1, max_val=slot_capacity(50000) // QUAD)
            with sp.Fori(0, n) as q:
                for h in range(2):
                    hold(sp, s_used, 4 * q + 2 * h + 2, s_pass)
                    b = q * QUAD + 2 * h
                    sp.dma_start(slots[:, h, :, :], table_of_blocks[bass.ds(b, 2), :, :].rearrange("b p s -> p b s")
                                 ).then_inc(s_slots, 16)
                    sp.dma_start(tiles[0:1, h, :], tile_of_block[bass.ds(b, 2)].rearrange("(o n) -> o n", o=1)
                                 ).then_inc(s_slots, 16)
                    hold(sp, s_slots, 64 * q + 32 * h + 32, s_pass)

        @block.gpsimd
        def _(pool):
            n = pool.value_load(turns[0:1, 0:1], min_val=1, max_val=slot_capacity(50000) // QUAD)
            with pool.Fori(0, n) as q:
                for h in range(2):
                    hold(pool, s_slots, 64 * q + 32 * h + 32, s_pass)
                    for u in range(2):
                        hold(pool, s_used, 4 * q + 2 * h + u + 3, s_pass)
                        for s in range(SLOTS):
                            r = u * SLOTS + s
                            pool.indirect_dma_start(rows[:, r, :], None, table[:, :],
                                                    bass.IndirectOffsetOnAxis(ap=slots[:, h, u, s:s + 1], axis=0)
                                                    ).then_inc(s_row[r], 16)
            for t in range(NT):
                pool.wait_ge(s_fin, t + 1)
                pool.indirect_dma_start(pooled[:, :], bass.IndirectOffsetOnAxis(ap=perm[:, t:t + 1], axis=0),
                                        acc[:, t, :], None).then_inc(s_out, 16)
            pool.wait_ge(s_out, 16 * NT)

        @block.vector
        def _(dve):
            chain = Chain(dve, s_acc)
            dve.memset(acc[:, :, :], init).then_inc(s_init, 1)
            dve.wait_ge(s_init, 1)
            dve.sem_inc(s_used, 4)
            n = dve.value_load(turns[0:1, 0:1], min_val=1, max_val=slot_capacity(50000) // QUAD)
            with dve.Fori(0, n) as q:
                for h in range(2):
                    hold(dve, s_slots, 64 * q + 32 * h + 32, s_pass)
                    for u in range(2):
                        t = dve.value_load(tiles[0:1, h, u:u + 1], min_val=0, max_val=NT)
                        into = acc[:, bass.ds(t, 1), :].rearrange("p o c -> p (o c)")
                        for s in range(SLOTS):
                            r = u * SLOTS + s
                            dve.wait_ge(s_row[r], 32 * q + 16 * h + 16)
                            chain.link(dve.tensor_tensor(into, into, rows[:, r, :], op))
                        dve.sem_inc(s_used, 1)
                chain.restart()
            for t in range(NT):
                if weight is None:
                    dve.sem_inc(s_fin, 1)
                else:
                    dve.tensor_scalar(acc[:, t, :], acc[:, t, :], weight[:, t:t + 1], None, ALU.mult).then_inc(s_fin, 1)


def normalise(dve, act_go, act_done, turn, chain, pair, stats, mean_var, spread, inverse, passed):
    for u in range(2):
        chain.mark(dve.bn_stats(stats[:, u, :], pair[:, u, :]))
    chain.wait()
    for u in range(2):
        chain.mark(dve.bn_aggr(mean_var[:, u, :], stats[:, u, :]))
    chain.wait()
    dve.sem_inc(act_go, 1)
    hold(dve, act_done, turn, passed)
    chain.link(dve.reciprocal(inverse[:, :], spread[:, :]))
    for u in range(2):
        chain.mark(dve.tensor_scalar(pair[:, u, :], pair[:, u, :], mean_var[:, u, 0:1], inverse[:, u:u + 1],
                                     ALU.subtract, ALU.mult))
    chain.wait()


def node_layer(nc, const, name, kind, own, pooled, w, bias, gamma, beta, x, out, table, x_dram=None,
               embedded=None):
    KC = 2 if kind == "embed" else 4
    TURNS = NL // 2
    normed = kind in ("mixnorm", "enter", "sage")
    renormed = kind in ("enter", "sage")
    per_turn = {"embed": 1, "mix": 0, "mixnorm": 1, "enter": 2, "sage": 2}[kind]
    ident, ones, eps = const["ident"], const["ones"], const["eps"]
    with ExitStack() as ctx:
        k = Kit(nc, ctx, name)
        w_sb = k.sb("w", [P, KC, C])
        bias_sb = k.sb("bias", [1, C])
        gamma_sb = k.sb("gamma", [P, C])
        beta_sb = k.sb("beta", [P, C])
        zero_row = k.sb("zero_row", [1, C])
        staged = k.sb("staged", [P, 2, KC * P])
        turned = k.sb("turned", [P, 2, KC * P])
        pair = k.sb("pair", [P, 2, C])
        stats = k.sb("stats", [P, 2, 6])
        mean_var = k.sb("mean_var", [P, 2, 2])
        spread = k.sb("spread", [P, 2])
        inverse = k.sb("inverse", [P, 2])
        flipped = k.ps("flipped", [P, 2, 512])
        product = k.ps("product", [P, 2, 512])
        (s_w, s_zero, s_load0, s_load1, s_stage, s_flip, s_turn, s_mm, s_evac, s_sqrt_go, s_sqrt, s_out, s_store, s_ch, s_pd, s_pp,
         s_pa, s_pv, s_ps, s_pad) = (
            k.sem(n) for n in ("w", "zero", "load0", "load1", "stage", "flip", "turn", "mm", "evac", "sqrt_go", "sqrt", "out", "store",
                               "ch", "pd", "pp", "pa", "pv", "ps", "pad"))
        s_load = (s_load0, s_load1)
        params = 2 + 2 * normed
        ahead = kind != "embed"

        block = ctx.enter_context(nc.Block())

        @block.sync
        def _(sp):
            sp.dma_start(w_sb[:, :, :], w.rearrange("(k p) n -> p k n", p=P)).then_inc(s_w, 16)
            sp.dma_start(bias_sb[:, :], bias.rearrange("(o n) -> o n", o=1)).then_inc(s_w, 16)
            if normed:
                sp.dma_start(gamma_sb[:, :], gamma.rearrange("(o n) -> o n", o=1).to_broadcast([P, C])).then_inc(s_w, 16)
                sp.dma_start(beta_sb[:, :], beta.rearrange("(o n) -> o n", o=1).to_broadcast([P, C])).then_inc(s_w, 16)
            if kind == "embed":
                sp.dma_start(x[:, 0:NT - 1, :], x_dram[0:(NT - 1) * P, :].rearrange("(t p) c -> p t c", p=P)).then_inc(s_load0, 16)
                sp.wait_ge(s_zero, 2)
                sp.dma_start(x[0:LAST, NT - 1, :], x_dram[(NT - 1) * P:N, :]).then_inc(s_load0, 16)
            sp.wait_ge(s_zero, 1)
            sp.dma_start(table[PAD_ROW:PAD_ROW + 1, :], zero_row[:, :]).then_inc(s_pad, 16)

            def load(i):
                for u in range(2):
                    hold(sp, s_flip, 2 * i + 1 + u, s_ps)
                    sp.dma_start(staged[:, u, 2 * P:4 * P], pooled[bass.ds((2 * i + u) * P, P), :]).then_inc(s_load[u], 16)

            def store(i):
                for u in range(2):
                    hold(sp, s_out, 2 * i + 1 + u, s_ps)
                    made = embedded if kind == "embed" else out
                    sp.dma_start(table[bass.ds((2 * i + u) * P, P), :],
                                 made[:, bass.ds(2 * i + u, 1), :].rearrange("p o c -> p (o c)")).then_inc(s_store, 16)

            if ahead:
                load(0)
                with sp.Fori(0, TURNS - 1) as i:
                    load(i + 1)
                    store(i)
                store(TURNS - 1)
            else:
                with sp.Fori(0, TURNS) as i:
                    store(i)
            sp.wait_ge(s_store, 16 * NL)
            sp.wait_ge(s_pad, 16)

        @block.gpsimd
        def _(pool):
            pool.memset(zero_row[:, :], LOWEST if kind == "mixnorm" else 0.0).then_inc(s_zero, 1)
            if kind == "embed":
                pool.memset(x[:, NT - 1:NL, :], 0.0).then_inc(s_zero, 1)
            else:
                with pool.Fori(0, TURNS) as i:
                    for u in range(2):
                        hold(pool, s_flip, 2 * i + 1 + u, s_pp)
                        pool.tensor_copy(staged[:, u, 0:2 * P],
                                         own[:, bass.ds(2 * i + u, 1), :].rearrange("p o c -> p (o c)")).then_inc(s_stage, 1)

        @block.tensor
        def _(pe):
            def turn_over(i):
                for u in range(2):
                    hold(pe, s_stage, 2 * i + u + 1, s_pd)
                    if kind != "embed":
                        hold(pe, s_load[u], 16 * i + 16, s_pd)
                    hold(pe, s_turn, 2 * i + 1 + u, s_pd)
                    for c in range(KC):
                        t = nc.tensor.transpose(flipped[:, u, c * P:(c + 1) * P], staged[:, u, c * P:(c + 1) * P], ident[:, :])
                    t.then_inc(s_flip, 1)

            def multiply(i):
                for u in range(2):
                    hold(pe, s_turn, 2 * i + u + 3, s_pd)
                    hold(pe, s_evac, 2 * i + 1 + u, s_pd)
                    for c in range(KC):
                        nc.tensor.matmul(product[:, u, 0:C], turned[:, u, c * P:(c + 1) * P], w_sb[:, c, :],
                                         start=(c == 0), stop=False)
                    nc.tensor.matmul(product[:, u, 0:C], ones[0:1, :], bias_sb[:, :], start=False, stop=True).then_inc(s_mm, 1)

            pe.sem_inc(s_flip, 2)
            pe.sem_inc(s_mm, 2)
            pe.wait_ge(s_w, 16 * params)
            if ahead:
                turn_over(0)
                with pe.Fori(0, TURNS - 1) as i:
                    turn_over(i + 1)
                    multiply(i)
                multiply(TURNS - 1)
            else:
                with pe.Fori(0, TURNS) as i:
                    turn_over(i)
                    multiply(i)

        @block.scalar
        def _(act):
            def copy_turned(i):
                for u in range(2):
                    hold(act, s_flip, 2 * i + u + 3, s_pa)
                    hold(act, s_mm, 2 * i + 1 + u, s_pa)
                    act.activation(turned[:, u, :], flipped[:, u, 0:KC * P], ACT.Copy).then_inc(s_turn, 1)

            def roots(i):
                for r in range(per_turn):
                    hold(act, s_sqrt_go, per_turn * i + r + 1, s_pa)
                    act.activation(spread[:, :], mean_var[:, :, 1], ACT.Sqrt, bias=eps[:, 0:1]).then_inc(s_sqrt, 1)

            act.sem_inc(s_turn, 2)
            if ahead:
                copy_turned(0)
                with act.Fori(0, TURNS - 1) as i:
                    copy_turned(i + 1)
                    roots(i)
                roots(TURNS - 1)
            else:
                with act.Fori(0, TURNS) as i:
                    roots(i)
                    copy_turned(i)

        @block.vector
        def _(dve):
            chain = Chain(dve, s_ch)
            dve.sem_inc(s_evac, 2)
            if kind == "embed":
                dve.wait_ge(s_load0, 32)
            else:
                dve.wait_ge(s_w, 16 * params)

            def tile(a, i, u):
                return a[:, bass.ds(2 * i + u, 1), :].rearrange("p o c -> p (o c)")

            with dve.Fori(0, TURNS) as i:
                if kind == "embed":
                    for u in range(2):
                        chain.mark(dve.tensor_copy(pair[:, u, :], tile(x, i, u)))
                    chain.wait()
                    normalise(dve, s_sqrt_go, s_sqrt, i + 1, chain, pair, stats, mean_var, spread, inverse, s_pv)
                    for u in range(2):
                        chain.mark(dve.tensor_copy(tile(out, i, u), pair[:, u, :]))
                        hold(dve, s_flip, 2 * i + 1 + u, s_pv)
                        dve.tensor_copy(staged[:, u, :], pair[:, u, :]).then_inc(s_stage, 1)
                    for u in range(2):
                        hold(dve, s_mm, 2 * i + u + 3, s_pv)
                        dve.tensor_scalar(tile(embedded, i, u), product[:, u, 0:C], 0.0, None, ALU.max).then_inc(s_evac, 1)
                    hold(dve, s_evac, 2 * i + 4, s_pv)
                    dve.sem_inc(s_out, 2)
                if kind == "mix":
                    for u in range(2):
                        hold(dve, s_mm, 2 * i + u + 3, s_pv)
                        dve.tensor_scalar(tile(out, i, u), product[:, u, 0:C], 0.0, None, ALU.max).then_inc(s_evac, 1)
                        hold(dve, s_evac, 2 * i + u + 3, s_pv)
                        dve.sem_inc(s_out, 1)
                if normed:
                    for u in range(2):
                        hold(dve, s_mm, 2 * i + u + 3, s_pv)
                        if kind == "sage":
                            dve.tensor_copy(pair[:, u, :], product[:, u, 0:C]).then_inc(s_evac, 1)
                        else:
                            dve.scalar_tensor_tensor(out=pair[:, u, :], in0=product[:, u, 0:C], scalar=0.0,
                                                     in1=tile(own, i, u), op0=ALU.max, op1=ALU.add).then_inc(s_evac, 1)
                    hold(dve, s_evac, 2 * i + 4, s_pv)
                    normalise(dve, s_sqrt_go, s_sqrt, per_turn * i + 1, chain, pair, stats, mean_var, spread, inverse, s_pv)
                    for u in range(2):
                        chain.mark(dve.tensor_tensor(pair[:, u, :], pair[:, u, :], gamma_sb[:, :], ALU.mult))
                    chain.wait()
                    for u in range(2):
                        into = tile(out, i, u) if kind == "mixnorm" else pair[:, u, :]
                        chain.mark(dve.tensor_tensor(into, pair[:, u, :], beta_sb[:, :], ALU.add))
                    chain.wait()
                    if kind == "mixnorm":
                        dve.sem_inc(s_out, 2)
                if renormed:
                    if kind == "sage":
                        for u in range(2):
                            chain.mark(dve.scalar_tensor_tensor(out=pair[:, u, :], in0=pair[:, u, :], scalar=0.0,
                                                                in1=tile(own, i, u), op0=ALU.max, op1=ALU.add))
                        chain.wait()
                    for u in range(2):
                        chain.mark(dve.tensor_tensor(pair[:, u, :], pair[:, u, :], tile(x, i, u), ALU.add))
                    chain.wait()
                    for u in range(2):
                        chain.mark(dve.tensor_copy(tile(x, i, u), pair[:, u, :]))
                    chain.wait()
                    normalise(dve, s_sqrt_go, s_sqrt, 2 * i + 2, chain, pair, stats, mean_var, spread, inverse, s_pv)
                    for u in range(2):
                        chain.mark(dve.tensor_copy(tile(out, i, u), pair[:, u, :]))
                    chain.wait()
                    dve.sem_inc(s_out, 2)
                if kind != "mix":
                    chain.restart()


def project(nc, const, name, own, w, width, out):
    TURNS = NL // 2
    with ExitStack() as ctx:
        k = Kit(nc, ctx, name)
        w_sb = k.sb("w", [P, 2, width])
        staged = k.sb("staged", [P, 2, C])
        turned = k.sb("turned", [P, 2, C])
        flipped = k.ps("flipped", [P, 2, 512])
        product = k.ps("product", [P, 2, 512])
        s_w, s_stage, s_flip, s_turn, s_mm, s_evac, s_pp, s_pt, s_pa, s_pv = (
            k.sem(n) for n in ("w", "stage", "flip", "turn", "mm", "evac", "pp", "pt", "pa", "pv"))
        block = ctx.enter_context(nc.Block())

        @block.sync
        def _(sp):
            sp.dma_start(w_sb[:, :, :], w.rearrange("(k p) n -> p k n", p=P)).then_inc(s_w, 16)

        @block.gpsimd
        def _(pool):
            with pool.Fori(0, TURNS) as i:
                for u in range(2):
                    hold(pool, s_flip, 2 * i + 1 + u, s_pp)
                    pool.tensor_copy(staged[:, u, :], own[:, bass.ds(2 * i + u, 1), :].rearrange("p o c -> p (o c)")
                                     ).then_inc(s_stage, 1)

        @block.tensor
        def _(pe):
            pe.sem_inc(s_flip, 2)
            pe.sem_inc(s_mm, 2)
            pe.wait_ge(s_w, 16)
            with pe.Fori(0, TURNS) as i:
                for u in range(2):
                    hold(pe, s_stage, 2 * i + u + 1, s_pt)
                    hold(pe, s_turn, 2 * i + 1 + u, s_pt)
                    for c in range(2):
                        t = nc.tensor.transpose(flipped[:, u, c * P:(c + 1) * P], staged[:, u, c * P:(c + 1) * P], ident_of(const))
                    t.then_inc(s_flip, 1)
                for u in range(2):
                    hold(pe, s_turn, 2 * i + u + 3, s_pt)
                    hold(pe, s_evac, 2 * i + 1 + u, s_pt)
                    nc.tensor.matmul(product[:, u, 0:width], turned[:, u, 0:P], w_sb[:, 0, :], start=True, stop=False)
                    nc.tensor.matmul(product[:, u, 0:width], turned[:, u, P:2 * P], w_sb[:, 1, :], start=False, stop=True
                                     ).then_inc(s_mm, 1)

        @block.scalar
        def _(act):
            act.sem_inc(s_turn, 2)
            with act.Fori(0, TURNS) as i:
                for u in range(2):
                    hold(act, s_flip, 2 * i + u + 3, s_pa)
                    hold(act, s_mm, 2 * i + 1 + u, s_pa)
                    act.activation(turned[:, u, :], flipped[:, u, 0:C], ACT.Copy).then_inc(s_turn, 1)

        @block.vector
        def _(dve):
            dve.sem_inc(s_evac, 2)
            with dve.Fori(0, TURNS) as i:
                for u in range(2):
                    hold(dve, s_mm, 2 * i + u + 3, s_pv)
                    dve.tensor_copy(out[:, bass.ds(2 * i + u, 1), :].rearrange("p o c -> p (o c)"), product[:, u, 0:width]
                                    ).then_inc(s_evac, 1)


def ident_of(const):
    return const["ident"][:, :]


HEADS, EXPERTS0 = 4, 4
HE = HEADS * EXPERTS0
GROW = HE + 2 * HEADS


def attention(nc, const, name, h, att_src, att_dst, b_gat, ln_gamma, ln_beta, slot_table, tile_of_block, turns, perm,
              gat_table, agg, scores):
    RING = 2 * SLOTS

    def over(ap, n):
        return ap.rearrange("p (o n) -> p o n", o=1).to_broadcast([P, NL, n])

    with ExitStack() as ctx:
        k = Kit(nc, ctx, name)
        att = k.sb("att", [P, 5, HE])
        table_rows = k.sb("table_rows", [P, NL, GROW])
        weighted = k.sb("weighted", [P, NL, HE])
        blank = k.sb("blank", [1, GROW])
        own = k.sb("own", [P, NT + 1, GROW])
        peak = k.sb("peak", [P, NT + 1, HEADS])
        total = k.sb("total", [P, NT + 1, HEADS])
        mixed = k.sb("mixed", [P, NT + 1, HE])
        inv = k.sb("inv", [P, NT + 1, HEADS])
        rows = k.sb("rows", [P, RING, GROW])
        slots = k.sb("slots", [P, 2, 2, SLOTS], I32)
        tiles = k.sb("tiles", [1, 2, 2], I32)
        e = k.sb("e", [P, SLOTS, HEADS])
        e2 = k.sb("e2", [P, SLOTS, HEADS])
        top = k.sb("top", [P, HEADS])
        grown = k.sb("grown", [P, HEADS])
        below = k.sb("below", [P, SLOTS + 1, HEADS])
        p = k.sb("p", [P, SLOTS + 1, HEADS])
        psum_ = k.sb("psum_", [P, HEADS])
        ph = k.sb("ph", [P, SLOTS, HE])
        phsum = k.sb("phsum", [P, HE])
        natural = k.sb("natural", [P, NL, HE])
        mean = k.sb("mean", [P, NL])
        var = k.sb("var", [P, NL])
        s_row = [k.pool_dma_sem(f"row{r}") for r in range(RING)]
        (s_att, s_rows, s_tab, s_slots, s_used, s_ch, s_exp_go, s_exp, s_fin, s_nat, s_sq, s_set, s_pass,
         s_pa, s_pp, s_pv) = (
            k.sem(n) for n in ("att", "rows", "tab", "slots", "used", "ch", "exp_go", "exp", "fin", "nat",
                               "sq", "set", "pass", "pa", "pp", "pv"))
        s_own, s_out = k.pool_dma_sem("own"), k.pool_dma_sem("out")
        table_of_blocks = slot_table.rearrange("(b p s) -> b p s", p=P, s=SLOTS)
        block = ctx.enter_context(nc.Block())

        @block.sync
        def _(sp):
            vectors = (att_src.rearrange("h e -> (h e)"), att_dst.rearrange("h e -> (h e)"), b_gat, ln_gamma, ln_beta)
            for j, v in enumerate(vectors):
                sp.dma_start(att[:, j, :], v.rearrange("(o n) -> o n", o=1).to_broadcast([P, HE])).then_inc(s_att, 16)
            sp.wait_ge(s_rows, 1)
            sp.dma_start(gat_table[0:NL * P, :].rearrange("(t p) c -> p t c", p=P), table_rows[:, :, :]).then_inc(s_tab, 16)
            sp.wait_ge(s_set, 2)
            sp.dma_start(gat_table[PAD_ROW:PAD_ROW + 1, :], blank[:, :]).then_inc(s_tab, 16)
            sp.wait_ge(s_tab, 32)
            n = sp.value_load(turns[0:1, 0:1], min_val=1, max_val=slot_capacity(32768) // QUAD)
            with sp.Fori(0, n) as q:
                for hf in range(2):
                    hold(sp, s_used, 4 * q + 2 * hf + 2, s_pass)
                    b = q * QUAD + 2 * hf
                    sp.dma_start(slots[:, hf, :, :], table_of_blocks[bass.ds(b, 2), :, :].rearrange("b p s -> p b s")
                                 ).then_inc(s_slots, 16)
                    sp.dma_start(tiles[0:1, hf, :], tile_of_block[bass.ds(b, 2)].rearrange("(o n) -> o n", o=1)
                                 ).then_inc(s_slots, 16)
                    hold(sp, s_slots, 64 * q + 32 * hf + 32, s_pass)
            sp.wait_ge(s_out, 16 * NT)
            sp.dma_start(natural[:, 0:NT, :], agg[0:NT * P, :].rearrange("(t p) c -> p t c", p=P)).then_inc(s_nat, 16)

        @block.gpsimd
        def _(pool):
            pool.memset(blank[:, :], 0.0).then_inc(s_set, 1)
            pool.wait_ge(s_set, 1)
            pool.memset(blank[:, HE:HE + HEADS], -1e30).then_inc(s_set, 1)
            pool.memset(own[:, NT, :], 0.0).then_inc(s_set, 1)
            pool.memset(natural[:, NT, :], 0.0).then_inc(s_set, 1)
            pool.wait_ge(s_tab, 32)
            for t in range(NT):
                pool.indirect_dma_start(own[:, t, :], None, gat_table[:, :],
                                        bass.IndirectOffsetOnAxis(ap=perm[:, t:t + 1], axis=0)).then_inc(s_own, 16)
            n = pool.value_load(turns[0:1, 0:1], min_val=1, max_val=slot_capacity(32768) // QUAD)
            with pool.Fori(0, n) as q:
                for hf in range(2):
                    hold(pool, s_slots, 64 * q + 32 * hf + 32, s_pp)
                    for u in range(2):
                        hold(pool, s_used, 4 * q + 2 * hf + u + 3, s_pp)
                        for s in range(SLOTS):
                            r = u * SLOTS + s
                            pool.indirect_dma_start(rows[:, r, :], None, gat_table[:, :],
                                                    bass.IndirectOffsetOnAxis(ap=slots[:, hf, u, s:s + 1], axis=0)
                                                    ).then_inc(s_row[r], 16)
            pool.wait_ge(s_fin, 1)
            for t in range(NT):
                pool.indirect_dma_start(agg[:, :], bass.IndirectOffsetOnAxis(ap=perm[:, t:t + 1], axis=0),
                                        mixed[:, t, :], None).then_inc(s_out, 16)

        @block.scalar
        def _(act):
            n = act.value_load(turns[0:1, 0:1], min_val=1, max_val=slot_capacity(32768) // QUAD)
            with act.Fori(0, n) as q:
                for b in range(QUAD):
                    hold(act, s_exp_go, 4 * q + b + 1, s_pa)
                    act.activation(p[:, :, :], below[:, :, :], ACT.Exp).then_inc(s_exp, 1)
            act.wait_ge(s_sq, 1)
            act.activation(var[:, :], mean[:, :], ACT.Sqrt, bias=const["eps"][:, 0:1]).then_inc(s_sq, 1)

        @block.vector
        def _(dve):
            chain = Chain(dve, s_ch)
            link = chain.link
            dve.wait_ge(s_att, 80)
            chain.mark(dve.tensor_copy(table_rows[:, :, 0:HE], h[:, :, :]))
            for j in range(2):
                link(dve.tensor_tensor(weighted[:, :, :], h[:, :, :], over(att[:, j, :], HE), ALU.mult))
                link(dve.tensor_reduce(table_rows[:, :, HE + j * HEADS:HE + (j + 1) * HEADS],
                                       weighted[:, :, :].rearrange("p t (h e) -> p t h e", h=HEADS), AX_X, ALU.add))
            dve.sem_inc(s_rows, 1)
            dve.wait_ge(s_own, 16 * NT)
            dve.wait_ge(s_set, 4)
            link(dve.tensor_tensor(inv[:, :, :], own[:, :, HE:HE + HEADS], own[:, :, HE + HEADS:GROW], ALU.add))
            link(dve.scalar_tensor_tensor(out=peak[:, :, :], in0=inv[:, :, :], scalar=0.2, in1=inv[:, :, :],
                                          op0=ALU.mult, op1=ALU.max))
            chain.mark(dve.memset(total[:, :, :], 1.0))
            link(dve.tensor_copy(mixed[:, :, :], own[:, :, 0:HE]))
            chain.restart()
            dve.sem_inc(s_used, 4)
            n = dve.value_load(turns[0:1, 0:1], min_val=1, max_val=slot_capacity(32768) // QUAD)
            with dve.Fori(0, n) as q:
                for hf in range(2):
                    hold(dve, s_slots, 64 * q + 32 * hf + 32, s_pv)
                    for u in range(2):
                        t = dve.value_load(tiles[0:1, hf, u:u + 1], min_val=0, max_val=NT)

                        def flat(a):
                            return a[:, bass.ds(t, 1), :].rearrange("p o c -> p (o c)")

                        a_dst = own[:, bass.ds(t, 1), HE + HEADS:GROW].to_broadcast([P, SLOTS, HEADS])
                        r0 = u * SLOTS
                        for s in range(SLOTS):
                            hold(dve, s_row[r0 + s], 32 * q + 16 * hf + 16, s_pv)
                        link(dve.tensor_tensor(e[:, :, :], rows[:, r0:r0 + SLOTS, HE:HE + HEADS], a_dst, ALU.add))
                        link(dve.scalar_tensor_tensor(out=e2[:, :, :], in0=e[:, :, :], scalar=0.2, in1=e[:, :, :],
                                                      op0=ALU.mult, op1=ALU.max))
                        link(dve.tensor_reduce(top[:, :], e2[:, :, :].rearrange("p s h -> p h s"), AX_X, ALU.max))
                        link(dve.tensor_tensor(grown[:, :], top[:, :], flat(peak), ALU.max))
                        chain.mark(dve.tensor_tensor(
                            below[:, 0:SLOTS, :], e2[:, :, :],
                            grown[:, :].rearrange("p (o h) -> p o h", o=1).to_broadcast([P, SLOTS, HEADS]), ALU.subtract))
                        link(dve.tensor_tensor(below[:, SLOTS, :], flat(peak), grown[:, :], ALU.subtract))
                        dve.sem_inc(s_exp_go, 1)
                        chain.mark(dve.tensor_copy(flat(peak), grown[:, :]))
                        hold(dve, s_exp, 4 * q + 2 * hf + u + 1, s_pv)
                        chain.mark(dve.tensor_tensor(
                            ph[:, :, :].rearrange("p s (h e) -> p s h e", h=HEADS),
                            rows[:, r0:r0 + SLOTS, 0:HE].rearrange("p s (h e) -> p s h e", h=HEADS),
                            p[:, 0:SLOTS, :].rearrange("p s (h o) -> p s h o", o=1).to_broadcast([P, SLOTS, HEADS, EXPERTS0]),
                            ALU.mult))
                        chain.mark(dve.tensor_reduce(psum_[:, :], p[:, 0:SLOTS, :].rearrange("p s h -> p h s"), AX_X, ALU.add))
                        chain.mark(dve.tensor_tensor(flat(total), flat(total), p[:, SLOTS, :], ALU.mult))
                        chain.mark(dve.tensor_tensor(
                            flat(mixed).rearrange("p (h e) -> p h e", h=HEADS), flat(mixed).rearrange("p (h e) -> p h e", h=HEADS),
                            p[:, SLOTS, :].rearrange("p (h o) -> p h o", o=1).to_broadcast([P, HEADS, EXPERTS0]), ALU.mult))
                        chain.wait()
                        chain.mark(dve.tensor_tensor(flat(total), flat(total), psum_[:, :], ALU.add))
                        link(dve.tensor_reduce(phsum[:, :], ph[:, :, :].rearrange("p s c -> p c s"), AX_X, ALU.add))
                        link(dve.tensor_tensor(flat(mixed), flat(mixed), phsum[:, :], ALU.add))
                        dve.sem_inc(s_used, 1)
                chain.restart()
            link(dve.tensor_scalar(total[:, :, :], total[:, :, :], 1e-16, None, ALU.add))
            link(dve.reciprocal(inv[:, :, :], total[:, :, :]))
            link(dve.tensor_tensor(mixed[:, :, :].rearrange("p t (h e) -> p (t h) e", h=HEADS),
                                   mixed[:, :, :].rearrange("p t (h e) -> p (t h) e", h=HEADS),
                                   inv[:, :, :].rearrange("p t (h o) -> p (t h) o", o=1).to_broadcast([P, (NT + 1) * HEADS, EXPERTS0]),
                                   ALU.mult))
            dve.sem_inc(s_fin, 1)
            dve.wait_ge(s_nat, 16)
            link(dve.tensor_tensor(natural[:, :, :], natural[:, :, :], over(att[:, 2, :], HE), ALU.add))
            link(dve.tensor_reduce(mean[:, :], natural[:, :, :], AX_X, ALU.add))
            link(dve.tensor_scalar(mean[:, :], mean[:, :], 1.0 / HE, None, ALU.mult))
            link(dve.tensor_tensor(natural[:, :, :], natural[:, :, :],
                                   mean[:, :].rearrange("p (t o) -> p t o", o=1).to_broadcast([P, NL, HE]), ALU.subtract))
            link(dve.tensor_tensor(weighted[:, :, :], natural[:, :, :], natural[:, :, :], ALU.mult))
            link(dve.tensor_reduce(mean[:, :], weighted[:, :, :], AX_X, ALU.add))
            link(dve.tensor_scalar(mean[:, :], mean[:, :], 1.0 / HE, None, ALU.mult))
            dve.sem_inc(s_sq, 1)
            dve.wait_ge(s_sq, 2)
            link(dve.reciprocal(mean[:, :], var[:, :]))
            link(dve.tensor_tensor(natural[:, :, :], natural[:, :, :],
                                   mean[:, :].rearrange("p (t o) -> p t o", o=1).to_broadcast([P, NL, HE]), ALU.mult))
            link(dve.tensor_tensor(natural[:, :, :], natural[:, :, :], over(att[:, 3, :], HE), ALU.mult))
            link(dve.tensor_tensor(natural[:, :, :], natural[:, :, :], over(att[:, 4, :], HE), ALU.add))
            link(dve.tensor_reduce(scores[:, :, :], natural[:, :, :].rearrange("p t (h e) -> p t e h", h=HEADS), AX_X, ALU.add))
            link(dve.tensor_scalar(scores[:, :, :], scores[:, :, :], 1.0 / HEADS, None, ALU.mult))


UNIT = 2 * P


def units_most(experts):
    return (2 * N + UNIT * experts) // UNIT


def spill_row(experts):
    return (units_most(experts) + 1) * UNIT


def route(nc, const, name, logits, experts, own, sorted_x, place, gates, units, cleared):
    E = experts
    with ExitStack() as ctx:
        k = Kit(nc, ctx, name)
        full = [P, NL, E]
        best = k.sb("best", [P, 2, NL])
        pick = k.sb("pick", [P, 2, NL, E])
        work = k.sb("work", full)
        rest = k.sb("rest", full)
        index = k.sb("index", [P, NL])
        node = k.sb("node", [P, NL])
        real = k.sb("real", [P, NL])
        spill = k.sb("spill", [P, 2, NL])
        seen = k.sb("seen", [P, NL + 1, E])
        count_i = k.sb("count_i", [P, E], I32)
        n_units = k.sb("n_units", [P, E])
        first = k.sb("first", [P, E])
        spot = k.sb("spot", [P, 2, NL])
        gap = k.sb("gap", [P, NL])
        grow = k.sb("grow", [P, NL])
        denom = k.sb("denom", [P, NL])
        store_at = k.sb("store_at", [P, 2, NL], I32)
        ahead = k.ps("ahead", [P, 512])
        tile_sum = k.ps("tile_sum", [P, 512])
        s_ch, s_set, s_mm, s_pick, s_exp, s_at = (k.sem(n) for n in ("ch", "set", "mm", "pick", "exp", "at"))
        s_store = k.pool_dma_sem("store")
        block = ctx.enter_context(nc.Block())

        def over_tiles(a):
            return a.rearrange("p (o e) -> p o e", o=1).to_broadcast(full)

        def over_experts(a):
            return a.rearrange("p (t o) -> p t o", o=1).to_broadcast(full)

        @block.gpsimd
        def _(pool):
            pool.iota(node[:, :], pattern=[[P, NL]], base=0, channel_multiplier=1,
                      allow_small_or_imprecise_dtypes=True).then_inc(s_set, 1)
            pool.wait_ge(s_at, 1)
            pool.wait_ge(cleared, 16 * CLEARS)
            for c in range(2):
                for t in range(NT):
                    pool.indirect_dma_start(sorted_x[:, :], bass.IndirectOffsetOnAxis(ap=store_at[:, c, t:t + 1], axis=0),
                                            own[:, t, :], None).then_inc(s_store, 16)
            pool.wait_ge(s_store, 16 * 2 * NT)

        @block.tensor
        def _(pe):
            pe.wait_ge(s_pick, 1)
            picks = work[:, :, :].rearrange("p t e -> p (t e)")
            nc.tensor.matmul(ahead[:, 0:NL * E], const["after"][:, :], picks, start=True, stop=True).then_inc(s_mm, 1)
            nc.tensor.matmul(tile_sum[:, 0:NL * E], const["ones"][:, :], picks, start=True, stop=True).then_inc(s_mm, 1)

        @block.scalar
        def _(act):
            act.wait_ge(s_exp, 1)
            act.activation(grow[:, :], gap[:, :], ACT.Exp).then_inc(s_exp, 1)

        @block.vector
        def _(dve):
            chain = Chain(dve, s_ch)
            link = chain.link
            ramp = const["ramp"]
            left = logits
            for c in range(2):
                link(dve.tensor_reduce(best[:, c, :], left[:, :, :], AX_X, ALU.max))
                link(dve.tensor_tensor(work[:, :, :], left[:, :, :], over_experts(best[:, c, :]), ALU.is_equal))
                link(dve.scalar_tensor_tensor(out=work[:, :, :], in0=work[:, :, :], scalar=-64.0,
                                              in1=over_tiles(ramp[:, 0:E]), op0=ALU.mult, op1=ALU.add))
                link(dve.tensor_reduce(index[:, :], work[:, :, :], AX_X, ALU.min))
                link(dve.tensor_scalar(index[:, :], index[:, :], 64.0, None, ALU.add))
                link(dve.tensor_tensor(pick[:, c, :, :], over_tiles(ramp[:, 0:E]), over_experts(index[:, :]), ALU.is_equal))
                if c == 0:
                    link(dve.scalar_tensor_tensor(out=rest[:, :, :], in0=pick[:, 0, :, :], scalar=LOWEST,
                                                  in1=logits[:, :, :], op0=ALU.mult, op1=ALU.add))
                    left = rest
            link(dve.tensor_tensor(gap[:, :], best[:, 1, :], best[:, 0, :], ALU.subtract))
            dve.sem_inc(s_exp, 1)
            dve.wait_ge(s_set, 1)
            link(dve.tensor_scalar(real[:, :], node[:, :], float(N), None, ALU.is_lt))
            for c in range(2):
                chain.mark(dve.tensor_tensor(pick[:, c, :, :], pick[:, c, :, :], over_experts(real[:, :]), ALU.mult))
            chain.wait()
            link(dve.tensor_tensor(work[:, :, :], pick[:, 0, :, :], pick[:, 1, :, :], ALU.add))
            dve.sem_inc(s_pick, 1)
            dve.wait_ge(s_exp, 2)
            link(dve.tensor_scalar(denom[:, :], grow[:, :], 1.0, None, ALU.add))
            link(dve.reciprocal(gates[:, 0, :], denom[:, :]))
            link(dve.tensor_tensor(gates[:, 1, :], grow[:, :], gates[:, 0, :], ALU.mult))
            link(dve.memset(seen[:, 0, :], 0.0))
            dve.wait_ge(s_mm, 2)
            for t in range(NL):
                link(dve.tensor_tensor(seen[:, t + 1, :], seen[:, t, :], tile_sum[:, t * E:(t + 1) * E], ALU.add))
            link(dve.tensor_scalar(n_units[:, :], seen[:, NL, :], UNIT - 1.0, None, ALU.add))
            link(dve.tensor_copy(count_i[:, :], n_units[:, :]))
            link(dve.tensor_scalar(count_i[:, :], count_i[:, :], 8, None, ALU.logical_shift_right))
            link(dve.tensor_scalar(n_units[:, :], count_i[:, :], 1.0, None, ALU.max))
            chain.mark(dve.tensor_copy(units[0:1, 0:E], n_units[0:1, :]))
            link(dve.tensor_tensor_scan(first[:, :], const["ones"][:, 0:E], n_units[:, :], 0.0, ALU.mult, ALU.add))
            link(dve.tensor_tensor(first[:, :], first[:, :], n_units[:, :], ALU.subtract))
            link(dve.tensor_scalar(first[:, :], first[:, :], float(UNIT), None, ALU.mult))
            link(dve.tensor_tensor(rest[:, :, :], seen[:, 0:NL, :], over_tiles(first[:, :]), ALU.add))
            link(dve.tensor_tensor(rest[:, :, :], rest[:, :, :], ahead[:, 0:NL * E].rearrange("p (t e) -> p t e", e=E), ALU.add))
            for c in range(2):
                link(dve.tensor_tensor(work[:, :, :], rest[:, :, :], pick[:, c, :, :], ALU.mult))
                link(dve.tensor_reduce(spot[:, c, :], work[:, :, :], AX_X, ALU.add))
                chain.mark(dve.tensor_copy(place[:, c, :], spot[:, c, :]))
                link(dve.tensor_scalar(spill[:, c, :], node[:, :], float(spill_row(E) - N + UNIT * c), None, ALU.add))
                link(dve.tensor_scalar(denom[:, :], real[:, :], -1.0, 1.0, ALU.mult, ALU.add))
                link(dve.tensor_tensor(spill[:, c, :], spill[:, c, :], denom[:, :], ALU.mult))
                link(dve.tensor_tensor(spot[:, c, :], spot[:, c, :], spill[:, c, :], ALU.add))
                link(dve.tensor_copy(store_at[:, c, :], spot[:, c, :]))
            dve.sem_inc(s_at, 1)


def run_experts(nc, const, name, experts, w1, b1, w2, b2, func, sorted_x, units):
    E, F = experts, w1.shape[2]
    M = F // P
    with ExitStack() as ctx:
        k = Kit(nc, ctx, name)
        w1_sb = k.sb("w1", [P, 2, 2, F])
        w2_sb = k.sb("w2", [P, 2, M, C])
        b1_sb = k.sb("b1", [P, 2, M])
        b2_sb = k.sb("b2", [P, 2, C])
        rows = k.sb("rows", [P, 2, C])
        turned = k.sb("turned", [P, 2, UNIT])
        hidden = k.sb("hidden", [P, M, UNIT])
        y = k.sb("y", [P, 2, C])
        primed = k.sb("primed", [1, 1])
        flipped = k.ps("flipped", [P, 2, UNIT])
        up = k.ps("up", [P, M, 512])
        down = k.ps("down", [P, 2, 512])
        (s_wfree, s_x, s_flip, s_turn, s_up, s_hid, s_down, s_y, s_store, s_pp, s_ps, s_pt, s_pa, s_pv) = (
            k.sem(n) for n in ("wfree", "x", "flip", "turn", "up", "hid", "down", "y", "store", "pp", "ps", "pt", "pa", "pv"))
        s_wt = k.pool_dma_sem("wt")
        block = ctx.enter_context(nc.Block())
        most = units_most(E)

        def per_unit(eng, prepare, work):
            done = eng.alloc_register(f"{name}_{eng.engine.name}_done")
            eng.reg_mov(done, 0)
            with eng.Fori(0, E // 2) as pair:
                for b in range(2):
                    prepare(2 * pair + b, b)
                    n = eng.value_load(units[0:1, bass.ds(2 * pair + b, 1)], min_val=1, max_val=most)
                    with eng.Fori(0, n):
                        work(eng.snap(done, min_val=0, max_val=most - 1), b)
                        eng.reg_add(done, done, 1)
                    if eng is nc.vector:
                        hold(eng, s_y, 2 * eng.snap(done, min_val=0, max_val=most) + 2, s_pv)
                        eng.sem_inc(s_wfree, 1)
            return done

        @block.gpsimd
        def _(pool):
            with pool.Fori(0, E // 2) as pair:
                for b in range(2):
                    hold(pool, s_wfree, 2 * pair + b + 1, s_pp)
                    e = bass.ds(2 * pair + b, 1)
                    pool.dma_start(w1_sb[:, b, :, :], w1[e, :, :].rearrange("o (k p) n -> p (o k) n", p=P)).then_inc(s_wt, 16)
                    pool.dma_start(w2_sb[:, b, :, :], w2[e, :, :].rearrange("o (k p) n -> p (o k) n", p=P)).then_inc(s_wt, 16)
                    pool.dma_start(b1_sb[:, b, :], b1[e, :, :].rearrange("o p m -> p (o m)")).then_inc(s_wt, 16)
                    pool.dma_start(b2_sb[:, b, :], b2[e, :].to_broadcast([P, C])).then_inc(s_wt, 16)
                    hold(pool, s_wt, 128 * pair + 64 * b + 64, s_pp)

        @block.sync
        def _(sp):
            def load(u):
                sp.dma_start(rows[:, :, :], sorted_x[bass.ds(u * UNIT, UNIT), :].rearrange("(h p) c -> p h c", p=P)).then_inc(s_x, 16)

            def work(u, b):
                hold(sp, s_flip, u + 1, s_ps)
                load(u + 1)
                hold(sp, s_y, 2 * u + 4, s_ps)
                sp.dma_start(sorted_x[bass.ds(u * UNIT, UNIT), :].rearrange("(h p) c -> p h c", p=P), y[:, :, :]).then_inc(s_store, 16)

            sp.dma_start(primed[:, :], b2[0:1, 0:1]).then_inc(s_store, 16)
            load(0)
            done = per_unit(sp, lambda e, b: None, work)
            hold(sp, s_store, 16 * sp.snap(done, min_val=1, max_val=most) + 16, s_ps)
            hold(sp, s_x, 16 * sp.snap(done, min_val=1, max_val=most) + 16, s_ps)

        @block.tensor
        def _(pe):
            def turn_over(u):
                hold(pe, s_x, 16 * u + 16, s_pt)
                hold(pe, s_turn, u + 1, s_pt)
                for h in range(2):
                    for c in range(2):
                        t = nc.tensor.transpose(flipped[:, c, h * P:(h + 1) * P], rows[:, h, c * P:(c + 1) * P], ident_of(const))
                t.then_inc(s_flip, 1)

            def work(u, b):
                hold(pe, s_turn, u + 2, s_pt)
                for m in range(M):
                    hold(pe, s_hid, M * u + m + 1, s_pt)
                    for c in range(2):
                        t = nc.tensor.matmul(up[:, m, 0:UNIT], w1_sb[:, b, c, m * P:(m + 1) * P], turned[:, c, :],
                                             start=(c == 0), stop=(c == 1))
                    t.then_inc(s_up, 1)
                turn_over(u + 1)
                for h in range(2):
                    hold(pe, s_y, 2 * u + h + 1, s_pt)
                    for m in range(M):
                        if h == 0:
                            hold(pe, s_hid, M * u + m + 1 + M, s_pt)
                        t = nc.tensor.matmul(down[:, h, 0:C], hidden[:, m, h * P:(h + 1) * P], w2_sb[:, b, m, :],
                                             start=(m == 0), stop=(m == M - 1))
                    t.then_inc(s_down, 1)

            pe.sem_inc(s_down, 2)
            turn_over(0)
            per_unit(pe, lambda e, b: hold(pe, s_wt, 64 * e + 64, s_pt), work)

        @block.scalar
        def _(act):
            def copy_turned(u):
                hold(act, s_flip, u + 1, s_pa)
                act.activation(turned[:, :, :], flipped[:, :, :], ACT.Copy).then_inc(s_turn, 1)

            def work(u, b):
                hold(act, s_down, 2 * u + 2, s_pa)
                for m in range(M):
                    hold(act, s_up, M * u + m + 1, s_pa)
                    act.activation(hidden[:, m, :], up[:, m, 0:UNIT], func, bias=b1_sb[:, b, m:m + 1]).then_inc(s_hid, 1)
                copy_turned(u + 1)

            act.sem_inc(s_turn, 1)
            act.sem_inc(s_hid, M)
            copy_turned(0)
            per_unit(act, lambda e, b: hold(act, s_wt, 64 * e + 64, s_pa), work)

        @block.vector
        def _(dve):
            def work(u, b):
                hold(dve, s_store, 16 * u + 16, s_pv)
                for h in range(2):
                    hold(dve, s_down, 2 * u + h + 3, s_pv)
                    dve.tensor_tensor(y[:, h, :], down[:, h, 0:C], b2_sb[:, b, :], ALU.add).then_inc(s_y, 1)

            dve.sem_inc(s_y, 2)
            dve.sem_inc(s_wfree, 2)
            per_unit(dve, lambda e, b: hold(dve, s_wt, 64 * e + 64, s_pv), work)


def combine(nc, const, name, sorted_y, place, gates, own, x, out, table=None, gamma=None, beta=None, result=None):
    TURNS = NL // 2
    final = gamma is not None
    with ExitStack() as ctx:
        k = Kit(nc, ctx, name)
        y = k.sb("y", [P, NL, 2, C])
        gamma_sb = k.sb("gamma", [P, C])
        beta_sb = k.sb("beta", [P, C])
        zero_row = k.sb("zero_row", [1, C])
        pair = k.sb("pair", [P, 2, C])
        stats = k.sb("stats", [P, 2, 6])
        mean_var = k.sb("mean_var", [P, 2, 2])
        spread = k.sb("spread", [P, 2])
        inverse = k.sb("inverse", [P, 2])
        s_y = [k.pool_dma_sem(f"y{i}") for i in range(2)]
        s_w, s_zero, s_got, s_sqrt_go, s_sqrt, s_out, s_store, s_ch, s_ps, s_pa, s_pv = (
            k.sem(n) for n in ("w", "zero", "got", "sqrt_go", "sqrt", "out", "store", "ch", "ps", "pa", "pv"))
        block = ctx.enter_context(nc.Block())

        @block.gpsimd
        def _(pool):
            pool.memset(y[:, NT, :, :], 0.0).then_inc(s_zero, 1)
            pool.memset(zero_row[:, :], 0.0).then_inc(s_zero, 1)
            for t in range(NT):
                for c in range(2):
                    pool.indirect_dma_start(y[:, t, c, :], None, sorted_y[:, :],
                                            bass.IndirectOffsetOnAxis(ap=place[:, c, t:t + 1], axis=0)
                                            ).then_inc(s_y[t // 2 % 2], 16)
                if t % 2 == 1 and t >= 3:
                    pool.wait_ge(s_y[(t // 2 - 1) % 2], 64 * ((t // 2 - 1) // 2 + 1))
                    pool.sem_inc(s_got, 1)
            pool.wait_ge(s_y[1], 64 * (TURNS // 2))
            pool.sem_inc(s_got, 1)
            pool.wait_ge(s_y[0], 64 * (TURNS // 2) + 32)
            pool.sem_inc(s_got, 1)

        @block.sync
        def _(sp):
            if final:
                sp.dma_start(gamma_sb[:, :], gamma.rearrange("(o n) -> o n", o=1).to_broadcast([P, C])).then_inc(s_w, 16)
                sp.dma_start(beta_sb[:, :], beta.rearrange("(o n) -> o n", o=1).to_broadcast([P, C])).then_inc(s_w, 16)
                for g in range(4):
                    sp.wait_ge(s_out, 3 * (g + 1))
                    sp.dma_start(result[6 * g * P:6 * (g + 1) * P, :].rearrange("(t p) c -> p t c", p=P),
                                 out[:, 6 * g:6 * (g + 1), :]).then_inc(s_store, 16)
                sp.wait_ge(s_out, TURNS)
                sp.dma_start(result[(NT - 1) * P:N, :], out[0:LAST, NT - 1, :]).then_inc(s_store, 16)
                sp.wait_ge(s_store, 80)
            else:
                sp.wait_ge(s_zero, 2)
                sp.dma_start(table[PAD_ROW:PAD_ROW + 1, :], zero_row[:, :]).then_inc(s_w, 16)
                with sp.Fori(0, TURNS) as i:
                    hold(sp, s_out, i + 1, s_ps)
                    sp.dma_start(table[bass.ds(i * 2 * P, 2 * P), :].rearrange("(t p) c -> p t c", p=P),
                                 out[:, bass.ds(2 * i, 2), :]).then_inc(s_store, 16)
                sp.wait_ge(s_store, 16 * TURNS)
                sp.wait_ge(s_w, 16)

        @block.scalar
        def _(act):
            with act.Fori(0, TURNS) as i:
                hold(act, s_sqrt_go, i + 1, s_pa)
                act.activation(spread[:, :], mean_var[:, :, 1], ACT.Sqrt, bias=const["eps"][:, 0:1]).then_inc(s_sqrt, 1)

        @block.vector
        def _(dve):
            chain = Chain(dve, s_ch)
            dve.wait_ge(s_zero, 2)
            if final:
                dve.wait_ge(s_w, 32)

            def tile(a, i, u):
                return a[:, bass.ds(2 * i + u, 1), :].rearrange("p o c -> p (o c)")

            with dve.Fori(0, TURNS) as i:
                hold(dve, s_got, i + 1, s_pv)
                for c in range(2):
                    for u in range(2):
                        row = y[:, bass.ds(2 * i + u, 1), c, :].rearrange("p o c -> p (o c)")
                        gate = gates[:, c, bass.ds(2 * i + u, 1)]
                        if c == 0:
                            chain.mark(dve.tensor_scalar(pair[:, u, :], row, gate, None, ALU.mult))
                        else:
                            chain.mark(dve.scalar_tensor_tensor(out=pair[:, u, :], in0=row, scalar=gate, in1=pair[:, u, :],
                                                                op0=ALU.mult, op1=ALU.add))
                    chain.wait()
                for u in range(2):
                    chain.mark(dve.tensor_tensor(pair[:, u, :], pair[:, u, :], tile(own if final else x, i, u), ALU.add))
                chain.wait()
                if not final:
                    for u in range(2):
                        chain.mark(dve.tensor_copy(tile(x, i, u), pair[:, u, :]))
                    chain.wait()
                normalise(dve, s_sqrt_go, s_sqrt, i + 1, chain, pair, stats, mean_var, spread, inverse, s_pv)
                if final:
                    for other, op in ((gamma_sb, ALU.mult), (beta_sb, ALU.add)):
                        for u in range(2):
                            chain.mark(dve.tensor_tensor(pair[:, u, :], pair[:, u, :], other[:, :], op))
                        chain.wait()
                for u in range(2):
                    if final:
                        chain.mark(dve.tensor_tensor(tile(out, i, u), pair[:, u, :], tile(x, i, u), ALU.add))
                    else:
                        chain.mark(dve.tensor_copy(tile(out, i, u), pair[:, u, :]))
                chain.wait()
                dve.sem_inc(s_out, 1)
                chain.restart()


CLEARS = 8


def build(nc, x, src, dst,
          g_wp1, g_bp1, g_wm1, g_bm1, g_wm2, g_bm2, g_wm3, g_bm3, g_ln2_g, g_ln2_b, g_ln3_g, g_ln3_b,
          f_wgat, f_att_src, f_att_dst, f_bgat, f_ln_g, f_ln_b, f_w1, f_b1, f_w2, f_b2, f_edges,
          s_w, s_bl, s_g, s_b, m_gate, m_gate_b, m_w1, m_b1, m_w2, m_b2, m_g, m_b, result):
    with ExitStack() as ctx:
        def sb(name, shape, dt=F32):
            return ctx.enter_context(nc.sbuf_tensor(name, shape, dt))

        def dram(name, shape, dt=F32):
            return nc.dram_tensor(name, shape, dt, kind="Internal").ap()

        const = {"ident": sb("ident", [P, P]), "before": sb("before", [P, P]), "after": sb("after", [P, P]),
                 "ones": sb("ones", [P, P]), "ramp": sb("ramp", [P, P]), "row": sb("row", [P, 1]),
                 "zero16": sb("zero16", [P, P], BF16), "eps": sb("eps", [P, 1]), "zeros": sb("zeros", [P, C])}
        state = sb("state", [P, NL, C])
        ping = sb("ping", [P, NL, C])
        pong = sb("pong", [P, NL, C])
        narrow = sb("narrow", [P, NL, HE])
        scores = sb("scores", [P, NL, EXPERTS0])
        place = sb("place", [P, 2, NL], I32)
        gates = sb("gates", [P, 2, NL])
        units = sb("units", [1, HE], I32)
        perm = sb("perm", [P, NT], I32)
        degree = sb("degree", [P, NT])
        weight = sb("weight", [P, NT])
        turns = sb("turns", [1, 2], I32)
        perm_f = sb("perm_f", [P, NT], I32)
        degree_f = sb("degree_f", [P, NT])
        turns_f = sb("turns_f", [1, 2], I32)

        edges, f_n = dst.shape[0], f_edges.shape[1]
        cap, cap_f = slot_capacity(edges), slot_capacity(f_n)
        slot_table, slot_table_f = dram("slot_table", [cap * BLOCK], I32), dram("slot_table_f", [cap_f * BLOCK], I32)
        block_tile, block_tile_f = dram("block_tile", [cap], I32), dram("block_tile_f", [cap_f], I32)
        ranked, ranked_f = dram("ranked", [NP, 2], I32), dram("ranked_f", [NP, 2], I32)
        tables = [dram(f"table{i}", [PAD_ROW + 1, C]) for i in range(5)]
        gat_table = dram("gat_table", [PAD_ROW + 1, GROW])
        pooled = [dram(f"pooled{i}", [NL * P, C]) for i in range(2)]
        agg = dram("agg", [NP, HE])
        most_rows = spill_row(HE) + 2 * UNIT
        sorted_x = dram("sorted_x", [-(-most_rows // (CLEARS * P)) * CLEARS * P, C])
        cleared = ctx.enter_context(nc.semaphore("cleared"))

        build_constants(nc, const, sorted_x, pooled, cleared)
        build_slots(nc, const, "A", dst, src, edges, 125, slot_table, block_tile, ranked, perm, degree, turns)
        build_slots(nc, const, "B", f_edges[1, :], f_edges[0, :], f_n, P, slot_table_f, block_tile_f, ranked_f,
                    perm_f, degree_f, turns_f)

        def pool_nodes(name, table, factor, into, op, init):
            gather_pass(nc, const, name, table, slot_table, block_tile, turns, perm, factor, into, op, init)

        node_layer(nc, const, "embed", "embed", None, None, g_wp1, g_bp1, None, None, state, ping, tables[0], x, pong)
        pool_nodes("p1", tables[0], None, pooled[0], ALU.max, 0.0)
        node_layer(nc, const, "mix1", "mix", ping, pooled[0], g_wm1, g_bm1, None, None, state, pong, tables[1])
        pool_nodes("p2", tables[1], None, pooled[1], ALU.max, 0.0)
        node_layer(nc, const, "mix2", "mixnorm", pong, pooled[1], g_wm2, g_bm2, g_ln2_g, g_ln2_b, state, ping, tables[2])
        has_edges(nc, degree, weight)
        pool_nodes("p3", tables[2], weight, pooled[0], ALU.max, LOWEST)
        node_layer(nc, const, "mix3", "enter", ping, pooled[0], g_wm3, g_bm3, g_ln3_g, g_ln3_b, state, pong, tables[3])
        project(nc, const, "gat", pong, f_wgat, HE, narrow)
        attention(nc, const, "att", narrow, f_att_src, f_att_dst, f_bgat, f_ln_g, f_ln_b, slot_table_f, block_tile_f,
                  turns_f, perm_f, gat_table, agg, scores)
        route(nc, const, "r0", scores, EXPERTS0, pong, sorted_x, place, gates, units, cleared)
        run_experts(nc, const, "e0", EXPERTS0, f_w1, f_b1, f_w2, f_b2, ACT.Gelu, sorted_x, units)
        combine(nc, const, "c0", sorted_x, place, gates, pong, state, ping, tables[4])
        one_over_degree(nc, degree, weight)
        pool_nodes("p4", tables[4], weight, pooled[1], ALU.add, 0.0)
        node_layer(nc, const, "sage", "sage", ping, pooled[1], s_w, s_bl, s_g, s_b, state, pong, tables[3])
        project(nc, const, "gate", pong, m_gate, HE, narrow)
        add_bias(nc, narrow, m_gate_b)
        route(nc, const, "r1", narrow, HE, pong, sorted_x, place, gates, units, cleared)
        run_experts(nc, const, "e1", HE, m_w1, m_b1, m_w2, m_b2, ACT.Relu, sorted_x, units)
        combine(nc, const, "c1", sorted_x, place, gates, pong, state, ping, None, m_g, m_b, result)


def has_edges(nc, degree, weight):
    with ExitStack() as ctx:
        k = Kit(nc, ctx, "has")
        s_v = k.sem("v")
        block = ctx.enter_context(nc.Block())

        @block.vector
        def _(dve):
            dve.tensor_scalar(weight[:, :], degree[:, :], 0.5, None, ALU.is_gt).then_inc(s_v, 1)
            dve.wait_ge(s_v, 1)


def one_over_degree(nc, degree, weight):
    with ExitStack() as ctx:
        k = Kit(nc, ctx, "inv")
        s_v = k.sem("v")
        block = ctx.enter_context(nc.Block())

        @block.vector
        def _(dve):
            dve.tensor_scalar(weight[:, :], degree[:, :], 1.0, None, ALU.max).then_inc(s_v, 1)
            dve.wait_ge(s_v, 1)
            dve.reciprocal(weight[:, :], weight[:, :]).then_inc(s_v, 1)
            dve.wait_ge(s_v, 2)


def add_bias(nc, narrow, bias):
    with ExitStack() as ctx:
        k = Kit(nc, ctx, "bias")
        b_sb = k.sb("b", [P, HE])
        s_b, s_v = k.sem("b"), k.sem("v")
        block = ctx.enter_context(nc.Block())

        @block.sync
        def _(sp):
            sp.dma_start(b_sb[:, :], bias.rearrange("(o n) -> o n", o=1).to_broadcast([P, HE])).then_inc(s_b, 16)

        @block.vector
        def _(dve):
            dve.wait_ge(s_b, 16)
            dve.tensor_tensor(narrow[:, :, :], narrow[:, :, :],
                              b_sb[:, :].rearrange("p (o n) -> p o n", o=1).to_broadcast([P, NL, HE]), ALU.add).then_inc(s_v, 1)
            dve.wait_ge(s_v, 1)


_INS = [
    "x", "src", "dst", "L0_gnn_Wp1", "L0_gnn_bp1", "L0_gnn_Wm1", "L0_gnn_bm1", "L0_gnn_Wm2", "L0_gnn_bm2", "L0_gnn_Wm3",
    "L0_gnn_bm3", "L0_gnn_ln2_g", "L0_gnn_ln2_b", "L0_gnn_ln3_g", "L0_gnn_ln3_b", "L0_ffn_W_gat", "L0_ffn_att_src",
    "L0_ffn_att_dst", "L0_ffn_b_gat", "L0_ffn_ln_gamma", "L0_ffn_ln_beta", "L0_ffn_W1", "L0_ffn_b1", "L0_ffn_W2",
    "L0_ffn_b2", "L0_ffn_edge_index", "L1_gnn_W", "L1_gnn_b_l", "L1_gnn_gamma", "L1_gnn_beta", "L1_ffn_gate_w",
    "L1_ffn_gate_b", "L1_ffn_w1", "L1_ffn_b1", "L1_ffn_w2", "L1_ffn_b2", "L1_ffn_gamma", "L1_ffn_beta",
]


def kernel(**inputs):
    import numpy as _np
    import concourse.bacc as _bacc
    from concourse import mybir as _mybir
    from concourse.bass_utils import run_bass_kernel_spmd as _run

    given = {n: _np.asarray(a) for n, a in inputs.items()}
    for n in ("Wp1", "Wm1", "Wm2", "Wm3"):
        given[f"L0_gnn_{n}"] = given[f"L0_gnn_{n}"].T
    given["L1_gnn_W"] = _np.concatenate([given["L1_gnn_W_r"].T, given["L1_gnn_W_l"].T])
    for n in ("L0_ffn_b1", "L1_ffn_b1"):
        e, f = given[n].shape
        given[n] = given[n].reshape(e, f // 128, 128).transpose(0, 2, 1)
    nc = _bacc.Bacc("TRN2", target_bir_lowering=False, num_devices=1)
    arrays, args = {}, []
    for name in _INS:
        a = _np.ascontiguousarray(given[name])
        arrays[f"in_{name}_dram"] = a
        args.append(nc.dram_tensor(f"in_{name}_dram", a.shape, _mybir.dt.from_np(a.dtype), kind="ExternalInput").ap())
    args.append(nc.dram_tensor("out_0_dram", (3125, 256), _mybir.dt.float32, kind="ExternalOutput").ap())
    build(nc, *args)
    r = _run(nc, [arrays], core_ids=[0])
    return r.results[0]["out_0_dram"]
```

```python
import concourse.bass as bass
from concourse import mybir
from contextlib import ExitStack

ALU = mybir.AluOpType
ACT = mybir.ActivationFunctionType
AX_X = mybir.AxisListType.X
F32 = mybir.dt.float32
I32 = mybir.dt.int32
BF16 = mybir.dt.bfloat16

P = 128
N = 3125
C = 256
NT = (N + P - 1) // P
NP = NT * P
LAST = N - (NT - 1) * P
GROUP = 4
GROUPS = NT // GROUP
REST = NT - GROUP * GROUPS
PAD_ROW = NP
POOL_SLOTS = 2
SLOTS = 4
TURN = 16
SPAN = 64
STEP = 4
EPS = 1e-5
LOWEST = -3.0e38


class Chain:

    def __init__(self, eng, sem):
        self.eng, self.sem, self.n = eng, sem, 0

    def mark(self, ins):
        self.n += 1
        return ins.then_inc(self.sem, 1)

    def wait(self):
        self.eng.wait_ge(self.sem, self.n)

    def link(self, ins):
        self.mark(ins)
        self.wait()

    def restart(self):
        self.wait()
        self.eng.sem_clear(self.sem)
        self.n = 0


def hold(eng, sem, value, passed):
    eng.wait_ge(sem, value)
    eng.sem_inc(passed, 1)


class Kit:

    def __init__(self, nc, ctx, stage):
        self.nc, self.ctx, self.stage = nc, ctx, stage
        self.sems = []
        ctx.callback(self.clear)

    def clear(self):
        if self.sems:
            self.nc.clear_and_free_semaphores(self.sems)
            self.nc.all_engine_barrier(sem_only=True)

    def sb(self, name, shape, dt=F32):
        return self.ctx.enter_context(self.nc.sbuf_tensor(f"{self.stage}_{name}", shape, dt))

    def ps(self, name, shape, dt=F32):
        return self.ctx.enter_context(self.nc.psum_tensor(f"{self.stage}_{name}", shape, dt))

    def sem(self, name):
        self.sems.append(self.nc.alloc_semaphore(f"{self.stage}_{name}"))
        return self.sems[-1]

    def pool_dma_sem(self, name):
        return self.nc.alloc_semaphore(f"{self.stage}_{name}")


def slot_capacity(edges, slots):
    most = (edges + edges // P) // slots + 2 * NT
    return -(-most // 640) * 640


def build_constants(nc, const, sorted_x, cleared):
    with ExitStack() as ctx:
        k = Kit(nc, ctx, "const")
        s_set, s_zero = k.sem("set"), k.sem("zero")
        zeros = const["zeros"]
        block = ctx.enter_context(nc.Block())
        per = sorted_x.shape[0] // CLEARS // P

        @block.sync
        def _(sp):
            sp.wait_ge(s_zero, 1)
            for c in range(CLEARS):
                sp.dma_start(sorted_x[c * per * P:(c + 1) * per * P, :].rearrange("(p r) c -> p r c", p=P),
                             zeros[:, 0:C].rearrange("p (o c) -> p o c", o=1).to_broadcast([P, per, C])).then_inc(cleared, 16)

        @block.gpsimd
        def _(pool):
            pool.memset(zeros[:, :], 0.0).then_inc(s_zero, 1)
            pool.memset(const["ident"][:, :], 0.0).then_inc(s_set, 1)
            pool.memset(const["before"][:, :], 1.0).then_inc(s_set, 1)
            pool.memset(const["after"][:, :], 1.0).then_inc(s_set, 1)
            pool.memset(const["ones"][:, :], 1.0).then_inc(s_set, 1)
            pool.memset(const["zero16"][:, :], 0.0).then_inc(s_set, 1)
            pool.memset(const["eps"][:, :], EPS).then_inc(s_set, 1)
            pool.wait_ge(s_set, 6)
            pool.affine_select(out=const["ident"][:, :], in_=const["ident"][:, :], compare_op=ALU.not_equal,
                               fill=1.0, base=0, pattern=[[-1, P]], channel_multiplier=1).then_inc(s_set, 1)
            pool.affine_select(out=const["before"][:, :], in_=const["before"][:, :], compare_op=ALU.is_gt,
                               fill=0.0, base=0, pattern=[[-1, P]], channel_multiplier=1).then_inc(s_set, 1)
            pool.affine_select(out=const["after"][:, :], in_=const["after"][:, :], compare_op=ALU.is_gt,
                               fill=0.0, base=0, pattern=[[1, P]], channel_multiplier=-1).then_inc(s_set, 1)
            pool.iota(const["ramp"][:, :], pattern=[[1, P]], base=0, channel_multiplier=0,
                      allow_small_or_imprecise_dtypes=True).then_inc(s_set, 1)
            pool.iota(const["row"][:, :], pattern=[[0, 1]], base=0, channel_multiplier=1,
                      allow_small_or_imprecise_dtypes=True).then_inc(s_set, 1)
            pool.wait_ge(s_set, 11)


def build_slots(nc, const, name, dst, src, edges, rows, slot_table, tile_of_block, ranked, perm, degree, turns,
                slots, segments=None):
    T = edges // rows
    CH = 20 if T % 20 == 0 else 16
    HALF = CH // 2
    NCH = T // CH
    assert T * rows == edges and NCH * CH == T
    STRIPE = 100 if T % 100 == 0 else P
    NS = T // STRIPE
    cap = slot_capacity(edges, slots)
    per_turn = TURN // slots
    TURN0 = 640 // slots
    META = 3 if segments is not None else 2
    ident, before, ramp, row, ones, zero16 = (const[k] for k in ("ident", "before", "ramp", "row", "ones", "zero16"))
    dst_rows = dst.rearrange("(t e) -> t e", e=rows)
    src_rows = src.rearrange("(t e) -> t e", e=rows)

    with ExitStack() as outer:
        k0 = Kit(nc, outer, name)
        dst_col = k0.sb("dst_col", [P, T])
        src_col = k0.sb("src_col", [P, T], I32)
        hi_col = k0.sb("hi_col", [P, T])
        lo_col = k0.sb("lo_col", [P, T])
        base = k0.sb("base", [P, NT])
        start = k0.sb("start", [P, NT], I32)
        ends_i = k0.sb("ends_i", [P, NT + 1], I32)
        unsorted = k0.sb("unsorted", [P, 1])
        general = k0.sb("general", [P, 1], I32)

        with ExitStack() as ctx:
            k = Kit(nc, ctx, name + "c")
            raw = k.sb("raw", [P, 2, NS, rows], I32)
            rawf = k.sb("rawf", [P, 2, NS, rows])
            hi_i = k.sb("hi_i", [P, T], I32)
            dst_i = k.sb("dst_i", [P, T], I32)
            turned = k.ps("turned", [P, 2, 512])
            s_raw, s_f, s_t, s_c, s_v = (k.sem(n) for n in ("raw", "f", "t", "c", "v"))
            block = ctx.enter_context(nc.Block())

            @block.sync
            def _(sp):
                for w, list_rows in enumerate((dst_rows, src_rows)):
                    sp.dma_start(raw[0:STRIPE, w, :, :], list_rows.rearrange("(s t) e -> t s e", t=STRIPE)).then_inc(s_raw, 16)
                sp.wait_ge(s_raw, 32)

            @block.tensor
            def _(pe):
                pe.wait_ge(s_f, 1)
                for w in range(2):
                    for s in range(NS):
                        nc.tensor.transpose(turned[0:rows, w, STRIPE * s:STRIPE * s + STRIPE], rawf[0:STRIPE, w, s, :],
                                            ident[0:STRIPE, 0:STRIPE]).then_inc(s_t, 1)

            @block.vector
            def _(dve):
                chain = Chain(dve, s_v)
                dve.wait_ge(s_raw, 32)
                dve.tensor_copy(rawf[0:STRIPE, :, :, :], raw[0:STRIPE, :, :, :]).then_inc(s_f, 1)
                dve.wait_ge(s_t, 2 * NS)
                chain.mark(dve.tensor_copy(dst_col[0:rows, :], turned[0:rows, 0, 0:T]))
                chain.mark(dve.tensor_copy(dst_i[0:rows, :], turned[0:rows, 0, 0:T]))
                chain.link(dve.tensor_copy(src_col[0:rows, :], turned[0:rows, 1, 0:T]))
                chain.link(dve.tensor_scalar(hi_i[0:rows, :], dst_i[0:rows, :], 7, None, ALU.logical_shift_right))
                chain.link(dve.tensor_copy(hi_col[0:rows, :], hi_i[0:rows, :]))
                chain.link(dve.scalar_tensor_tensor(out=lo_col[0:rows, :], in0=hi_col[0:rows, :], scalar=-float(P),
                                                    in1=dst_col[0:rows, :], op0=ALU.mult, op1=ALU.add))

        with ExitStack() as ctx:
            k = Kit(nc, ctx, name + "h")
            oh_lo = k.sb("oh_lo", [P, 2, HALF, P], BF16)
            oh_hi = k.sb("oh_hi", [P, 2, HALF, NT], BF16)
            counts = k.ps("counts", [P, NT])
            wrong_total = k.ps("wrong_total", [P, 1])
            s_oh, s_used, s_done, s_pass, s_list, s_seg, s_ch, s_big, s_wrong, s_tail = (
                k.sem(n) for n in ("oh", "used", "done", "pass", "list", "seg", "ch", "big", "wrong", "tail"))
            if segments is not None:
                per = edges // rows
                here = k.sb("here", [P, per], I32)
                next_ = k.sb("next_", [P, per], I32)
                out_of_order = k.sb("out_of_order", [P, per])
                wrong = k.sb("wrong", [P, 1])
                part = edges // STEP // 100
                wide = k.sb("wide", [P, part * STEP + SPAN], I32)
            block = ctx.enter_context(nc.Block())

            if segments is not None:
                @block.sync
                def _(sp):
                    sp.dma_start(here[0:rows, :], dst.rearrange("(p n) -> p n", p=rows)).then_inc(s_list, 16)
                    sp.wait_ge(s_big, 1)
                    whole = (rows - 1) * per
                    sp.dma_start(next_[0:rows - 1, :], dst[1:1 + whole].rearrange("(p n) -> p n", n=per)).then_inc(s_list, 16)
                    sp.dma_start(next_[rows - 1:rows, 0:per - 1], dst[1 + whole:edges].rearrange("(o n) -> o n", o=1)
                                 ).then_inc(s_list, 16)
                    width = part * STEP
                    sp.wait_ge(s_big, 2)
                    sp.dma_start(wide[0:100, 0:width], src.rearrange("(p n) -> p n", n=width)).then_inc(s_tail, 16)
                    sp.dma_start(wide[0:99, width:width + SPAN],
                                 src[width:edges].rearrange("(p n) -> p n", n=width)[:, 0:SPAN]).then_inc(s_tail, 16)
                    sp.wait_ge(s_tail, 32)
                    begin = wide[0:100, 0:1]
                    sp.dma_start(segments.rearrange("(p r) n -> p r n", p=100),
                                 bass.AP(begin.tensor, begin.offset, [begin.ap[0], [STEP, part], [1, SPAN + STEP]])
                                 ).then_inc(s_seg, 16)
                    sp.wait_ge(s_list, 48)
                    sp.wait_ge(s_seg, 16)

                @block.gpsimd
                def _(pool):
                    pool.memset(next_[:, :], 1 << 20).then_inc(s_big, 1)
                    pool.memset(wide[:, :], 0).then_inc(s_big, 1)
                    pool.memset(wrong[:, :], 0.0).then_inc(s_big, 1)

            @block.vector
            def _(dve):
                with dve.Fori(0, NCH) as c:
                    for h in range(2):
                        hold(dve, s_used, 2 * c + h + 1, s_pass)
                        at = bass.ds(c * CH + h * HALF, HALF)
                        dve.tensor_tensor(oh_lo[0:rows, h, :, :],
                                          lo_col[0:rows, at].rearrange("p (t o) -> p t o", o=1).to_broadcast([rows, HALF, P]),
                                          ramp[0:rows, :].rearrange("p (o n) -> p o n", o=1).to_broadcast([rows, HALF, P]),
                                          ALU.is_equal).then_inc(s_oh, 1)
                        dve.tensor_tensor(oh_hi[0:rows, h, :, :],
                                          hi_col[0:rows, at].rearrange("p (t o) -> p t o", o=1).to_broadcast([rows, HALF, NT]),
                                          ramp[0:rows, 0:NT].rearrange("p (o n) -> p o n", o=1).to_broadcast([rows, HALF, NT]),
                                          ALU.is_equal).then_inc(s_oh, 1)
                dve.wait_ge(s_done, 1)
                dve.tensor_copy(degree[:, :], counts[:, :]).then_inc(s_done, 1)
                if segments is not None:
                    chain = Chain(dve, s_ch)
                    dve.wait_ge(s_list, 48)
                    dve.wait_ge(s_big, 3)
                    chain.link(dve.tensor_tensor(out_of_order[0:rows, :], here[0:rows, :], next_[0:rows, :], ALU.is_gt))
                    chain.link(dve.tensor_reduce(wrong[0:rows, :], out_of_order[0:rows, :], AX_X, ALU.add))
                    dve.sem_inc(s_wrong, 1)
                    dve.wait_ge(s_wrong, 2)
                    dve.tensor_copy(unsorted[:, :], wrong_total[:, :]).then_inc(s_wrong, 1)

            @block.tensor
            def _(pe):
                pe.sem_inc(s_used, 2)
                nc.tensor.matmul(counts[:, :], zero16[:, 0:P], zero16[:, 0:NT], start=True, stop=False,
                                 skip_group_check=True)
                with pe.Fori(0, NCH) as c:
                    for h in range(2):
                        pe.wait_ge(s_oh, 4 * c + 2 * h + 2)
                        for j in range(HALF):
                            last = nc.tensor.matmul(counts[:, :], oh_lo[0:rows, h, j, :], oh_hi[0:rows, h, j, :],
                                                    start=False, stop=False, skip_group_check=True)
                        last.then_inc(s_used, 1)
                nc.tensor.matmul(counts[:, :], zero16[:, 0:P], zero16[:, 0:NT], start=False, stop=True,
                                 skip_group_check=True).then_inc(s_done, 1)
                if segments is not None:
                    pe.wait_ge(s_wrong, 1)
                    nc.tensor.matmul(wrong_total[:, :], ones[:, :], wrong[:, :], start=True, stop=True).then_inc(s_wrong, 1)

        with ExitStack() as ctx:
            k = Kit(nc, ctx, name + "r")
            key = k.sb("key", [P, NT])
            node = k.sb("node", [P, NT])
            key_rows = k.sb("key_rows", [NT, P])
            all_keys = k.sb("all_keys", [P, NP])
            larger = k.sb("larger", [P, NP])
            rank = k.sb("rank", [P, NT])
            rank_i = k.sb("rank_i", [P, NT], I32)
            meta = k.sb("meta", [P, NT, META], I32)
            ranked_in = k.sb("ranked_in", [P, NT, META], I32)
            deg_rows = k.sb("deg_rows", [NT, P, META], I32)
            deg_rows_f = k.sb("deg_rows_f", [NT, P])
            most = k.sb("most", [NT, 1])
            most_i = k.sb("most_i", [NT, 1], I32)
            blocks = k.sb("blocks", [NT, 1])
            diag = k.sb("diag", [NT, NT])
            tile_blocks = k.sb("tile_blocks", [P, NT])
            ends = k.sb("ends", [P, NT + 1])
            turn_i = k.sb("turn_i", [P, 2], I32)
            limits = k.sb("limits", [P, NT])
            past = k.sb("past", [P, NT, NT])
            tile_i = k.sb("tile_i", [P, NT], I32)
            tile_f = k.sb("tile_f", [P, NT])
            CB = cap // P
            block_no = k.sb("block_no", [P, CB])
            block_past = k.sb("block_past", [P, CB])
            block_i = k.sb("block_i", [P, CB], I32)
            empty = k.sb("empty", [P, TURN0 * slots], I32)
            signs = k.sb("signs", [P, NP])
            key_less = k.sb("key_less", [P, NT])
            before_tile = k.sb("before_tile", [P, NT])
            too_many = k.sb("too_many", [P, 1])
            keys_t = k.ps("keys_t", [NT, P])
            in_tile_before = k.ps("in_tile_before", [P, NT])
            tile_edges = k.ps("tile_edges", [P, NT])
            blocks_t = k.ps("blocks_t", [P, NT])
            (s_v, s_iota, s_kt, s_kr, s_kd, s_ka, s_ranked, s_rk, s_rd, s_bt, s_bo, s_em, s_tn, s_start, s_pass) = (
                k.sem(n) for n in ("v", "iota", "kt", "kr", "kd", "ka", "ranked", "rk", "rd", "bt", "bo", "em", "tn", "start",
                                   "pass"))
            DVE_TILES = 13
            s_scat = k.pool_dma_sem("scat")
            key_dram = nc.dram_tensor(f"{name}_keys", [NP], F32, kind="Internal").ap()
            block = ctx.enter_context(nc.Block())

            @block.gpsimd
            def _(pool):
                pool.iota(node[:, :], pattern=[[P, NT]], base=0, channel_multiplier=1,
                          allow_small_or_imprecise_dtypes=True).then_inc(s_iota, 1)
                pool.iota(block_no[:, :], pattern=[[1, CB]], base=0, channel_multiplier=CB,
                          allow_small_or_imprecise_dtypes=True).then_inc(s_iota, 1)
                pool.iota(limits[:, :], pattern=[[P, NT]], base=P, channel_multiplier=0,
                          allow_small_or_imprecise_dtypes=True).then_inc(s_iota, 1)
                pool.memset(empty[:, :], PAD_ROW).then_inc(s_iota, 1)
                pool.wait_ge(s_rk, 1)
                for t in range(NT):
                    pool.indirect_dma_start(ranked[:, :], bass.IndirectOffsetOnAxis(ap=rank_i[:, t:t + 1], axis=0),
                                            meta[:, t, :], None).then_inc(s_scat, 16)

            @block.tensor
            def _(pe):
                pe.wait_ge(s_v, 3)
                nc.tensor.transpose(keys_t[:, :], key[:, :], ident[:, :]).then_inc(s_kt, 1)
                if segments is not None:
                    nc.tensor.matmul(in_tile_before[:, :], const["after"][:, :], degree[:, :], start=True, stop=True)
                    nc.tensor.matmul(tile_edges[:, :], ones[:, :], degree[:, :], start=True, stop=True).then_inc(s_start, 1)
                pe.wait_ge(s_bt, 1)
                nc.tensor.matmul(blocks_t[:, :], ones[0:NT, :], diag[:, :], start=True, stop=True).then_inc(s_bt, 1)

            @block.scalar
            def _(act):
                act.wait_ge(s_ka, 16)
                for t in range(DVE_TILES, NT):
                    act.activation(signs[:, :], all_keys[:, :], ACT.Sign, bias=key_less[:, t:t + 1],
                                   accum_out=rank[:, t:t + 1]).then_inc(s_ranked, 1)
                    act.wait_ge(s_ranked, t - DVE_TILES + 1)

            @block.sync
            def _(sp):
                sp.wait_ge(s_kr, 1)
                sp.dma_start(key_dram.rearrange("(t p) -> t p", p=P), key_rows[:, :]).then_inc(s_kd, 16)
                sp.wait_ge(s_kd, 16)
                sp.dma_start(all_keys[:, :], key_dram.rearrange("(o n) -> o n", o=1).to_broadcast([P, NP])).then_inc(s_ka, 16)
                sp.wait_ge(s_scat, 16 * NT)
                sp.dma_start(deg_rows[:, :, :], ranked.rearrange("(t p) w -> t p w", p=P)).then_inc(s_rd, 16)
                sp.dma_start(ranked_in[:, :, :], ranked.rearrange("(t p) w -> p t w", p=P)).then_inc(s_rd, 16)
                sp.wait_ge(s_tn, 1)
                sp.wait_ge(s_iota, 4)
                n_clear = sp.value_load(turn_i[0:1, 1:2], min_val=1, max_val=cap // TURN0)
                with sp.Fori(0, n_clear) as c:
                    sp.dma_start(slot_table[:, bass.ds(c * (TURN0 * slots), TURN0 * slots)], empty[:, :]).then_inc(s_em, 16)
                    hold(sp, s_em, c * 16 + 16, s_pass)
                sp.wait_ge(s_bo, 1)
                sp.dma_start(tile_of_block.rearrange("(p n) -> p n", p=P), block_i[:, :]).then_inc(s_bo, 16)
                sp.wait_ge(s_bo, 17)
                sp.wait_ge(s_rd, 32)

            @block.vector
            def _(dve):
                chain = Chain(dve, s_v)
                dve.wait_ge(s_iota, 3)
                chain.link(dve.tensor_scalar(key[:, :], degree[:, :], 4095.0, 4096.0, ALU.min, ALU.mult))
                chain.link(dve.tensor_tensor(key[:, :], key[:, :], node[:, :], ALU.subtract))
                chain.link(dve.tensor_scalar(key[:, :], key[:, :], 4095.0, None, ALU.add))
                chain.mark(dve.tensor_scalar(key_less[:, :], key[:, :], -1.0, None, ALU.mult))
                chain.mark(dve.tensor_copy(meta[:, :, 0], degree[:, :]))
                chain.mark(dve.tensor_copy(meta[:, :, 1], node[:, :]))
                dve.wait_ge(s_kt, 1)
                dve.tensor_copy(key_rows[:, :], keys_t[:, :]).then_inc(s_kr, 1)
                if segments is not None:
                    dve.wait_ge(s_start, 1)
                    chain.link(dve.tensor_tensor_scan(before_tile[:, :], ones[:, 0:NT], tile_edges[:, :], 0.0, ALU.mult, ALU.add))
                    chain.link(dve.tensor_tensor(before_tile[:, :], before_tile[:, :], tile_edges[:, :], ALU.subtract))
                    chain.link(dve.tensor_tensor(before_tile[:, :], before_tile[:, :], in_tile_before[:, :], ALU.add))
                    chain.link(dve.tensor_copy(meta[:, :, 2], before_tile[:, :]))
                dve.wait_ge(s_ka, 16)
                for t in range(DVE_TILES):
                    chain.mark(dve.tensor_scalar(larger[:, :], all_keys[:, :], key[:, t:t + 1], 0.0, ALU.is_gt, ALU.add,
                                                 accum_out=rank[:, t:t + 1]))
                    chain.wait()
                dve.wait_ge(s_ranked, NT - DVE_TILES)
                chain.link(dve.tensor_scalar(rank[:, DVE_TILES:NT], rank[:, DVE_TILES:NT], NP - 1.0, 0.5, ALU.add, ALU.mult))
                dve.tensor_copy(rank_i[:, :], rank[:, :]).then_inc(s_rk, 1)
                dve.wait_ge(s_rk, 1)
                chain.link(dve.tensor_scalar(tile_i[:, :], rank_i[:, :], 7, None, ALU.logical_shift_right))
                chain.link(dve.tensor_copy(tile_f[:, :], tile_i[:, :]))
                dve.wait_ge(s_rd, 32)
                chain.mark(dve.tensor_copy(perm[:, :], ranked_in[:, :, 1]))
                chain.mark(dve.tensor_copy(degree[:, :], ranked_in[:, :, 0]))
                if segments is not None:
                    chain.mark(dve.tensor_copy(start[:, :], ranked_in[:, :, 2]))
                chain.link(dve.tensor_copy(deg_rows_f[:, :], deg_rows[:, :, 0]))
                chain.link(dve.tensor_reduce(most[:, :], deg_rows_f[:, :], AX_X, ALU.max))
                chain.link(dve.tensor_scalar(most[:, :], most[:, :], slots - 1.0, None, ALU.add))
                chain.link(dve.tensor_copy(most_i[:, :], most[:, :]))
                chain.link(dve.tensor_scalar(most_i[:, :], most_i[:, :], slots.bit_length() - 1, None, ALU.logical_shift_right))
                chain.link(dve.tensor_copy(blocks[:, :], most_i[:, :]))
                chain.mark(dve.tensor_scalar(diag[:, :], ident[0:NT, 0:NT], blocks[:, 0:1], None, ALU.mult))
                chain.wait()
                dve.sem_inc(s_bt, 1)
                dve.wait_ge(s_bt, 2)
                chain.link(dve.tensor_copy(tile_blocks[:, :], blocks_t[:, :]))
                chain.link(dve.tensor_tensor_scan(ends[:, 0:NT], ones[:, 0:NT], tile_blocks[:, :], 0.0, ALU.mult, ALU.add))
                if segments is not None:
                    chain.link(dve.tensor_scalar(too_many[:, :], tile_blocks[:, 0:1], float(SPAN // slots), None, ALU.is_gt))
                    chain.link(dve.tensor_tensor(too_many[:, :], too_many[:, :], unsorted[:, :], ALU.add))
                    chain.link(dve.tensor_scalar(too_many[:, :], too_many[:, :], 1.0, None, ALU.min))
                    chain.mark(dve.tensor_copy(general[:, :], too_many[:, :]))
                    chain.mark(dve.memset(ends_i[:, 0:1], 0))
                    chain.mark(dve.tensor_copy(ends_i[:, 1:NT + 1], ends[:, 0:NT]))
                chain.link(dve.tensor_scalar(ends[:, NT:NT + 1], ends[:, NT - 1:NT], per_turn - 1.0, float(per_turn), ALU.add, ALU.max))
                chain.link(dve.tensor_copy(turn_i[:, 0:1], ends[:, NT:NT + 1]))
                chain.mark(dve.tensor_scalar(turns[0:1, 0:1], turn_i[0:1, 0:1], per_turn.bit_length() - 1, None, ALU.logical_shift_right))
                chain.link(dve.tensor_scalar(ends[:, NT:NT + 1], ends[:, NT - 1:NT], TURN0 + per_turn - 1.0, 1.0 / TURN0, ALU.add, ALU.mult))
                chain.link(dve.tensor_scalar(ends[:, NT:NT + 1], ends[:, NT:NT + 1], 1.0, float(cap // TURN0), ALU.max, ALU.min))
                chain.link(dve.tensor_copy(turn_i[:, 1:2], ends[:, NT:NT + 1]))
                dve.sem_inc(s_tn, 1)
                chain.link(dve.tensor_tensor(
                    past[:, :, :], rank[:, :].rearrange("p (t o) -> p t o", o=1).to_broadcast([P, NT, NT]),
                    limits[:, :].rearrange("p (o j) -> p o j", o=1).to_broadcast([P, NT, NT]), ALU.is_ge))
                chain.link(dve.tensor_tensor(
                    past[:, :, :], past[:, :, :],
                    tile_blocks[:, :].rearrange("p (o j) -> p o j", o=1).to_broadcast([P, NT, NT]), ALU.mult))
                chain.link(dve.tensor_reduce(base[:, :], past[:, :, :], AX_X, ALU.add))
                chain.link(dve.tensor_scalar(base[:, :], base[:, :], float(slots), None, ALU.mult))
                chain.link(dve.scalar_tensor_tensor(out=tile_f[:, :], in0=tile_f[:, :], scalar=-float(P), in1=rank[:, :],
                                                    op0=ALU.mult, op1=ALU.add))
                chain.link(dve.scalar_tensor_tensor(out=base[:, :], in0=tile_f[:, :], scalar=float(cap * slots), in1=base[:, :],
                                                    op0=ALU.mult, op1=ALU.add))
                chain.link(dve.tensor_scalar(block_past[:, :], block_no[:, :], ends[:, 0:1], None, ALU.is_ge))
                for t in range(1, NT):
                    chain.link(dve.scalar_tensor_tensor(out=block_past[:, :], in0=block_no[:, :], scalar=ends[:, t:t + 1],
                                                        in1=block_past[:, :], op0=ALU.is_ge, op1=ALU.add))
                chain.link(dve.tensor_copy(block_i[:, :], block_past[:, :]))
                dve.sem_inc(s_bo, 1)

        with ExitStack() as ctx:
            k = Kit(nc, ctx, name + "s")
            dst_bc = k.sb("dst_bc", [P, 2, HALF * rows], I32)
            dst_lo = k.sb("dst_lo", [P, 2, HALF * rows], I32)
            oh_lo = k.sb("oh_lo", [P, 2, HALF, P], BF16)
            oh_hi = k.sb("oh_hi", [P, 2, HALF, NT], BF16)
            oh_lo_t = k.sb("oh_lo_t", [P, 2, HALF * rows])
            same = k.sb("same", [P, 2, P])
            in_tile = k.sb("in_tile", [P, 2, HALF])
            lookup = k.sb("lookup", [P, 2, NT])
            picked = k.sb("picked", [P, HALF, NT])
            found = k.sb("found", [P, HALF])
            slot_i = k.sb("slot_i", [P, 2, HALF], I32)
            src_i = k.sb("src_i", [P, 2, HALF], I32)
            primed = k.sb("primed", [1, 2], I32)
            counts = k.ps("counts", [P, NT])
            got = k.ps("got", [P, 2, 512])
            (s_bc, s_oh, s_lt, s_cnt, s_snap, s_got, s_slot, s_looked, s_ch, s_pass, s_pass2, s_pass3,
             s_pass4, s_free, s_base, s_blank, s_idx, s_packed) = (
                k.sem(n) for n in ("bc", "oh", "lt", "cnt", "snap", "got", "slot", "looked", "ch", "pass", "pass2",
                                   "pass3", "pass4", "free", "base", "blank", "idx", "packed"))
            s_st = (k.pool_dma_sem("st0"), k.pool_dma_sem("st1"))
            if segments is not None:
                W = NT * SPAN + SPAN
                pieces = k.sb("pieces", [P, NT, SPAN + STEP], I32)
                piecef = k.sb("piecef", [P, NT, SPAN + STEP])
                moved = k.sb("moved", [P, NT, SPAN + STEP])
                valid = k.sb("valid", [P, NT, SPAN])
                packed = k.sb("packed", [P, W], I32)
                piece_row = k.sb("piece_row", [P, NT], I32)
                bit_i = k.sb("bit_i", [P, 2, NT], I32)
                bit = k.sb("bit", [P, 2, NT])
                s_piece = k.pool_dma_sem("piece")
            block = ctx.enter_context(nc.Block())

            def ways(eng, short, long):
                if segments is None:
                    long()
                else:
                    way = eng.value_load(general[0:1, 0:1], min_val=0, max_val=1)
                    with eng.If(way == 0):
                        short()
                    with eng.Else():
                        long()

            @block.sync
            def _(sp):
                def long():
                    with sp.Fori(0, NCH) as c:
                        for h in range(2):
                            hold(sp, s_free, 2 * c + h + 1, s_pass4)
                            sp.dma_start(dst_bc[:, h, :],
                                         dst[bass.ds((c * CH + h * HALF) * rows, HALF * rows)]
                                         .rearrange("(o n) -> o n", o=1).to_broadcast([P, HALF * rows])).then_inc(s_bc, 16)
                            hold(sp, s_bc, (2 * c + h + 1) * 16, s_pass4)

                def short():
                    sp.wait_ge(s_packed, 1)
                    sp.dma_start(slot_table[:, 0:W], packed[:, :]).then_inc(s_packed, 16)
                    sp.wait_ge(s_packed, 17)

                ways(sp, short, long)

            @block.vector
            def _(dve):
                def short():
                    chain = Chain(dve, s_ch)
                    chain.link(dve.tensor_scalar(piece_row[:, :], start[:, :], 2, None, ALU.logical_shift_right))
                    chain.link(dve.tensor_scalar(piece_row[:, :], piece_row[:, :], edges / STEP - 1, None, ALU.min))
                    dve.sem_inc(s_idx, 1)
                    chain.mark(dve.tensor_scalar(bit_i[:, 0, :], start[:, :], 1, None, ALU.bitwise_and))
                    chain.link(dve.tensor_scalar(bit_i[:, 1, :], start[:, :], 1, 1, ALU.logical_shift_right, ALU.bitwise_and))
                    chain.mark(dve.tensor_copy(bit[:, :, :], bit_i[:, :, :]))
                    chain.link(dve.tensor_tensor(
                        valid[:, :, :], ramp[:, 0:SPAN].rearrange("p (o n) -> p o n", o=1).to_broadcast([P, NT, SPAN]),
                        degree[:, :].rearrange("p (t o) -> p t o", o=1).to_broadcast([P, NT, SPAN]), ALU.is_lt))
                    dve.wait_ge(s_piece, 16 * NT)
                    chain.link(dve.tensor_copy(piecef[:, :, :], pieces[:, :, :]))
                    for b, width in ((1, SPAN + 2), (0, SPAN)):
                        by = b + 1
                        chain.link(dve.tensor_tensor(moved[:, :, 0:width], piecef[:, :, by:by + width], piecef[:, :, 0:width],
                                                     ALU.subtract))
                        chain.link(dve.tensor_tensor(
                            moved[:, :, 0:width], moved[:, :, 0:width],
                            bit[:, b, :].rearrange("p (t o) -> p t o", o=1).to_broadcast([P, NT, width]), ALU.mult))
                        chain.link(dve.tensor_tensor(piecef[:, :, 0:width], piecef[:, :, 0:width], moved[:, :, 0:width], ALU.add))
                    chain.link(dve.scalar_tensor_tensor(out=valid[:, :, :], in0=piecef[:, :, 0:SPAN], scalar=-float(PAD_ROW),
                                                        in1=valid[:, :, :], op0=ALU.add, op1=ALU.mult))
                    dve.wait_ge(s_blank, 1)
                    with dve.Fori(0, NT) as t:
                        at = dve.value_load(ends_i[0:1, bass.ds(t, 1)], min_val=0, max_val=NT * SPAN // slots)
                        dve.tensor_scalar(packed[:, bass.ds(at * slots, SPAN)],
                                          valid[:, bass.ds(t, 1), :].rearrange("p o n -> p (o n)"), float(PAD_ROW), None,
                                          ALU.add).then_inc(s_free, 1)
                        hold(dve, s_free, t + 1, s_pass)
                    dve.sem_inc(s_packed, 1)

                def long():
                    chain = Chain(dve, s_ch)
                    dve.sem_inc(s_free, 2)
                    with dve.Fori(0, NCH) as c:
                        for h in range(2):
                            at = bass.ds(c * CH + h * HALF, HALF)
                            hold(dve, s_got, 2 * c + h + 1, s_pass)
                            dve.tensor_tensor(oh_lo[0:rows, h, :, :],
                                              lo_col[0:rows, at].rearrange("p (t o) -> p t o", o=1).to_broadcast([rows, HALF, P]),
                                              ramp[0:rows, :].rearrange("p (o n) -> p o n", o=1).to_broadcast([rows, HALF, P]),
                                              ALU.is_equal).then_inc(s_oh, 1)
                            dve.tensor_tensor(oh_hi[0:rows, h, :, :],
                                              hi_col[0:rows, at].rearrange("p (t o) -> p t o", o=1).to_broadcast([rows, HALF, NT]),
                                              ramp[0:rows, 0:NT].rearrange("p (o n) -> p o n", o=1).to_broadcast([rows, HALF, NT]),
                                              ALU.is_equal).then_inc(s_oh, 1)
                            hold(dve, s_bc, (2 * c + h + 1) * 16, s_pass)
                            chain.link(dve.tensor_scalar(dst_lo[:, h, :], dst_bc[:, h, :], P - 1, None, ALU.bitwise_and))
                            dve.tensor_scalar(oh_lo_t[:, h, :], dst_lo[:, h, :], row[:, 0:1], None, ALU.is_equal).then_inc(s_lt, 1)
                            for j in range(HALF):
                                col = dst_col[0:rows, bass.ds(c * CH + h * HALF + j, 1)]
                                chain.mark(dve.scalar_tensor_tensor(
                                    out=same[0:rows, j % 2, 0:rows], in0=dst_bc[0:rows, h, j * rows:(j + 1) * rows], scalar=col,
                                    in1=before[0:rows, 0:rows], op0=ALU.is_equal, op1=ALU.mult,
                                    accum_out=in_tile[0:rows, h, j:j + 1]))
                                if j % 2 == 1 or j == HALF - 1:
                                    chain.wait()
                            dve.sem_inc(s_free, 1)
                            hold(dve, s_got, 2 * c + h + 3, s_pass)
                            chain.link(dve.tensor_tensor(
                                picked[0:rows, :, :], got[0:rows, h, 0:HALF * NT].rearrange("p (t n) -> p t n", n=NT),
                                oh_hi[0:rows, h, :, :], ALU.mult))
                            chain.link(dve.tensor_reduce(found[0:rows, :], picked[0:rows, :, :], AX_X, ALU.add))
                            hold(dve, s_st[h], 16 * HALF * c + 16, s_pass)
                            chain.mark(dve.tensor_tensor(slot_i[0:rows, h, :], found[0:rows, :], in_tile[0:rows, h, :], ALU.add))
                            chain.link(dve.tensor_copy(src_i[0:rows, h, :], src_col[0:rows, at]))
                            dve.sem_inc(s_slot, 1)
                        chain.restart()

                ways(dve, short, long)

            @block.tensor
            def _(pe):
                def long():
                    pe.sem_inc(s_got, 2)
                    nc.tensor.matmul(counts[:, :], ident[:, :], base[:, :], start=True, stop=False,
                                     skip_group_check=True).then_inc(s_cnt, 1)
                    with pe.Fori(0, NCH) as c:
                        for h in range(2):
                            hold(pe, s_oh, 4 * c + 2 * h + 2, s_pass2)
                            hold(pe, s_lt, 2 * c + h + 1, s_pass2)
                            for j in range(HALF):
                                n = c * CH + h * HALF + j
                                pe.wait_ge(s_snap, n + 1)
                                nc.tensor.matmul(counts[:, :], oh_lo[0:rows, h, j, :], oh_hi[0:rows, h, j, :],
                                                 start=False, stop=False, skip_group_check=True).then_inc(s_cnt, 1)
                                last = nc.tensor.matmul(got[0:rows, h, j * NT:(j + 1) * NT],
                                                        oh_lo_t[:, h, j * rows:(j + 1) * rows], lookup[:, j % 2, :],
                                                        start=True, stop=True, skip_group_check=True)
                                if j == HALF - 1:
                                    last.then_inc(s_got, 1)
                                else:
                                    last.then_inc(s_looked, 1)

                ways(pe, lambda: None, long)

            @block.scalar
            def _(act):
                def long():
                    with act.Fori(0, NCH) as c:
                        for h in range(2):
                            for j in range(HALF):
                                n = c * CH + h * HALF + j
                                act.wait_ge(s_cnt, n + 1)
                                act.activation(lookup[:, j % 2, :], counts[:, :], ACT.Copy).then_inc(s_snap, 1)

                ways(act, lambda: None, long)

            @block.gpsimd
            def _(pool):
                def short():
                    pool.memset(packed[:, :], PAD_ROW).then_inc(s_blank, 1)
                    pool.wait_ge(s_idx, 1)
                    for t in range(NT):
                        pool.indirect_dma_start(pieces[:, t, :], None, segments[:, :],
                                                bass.IndirectOffsetOnAxis(ap=piece_row[:, t:t + 1], axis=0)).then_inc(s_piece, 16)

                def long():
                    for h in range(2):
                        pool.dma_start(primed[0:1, h:h + 1], dst[0:1].rearrange("(o n) -> o n", o=1)).then_inc(s_st[h], 16)
                    with pool.Fori(0, NCH) as c:
                        for h in range(2):
                            hold(pool, s_slot, 2 * c + h + 1, s_pass3)
                            for j in range(HALF):
                                pool.indirect_dma_start(
                                    slot_table.rearrange("p (n o) -> (p n) o", o=1),
                                    bass.IndirectOffsetOnAxis(ap=slot_i[0:rows, h, j:j + 1], axis=0),
                                    src_i[0:rows, h, j:j + 1], None).then_inc(s_st[h], 16)
                    for h in range(2):
                        pool.wait_ge(s_st[h], 16 + 16 * HALF * NCH)

                ways(pool, short, long)


def gather_pass(nc, const, name, table, slot_table, tile_of_block, turns, perm, weight, pooled, op, init):
    slots_of = POOL_SLOTS
    RING = TURN // 2
    NB = RING // slots_of
    most_turns = slot_capacity(50000, slots_of) * slots_of // TURN
    with ExitStack() as ctx:
        k = Kit(nc, ctx, name)
        acc = k.sb("acc", [P, NT + 1, C])
        rows = k.sb("rows", [P, RING, C])
        slots = k.sb("slots", [P, 2, RING], I32)
        tiles = k.sb("tiles", [1, 2, NB], I32)
        s_row = [k.pool_dma_sem(f"row{r}") for r in range(RING)]
        s_slots, s_used, s_acc, s_init, s_fin, s_pass = (
            k.sem(n) for n in ("slots", "used", "acc", "init", "fin", "pass"))
        s_out = k.pool_dma_sem("out")
        block = ctx.enter_context(nc.Block())

        @block.sync
        def _(sp):
            n = sp.value_load(turns[0:1, 0:1], min_val=1, max_val=most_turns)
            with sp.Fori(0, n) as q:
                for h in range(2):
                    hold(sp, s_used, 2 * NB * q + NB * h + NB, s_pass)
                    b = 2 * NB * q + NB * h
                    sp.dma_start(slots[:, h, :], slot_table[:, bass.ds(q * TURN + h * RING, RING)]).then_inc(s_slots, 16)
                    sp.dma_start(tiles[0:1, h, :], tile_of_block[bass.ds(b, NB)].rearrange("(o n) -> o n", o=1)
                                 ).then_inc(s_slots, 16)
                    hold(sp, s_slots, 64 * q + 32 * h + 32, s_pass)

        @block.gpsimd
        def _(pool):
            n = pool.value_load(turns[0:1, 0:1], min_val=1, max_val=most_turns)
            with pool.Fori(0, n) as q:
                for h in range(2):
                    hold(pool, s_slots, 64 * q + 32 * h + 32, s_pass)
                    for u in range(NB):
                        hold(pool, s_used, 2 * NB * q + NB * h + u + NB + 1, s_pass)
                        for s in range(slots_of):
                            r = u * slots_of + s
                            pool.indirect_dma_start(rows[:, r, :], None, table[:, :],
                                                    bass.IndirectOffsetOnAxis(ap=slots[:, h, r:r + 1], axis=0)
                                                    ).then_inc(s_row[r], 16)
            for t in range(NT):
                pool.wait_ge(s_fin, t + 1)
                pool.indirect_dma_start(pooled[:, :], bass.IndirectOffsetOnAxis(ap=perm[:, t:t + 1], axis=0),
                                        acc[:, t, :], None).then_inc(s_out, 16)
            pool.wait_ge(s_out, 16 * NT)

        @block.vector
        def _(dve):
            chain = Chain(dve, s_acc)
            dve.memset(acc[:, :, :], init).then_inc(s_init, 1)
            dve.wait_ge(s_init, 1)
            dve.sem_inc(s_used, 2 * NB)
            n = dve.value_load(turns[0:1, 0:1], min_val=1, max_val=most_turns)
            with dve.Fori(0, n) as q:
                for h in range(2):
                    hold(dve, s_slots, 64 * q + 32 * h + 32, s_pass)
                    for u in range(NB):
                        t = dve.value_load(tiles[0:1, h, u:u + 1], min_val=0, max_val=NT)
                        into = acc[:, bass.ds(t, 1), :].rearrange("p o c -> p (o c)")
                        for s in range(slots_of):
                            r = u * slots_of + s
                            dve.wait_ge(s_row[r], 32 * q + 16 * h + 16)
                            chain.link(dve.tensor_tensor(into, into, rows[:, r, :], op))
                        dve.sem_inc(s_used, 1)
                chain.restart()
            for t in range(NT):
                if weight is None:
                    dve.sem_inc(s_fin, 1)
                else:
                    dve.tensor_scalar(acc[:, t, :], acc[:, t, :], weight[:, t:t + 1], None, ALU.mult).then_inc(s_fin, 1)


def normalise(dve, act_go, act_done, count, chain, n, source, into, stats, mean_var, inverse, passed):
    for u in range(n):
        chain.mark(dve.bn_stats(stats[:, u, :], source(u)))
    chain.wait()
    for u in range(n):
        chain.mark(dve.bn_aggr(mean_var[:, u, :], stats[:, u, :]))
    chain.wait()
    dve.sem_inc(act_go, GROUP)
    hold(dve, act_done, count, passed)
    chain.link(dve.reciprocal(inverse[:, 0:n], inverse[:, 0:n]))
    for u in range(n):
        chain.mark(dve.tensor_scalar(into(u), source(u), mean_var[:, u, 0:1], inverse[:, u:u + 1], ALU.subtract, ALU.mult))
    chain.wait()


def every_turn(eng, first, then):
    if first:
        first(0, GROUP)
    with eng.Fori(0, GROUPS - 1) as i:
        if first:
            first(GROUP * i + GROUP, GROUP)
        then(GROUP * i, GROUP)
    if first:
        first(GROUP * GROUPS, REST)
    then(GROUP * (GROUPS - 1), GROUP)
    then(GROUP * GROUPS, REST)


def tiles_of(a, t, n=1):
    return a[:, bass.ds(t, n), :]


def tile_of(a, t):
    return tiles_of(a, t).rearrange("p o c -> p (o c)")


def same_for(a, n):
    return a[:, :].rearrange("p (o c) -> p o c", o=1).to_broadcast([P, n, C])


def by_tile(dram, t, n):
    return dram[bass.ds(t * P, n * P), :].rearrange("(t p) c -> p t c", p=P)


def node_layer(nc, const, name, kind, own, pooled, w, bias, gamma, beta, x, out, table, x_dram=None,
               embedded=None):
    embed = kind == "embed"
    KC = 2 if embed else 4
    normed = kind in ("mixnorm", "enter", "sage")
    renormed = kind in ("enter", "sage")
    per_turn = {"embed": 1, "mix": 0, "mixnorm": 1, "enter": 2, "sage": 2}[kind]
    if embed:
        own = out
    ident, eps = const["ident"], const["eps"]
    with ExitStack() as ctx:
        k = Kit(nc, ctx, name)
        w_sb = k.sb("w", [P, KC, C])
        bias_sb = k.sb("bias", [P, C])
        gamma_sb = k.sb("gamma", [P, C])
        beta_sb = k.sb("beta", [P, C])
        zero_row = k.sb("zero_row", [1, C])
        staged = k.sb("staged", [P, GROUP, KC * P])
        turned = k.sb("turned", [P, GROUP, KC * P])
        y = k.sb("y", [P, GROUP, C])
        stats = k.sb("stats", [P, GROUP, 6])
        mean_var = k.sb("mean_var", [P, GROUP, 2])
        inverse = k.sb("inverse", [P, GROUP])
        flipped = k.ps("flipped", [P, GROUP, 512])
        product = k.ps("product", [P, GROUP, C])
        (s_w, s_zero, s_x, s_load, s_stage, s_flip, s_turn, s_mm, s_evac, s_sqrt_go, s_sqrt, s_normed, s_out, s_store,
         s_ch, s_pd, s_pp, s_pa, s_pv, s_ps, s_pad) = (
            k.sem(n) for n in ("w", "zero", "x", "load", "stage", "flip", "turn", "mm", "evac", "sqrt_go", "sqrt",
                               "normed", "out", "store", "ch", "pd", "pp", "pa", "pv", "ps", "pad"))
        params = 2 + 2 * normed
        block = ctx.enter_context(nc.Block())

        @block.sync
        def _(sp):
            def parameters():
                sp.dma_start(w_sb[:, :, :], w.rearrange("(k p) n -> p k n", p=P)).then_inc(s_w, 16)
                for to, v in ((bias_sb, bias), (gamma_sb, gamma), (beta_sb, beta))[0:params - 1]:
                    sp.dma_start(to[:, :], v.rearrange("(o n) -> o n", o=1).to_broadcast([P, C])).then_inc(s_w, 16)

            parameters()
            if embed:
                for g in range(GROUPS):
                    sp.dma_start(x[:, GROUP * g:GROUP * g + GROUP, :],
                                 x_dram[GROUP * g * P:GROUP * (g + 1) * P, :].rearrange("(t p) c -> p t c", p=P)).then_inc(s_x, 16)
                    sp.wait_ge(s_x, 16 * g + 16)
                sp.wait_ge(s_zero, 2)
                sp.dma_start(x[0:LAST, NT - 1, :], x_dram[(NT - 1) * P:N, :]).then_inc(s_x, 16)

            def load(t, n):
                hold(sp, s_flip, t + GROUP, s_ps)
                sp.dma_start(staged[:, 0:n, 2 * P:4 * P], by_tile(pooled, t, n)).then_inc(s_load, 16)

            def store(t, n):
                hold(sp, s_out, t + n, s_ps)
                sp.dma_start(by_tile(table, t, n), tiles_of(embedded if embed else out, t, n)).then_inc(s_store, 16)

            if embed:
                every_turn(sp, None, store)
            else:
                load(0, GROUP)
                load(GROUP, GROUP)
                with sp.Fori(0, GROUPS - 2) as i:
                    load(GROUP * i + 2 * GROUP, GROUP)
                    store(GROUP * i, GROUP)
                load(GROUP * GROUPS, REST)
                store(GROUP * (GROUPS - 2), GROUP)
                store(GROUP * (GROUPS - 1), GROUP)
                store(GROUP * GROUPS, REST)
            sp.wait_ge(s_zero, 1)
            sp.dma_start(table[PAD_ROW:PAD_ROW + 1, :], zero_row[:, :]).then_inc(s_pad, 16)
            sp.wait_ge(s_store, 16 * (GROUPS + 1))
            sp.wait_ge(s_pad, 16)

        @block.gpsimd
        def _(pool):
            def stage(t, n):
                for u in range(n):
                    if embed:
                        hold(pool, s_normed, t + u + 1, s_pp)
                    hold(pool, s_flip, t + u + 1, s_pp)
                    pool.tensor_copy(staged[:, u, 0:2 * P], tile_of(own, t + u)).then_inc(s_stage, 1)

            pool.memset(zero_row[:, :], LOWEST if kind == "mixnorm" else 0.0).then_inc(s_zero, 1)
            if embed:
                pool.memset(x[:, NT - 1, :], 0.0).then_inc(s_zero, 1)
            every_turn(pool, None, stage)

        @block.tensor
        def _(pe):
            def turn_over(t, n):
                if not embed:
                    hold(pe, s_load, 4 * t + 16, s_pd)
                for u in range(n):
                    hold(pe, s_stage, t + u + 1, s_pd)
                    hold(pe, s_turn, t + u + 1, s_pd)
                    for c in range(KC):
                        last = nc.tensor.transpose(flipped[:, u, c * P:(c + 1) * P], staged[:, u, c * P:(c + 1) * P], ident[:, :])
                    last.then_inc(s_flip, 1)

            def multiply(t, n):
                hold(pe, s_evac, t + GROUP, s_pd)
                for u in range(n):
                    hold(pe, s_turn, t + u + 1 + GROUP, s_pd)
                    for c in range(KC):
                        last = nc.tensor.matmul(product[:, u, :], turned[:, u, c * P:(c + 1) * P], w_sb[:, c, :],
                                                start=(c == 0), stop=(c == KC - 1))
                    last.then_inc(s_mm, 1)

            pe.sem_inc(s_flip, GROUP)
            pe.sem_inc(s_mm, GROUP)
            pe.wait_ge(s_w, 16 * params)
            every_turn(pe, turn_over, multiply)

        @block.scalar
        def _(act):
            def roots(t, n, r):
                hold(act, s_sqrt_go, per_turn * t + GROUP * (r + 1), s_pa)
                act.activation(inverse[:, 0:n], mean_var[:, 0:n, 1], ACT.Sqrt, bias=eps[:, 0:1]).then_inc(s_sqrt, GROUP)

            def ahead(t, n):
                if embed:
                    roots(t, n, 0)
                for u in range(n):
                    hold(act, s_flip, t + u + 1 + GROUP, s_pa)
                    hold(act, s_mm, t + u + 1, s_pa)
                    act.activation(turned[:, u, :], flipped[:, u, 0:KC * P], ACT.Copy).then_inc(s_turn, 1)

            def then(t, n):
                if not embed:
                    for r in range(per_turn):
                        roots(t, n, r)

            act.sem_inc(s_turn, GROUP)
            every_turn(act, ahead, then)

        @block.vector
        def _(dve):
            chain = Chain(dve, s_ch)
            dve.sem_inc(s_evac, GROUP)
            dve.wait_ge(s_w, 16 * params)

            def norm(t, n, r, source, into):
                normalise(dve, s_sqrt_go, s_sqrt, per_turn * t + GROUP * (r + 1), chain, n, source, into,
                          stats, mean_var, inverse, s_pv)

            def norm_input(t, n):
                hold(dve, s_x, 4 * t + 16, s_pv)
                norm(t, n, 0, lambda u: tile_of(x, t + u), lambda u: tile_of(out, t + u))
                dve.sem_inc(s_normed, n)
                chain.restart()

            def finish(t, n):
                ys, y_tile = y[:, 0:n, :], lambda u: y[:, u, :]
                hold(dve, s_mm, t + n + GROUP, s_pv)
                dve.tensor_tensor(ys, product[:, 0:n, :], same_for(bias_sb, n), ALU.add).then_inc(s_evac, n)
                hold(dve, s_evac, t + n + GROUP, s_pv)
                if not normed:
                    chain.link(dve.tensor_scalar(tiles_of(embedded if embed else out, t, n), ys, 0.0, None, ALU.max))
                else:
                    if kind != "sage":
                        chain.link(dve.scalar_tensor_tensor(out=ys, in0=ys, scalar=0.0, in1=tiles_of(own, t, n),
                                                            op0=ALU.max, op1=ALU.add))
                    norm(t, n, 0, y_tile, y_tile)
                    chain.link(dve.tensor_tensor(ys, ys, same_for(gamma_sb, n), ALU.mult))
                    chain.link(dve.tensor_tensor(ys if renormed else tiles_of(out, t, n), ys, same_for(beta_sb, n), ALU.add))
                if renormed:
                    if kind == "sage":
                        chain.link(dve.scalar_tensor_tensor(out=ys, in0=ys, scalar=0.0, in1=tiles_of(own, t, n),
                                                            op0=ALU.max, op1=ALU.add))
                    chain.link(dve.tensor_tensor(tiles_of(x, t, n), ys, tiles_of(x, t, n), ALU.add))
                    norm(t, n, 1, lambda u: tile_of(x, t + u), lambda u: tile_of(out, t + u))
                dve.sem_inc(s_out, n)
                chain.restart()

            every_turn(dve, norm_input if embed else None, finish)




def project(nc, const, name, own, w, width, out):
    with ExitStack() as ctx:
        k = Kit(nc, ctx, name)
        w_sb = k.sb("w", [P, 2, width])
        staged = k.sb("staged", [P, GROUP, C])
        turned = k.sb("turned", [P, GROUP, C])
        flipped = k.ps("flipped", [P, GROUP, 512])
        product = k.ps("product", [P, GROUP, width])
        s_w, s_stage, s_flip, s_turn, s_mm, s_evac, s_pp, s_pt, s_pa, s_pv = (
            k.sem(n) for n in ("w", "stage", "flip", "turn", "mm", "evac", "pp", "pt", "pa", "pv"))
        block = ctx.enter_context(nc.Block())

        @block.sync
        def _(sp):
            sp.dma_start(w_sb[:, :, :], w.rearrange("(k p) n -> p k n", p=P)).then_inc(s_w, 16)

        @block.gpsimd
        def _(pool):
            def stage(t, n):
                for u in range(n):
                    hold(pool, s_flip, t + u + 1, s_pp)
                    pool.tensor_copy(staged[:, u, :], tile_of(own, t + u)).then_inc(s_stage, 1)

            every_turn(pool, None, stage)

        @block.tensor
        def _(pe):
            def turn_over(t, n):
                for u in range(n):
                    hold(pe, s_stage, t + u + 1, s_pt)
                    hold(pe, s_turn, t + u + 1, s_pt)
                    for c in range(2):
                        last = nc.tensor.transpose(flipped[:, u, c * P:(c + 1) * P], staged[:, u, c * P:(c + 1) * P], ident_of(const))
                    last.then_inc(s_flip, 1)

            def multiply(t, n):
                hold(pe, s_evac, t + GROUP, s_pt)
                for u in range(n):
                    hold(pe, s_turn, t + u + 1 + GROUP, s_pt)
                    for c in range(2):
                        last = nc.tensor.matmul(product[:, u, :], turned[:, u, c * P:(c + 1) * P], w_sb[:, c, :],
                                                start=(c == 0), stop=(c == 1))
                    last.then_inc(s_mm, 1)

            pe.sem_inc(s_flip, GROUP)
            pe.sem_inc(s_mm, GROUP)
            pe.wait_ge(s_w, 16)

            def both(t, n):
                turn_over(t, n)
                multiply(t, n)

            every_turn(pe, None, both)

        @block.scalar
        def _(act):
            def copy_turned(t, n):
                for u in range(n):
                    hold(act, s_flip, t + u + 1 + GROUP, s_pa)
                    hold(act, s_mm, t + u + 1, s_pa)
                    act.activation(turned[:, u, :], flipped[:, u, 0:C], ACT.Copy).then_inc(s_turn, 1)

            act.sem_inc(s_turn, GROUP)
            every_turn(act, None, copy_turned)

        @block.vector
        def _(dve):
            def take(t, n):
                hold(dve, s_mm, t + n + GROUP, s_pv)
                dve.tensor_copy(out[:, bass.ds(t, n), :], product[:, 0:n, :]).then_inc(s_evac, n)

            dve.sem_inc(s_evac, GROUP)
            every_turn(dve, None, take)


def ident_of(const):
    return const["ident"][:, :]


HEADS, EXPERTS0 = 4, 4
HE = HEADS * EXPERTS0
GROW = HE + 2 * HEADS


def attention(nc, const, name, h, att_src, att_dst, b_gat, ln_gamma, ln_beta, slot_table, tile_of_block, turns, perm,
              gat_table, agg, scores):
    RING = 2 * SLOTS

    def over(ap, n):
        return ap.rearrange("p (o n) -> p o n", o=1).to_broadcast([P, NT, n])

    with ExitStack() as ctx:
        k = Kit(nc, ctx, name)
        att = k.sb("att", [P, 5, HE])
        table_rows = k.sb("table_rows", [P, NT, GROW])
        weighted = k.sb("weighted", [P, NT, HE])
        blank = k.sb("blank", [1, GROW])
        own = k.sb("own", [P, NT + 1, GROW])
        peak = k.sb("peak", [P, NT + 1, HEADS])
        total = k.sb("total", [P, NT + 1, HEADS])
        mixed = k.sb("mixed", [P, NT + 1, HE])
        inv = k.sb("inv", [P, NT + 1, HEADS])
        rows = k.sb("rows", [P, RING, GROW])
        slots = k.sb("slots", [P, 2, 2 * SLOTS], I32)
        tiles = k.sb("tiles", [1, 2, 2], I32)
        e = k.sb("e", [P, SLOTS, HEADS])
        e2 = k.sb("e2", [P, SLOTS, HEADS])
        top = k.sb("top", [P, HEADS])
        grown = k.sb("grown", [P, HEADS])
        below = k.sb("below", [P, SLOTS + 1, HEADS])
        p = k.sb("p", [P, SLOTS + 1, HEADS])
        psum_ = k.sb("psum_", [P, HEADS])
        ph = k.sb("ph", [P, SLOTS, HE])
        phsum = k.sb("phsum", [P, HE])
        natural = k.sb("natural", [P, NT, HE])
        mean = k.sb("mean", [P, NT])
        var = k.sb("var", [P, NT])
        s_row = [k.pool_dma_sem(f"row{r}") for r in range(RING)]
        (s_att, s_rows, s_tab, s_slots, s_used, s_ch, s_exp_go, s_exp, s_fin, s_nat, s_sq, s_set, s_pass,
         s_pa, s_pp, s_pv) = (
            k.sem(n) for n in ("att", "rows", "tab", "slots", "used", "ch", "exp_go", "exp", "fin", "nat",
                               "sq", "set", "pass", "pa", "pp", "pv"))
        s_own, s_out = k.pool_dma_sem("own"), k.pool_dma_sem("out")
        block = ctx.enter_context(nc.Block())

        @block.sync
        def _(sp):
            vectors = (att_src.rearrange("h e -> (h e)"), att_dst.rearrange("h e -> (h e)"), b_gat, ln_gamma, ln_beta)
            for j, v in enumerate(vectors):
                sp.dma_start(att[:, j, :], v.rearrange("(o n) -> o n", o=1).to_broadcast([P, HE])).then_inc(s_att, 16)
            sp.wait_ge(s_rows, 1)
            sp.dma_start(gat_table[0:NP, :].rearrange("(t p) c -> p t c", p=P), table_rows[:, :, :]).then_inc(s_tab, 16)
            sp.wait_ge(s_set, 2)
            sp.dma_start(gat_table[PAD_ROW:PAD_ROW + 1, :], blank[:, :]).then_inc(s_tab, 16)
            sp.wait_ge(s_tab, 32)
            n = sp.value_load(turns[0:1, 0:1], min_val=1, max_val=slot_capacity(32768, SLOTS) * SLOTS // TURN)
            with sp.Fori(0, n) as q:
                for hf in range(2):
                    hold(sp, s_used, 4 * q + 2 * hf + 2, s_pass)
                    b = 4 * q + 2 * hf
                    sp.dma_start(slots[:, hf, :], slot_table[:, bass.ds(b * SLOTS, 2 * SLOTS)]).then_inc(s_slots, 16)
                    sp.dma_start(tiles[0:1, hf, :], tile_of_block[bass.ds(b, 2)].rearrange("(o n) -> o n", o=1)
                                 ).then_inc(s_slots, 16)
                    hold(sp, s_slots, 64 * q + 32 * hf + 32, s_pass)
            sp.wait_ge(s_out, 16 * NT)
            sp.dma_start(natural[:, :, :], agg.rearrange("(t p) c -> p t c", p=P)).then_inc(s_nat, 16)

        @block.gpsimd
        def _(pool):
            pool.memset(blank[:, :], 0.0).then_inc(s_set, 1)
            pool.wait_ge(s_set, 1)
            pool.memset(blank[:, HE:HE + HEADS], -1e30).then_inc(s_set, 1)
            pool.memset(own[:, NT, :], 0.0).then_inc(s_set, 1)
            pool.wait_ge(s_tab, 32)
            for t in range(NT):
                pool.indirect_dma_start(own[:, t, :], None, gat_table[:, :],
                                        bass.IndirectOffsetOnAxis(ap=perm[:, t:t + 1], axis=0)).then_inc(s_own, 16)
            n = pool.value_load(turns[0:1, 0:1], min_val=1, max_val=slot_capacity(32768, SLOTS) * SLOTS // TURN)
            with pool.Fori(0, n) as q:
                for hf in range(2):
                    hold(pool, s_slots, 64 * q + 32 * hf + 32, s_pp)
                    for u in range(2):
                        hold(pool, s_used, 4 * q + 2 * hf + u + 3, s_pp)
                        for s in range(SLOTS):
                            r = u * SLOTS + s
                            pool.indirect_dma_start(rows[:, r, :], None, gat_table[:, :],
                                                    bass.IndirectOffsetOnAxis(ap=slots[:, hf, r:r + 1], axis=0)
                                                    ).then_inc(s_row[r], 16)
            pool.wait_ge(s_fin, 1)
            for t in range(NT):
                pool.indirect_dma_start(agg[:, :], bass.IndirectOffsetOnAxis(ap=perm[:, t:t + 1], axis=0),
                                        mixed[:, t, :], None).then_inc(s_out, 16)

        @block.scalar
        def _(act):
            n = act.value_load(turns[0:1, 0:1], min_val=1, max_val=slot_capacity(32768, SLOTS) * SLOTS // TURN)
            with act.Fori(0, n) as q:
                for b in range(4):
                    hold(act, s_exp_go, 4 * q + b + 1, s_pa)
                    act.activation(p[:, :, :], below[:, :, :], ACT.Exp).then_inc(s_exp, 1)
            act.wait_ge(s_sq, 1)
            act.activation(var[:, :], mean[:, :], ACT.Sqrt, bias=const["eps"][:, 0:1]).then_inc(s_sq, 1)

        @block.vector
        def _(dve):
            chain = Chain(dve, s_ch)
            link = chain.link
            dve.wait_ge(s_att, 80)
            chain.mark(dve.tensor_copy(table_rows[:, :, 0:HE], h[:, :, :]))
            for j in range(2):
                link(dve.tensor_tensor(weighted[:, :, :], h[:, :, :], over(att[:, j, :], HE), ALU.mult))
                link(dve.tensor_reduce(table_rows[:, :, HE + j * HEADS:HE + (j + 1) * HEADS],
                                       weighted[:, :, :].rearrange("p t (h e) -> p t h e", h=HEADS), AX_X, ALU.add))
            dve.sem_inc(s_rows, 1)
            dve.wait_ge(s_own, 16 * NT)
            dve.wait_ge(s_set, 3)
            link(dve.tensor_tensor(inv[:, :, :], own[:, :, HE:HE + HEADS], own[:, :, HE + HEADS:GROW], ALU.add))
            link(dve.scalar_tensor_tensor(out=peak[:, :, :], in0=inv[:, :, :], scalar=0.2, in1=inv[:, :, :],
                                          op0=ALU.mult, op1=ALU.max))
            chain.mark(dve.memset(total[:, :, :], 1.0))
            link(dve.tensor_copy(mixed[:, :, :], own[:, :, 0:HE]))
            chain.restart()
            dve.sem_inc(s_used, 4)
            n = dve.value_load(turns[0:1, 0:1], min_val=1, max_val=slot_capacity(32768, SLOTS) * SLOTS // TURN)
            with dve.Fori(0, n) as q:
                for hf in range(2):
                    hold(dve, s_slots, 64 * q + 32 * hf + 32, s_pv)
                    for u in range(2):
                        t = dve.value_load(tiles[0:1, hf, u:u + 1], min_val=0, max_val=NT)

                        def flat(a):
                            return a[:, bass.ds(t, 1), :].rearrange("p o c -> p (o c)")

                        a_dst = own[:, bass.ds(t, 1), HE + HEADS:GROW].to_broadcast([P, SLOTS, HEADS])
                        r0 = u * SLOTS
                        for s in range(SLOTS):
                            hold(dve, s_row[r0 + s], 32 * q + 16 * hf + 16, s_pv)
                        link(dve.tensor_tensor(e[:, :, :], rows[:, r0:r0 + SLOTS, HE:HE + HEADS], a_dst, ALU.add))
                        link(dve.scalar_tensor_tensor(out=e2[:, :, :], in0=e[:, :, :], scalar=0.2, in1=e[:, :, :],
                                                      op0=ALU.mult, op1=ALU.max))
                        link(dve.tensor_reduce(top[:, :], e2[:, :, :].rearrange("p s h -> p h s"), AX_X, ALU.max))
                        link(dve.tensor_tensor(grown[:, :], top[:, :], flat(peak), ALU.max))
                        chain.mark(dve.tensor_tensor(
                            below[:, 0:SLOTS, :], e2[:, :, :],
                            grown[:, :].rearrange("p (o h) -> p o h", o=1).to_broadcast([P, SLOTS, HEADS]), ALU.subtract))
                        link(dve.tensor_tensor(below[:, SLOTS, :], flat(peak), grown[:, :], ALU.subtract))
                        dve.sem_inc(s_exp_go, 1)
                        chain.mark(dve.tensor_copy(flat(peak), grown[:, :]))
                        hold(dve, s_exp, 4 * q + 2 * hf + u + 1, s_pv)
                        chain.mark(dve.tensor_tensor(
                            ph[:, :, :].rearrange("p s (h e) -> p s h e", h=HEADS),
                            rows[:, r0:r0 + SLOTS, 0:HE].rearrange("p s (h e) -> p s h e", h=HEADS),
                            p[:, 0:SLOTS, :].rearrange("p s (h o) -> p s h o", o=1).to_broadcast([P, SLOTS, HEADS, EXPERTS0]),
                            ALU.mult))
                        chain.mark(dve.tensor_reduce(psum_[:, :], p[:, 0:SLOTS, :].rearrange("p s h -> p h s"), AX_X, ALU.add))
                        chain.mark(dve.tensor_tensor(flat(total), flat(total), p[:, SLOTS, :], ALU.mult))
                        chain.mark(dve.tensor_tensor(
                            flat(mixed).rearrange("p (h e) -> p h e", h=HEADS), flat(mixed).rearrange("p (h e) -> p h e", h=HEADS),
                            p[:, SLOTS, :].rearrange("p (h o) -> p h o", o=1).to_broadcast([P, HEADS, EXPERTS0]), ALU.mult))
                        chain.wait()
                        chain.mark(dve.tensor_tensor(flat(total), flat(total), psum_[:, :], ALU.add))
                        link(dve.tensor_reduce(phsum[:, :], ph[:, :, :].rearrange("p s c -> p c s"), AX_X, ALU.add))
                        link(dve.tensor_tensor(flat(mixed), flat(mixed), phsum[:, :], ALU.add))
                        dve.sem_inc(s_used, 1)
                chain.restart()
            link(dve.tensor_scalar(total[:, :, :], total[:, :, :], 1e-16, None, ALU.add))
            link(dve.reciprocal(inv[:, :, :], total[:, :, :]))
            link(dve.tensor_tensor(mixed[:, :, :].rearrange("p t (h e) -> p (t h) e", h=HEADS),
                                   mixed[:, :, :].rearrange("p t (h e) -> p (t h) e", h=HEADS),
                                   inv[:, :, :].rearrange("p t (h o) -> p (t h) o", o=1).to_broadcast([P, (NT + 1) * HEADS, EXPERTS0]),
                                   ALU.mult))
            dve.sem_inc(s_fin, 1)
            dve.wait_ge(s_nat, 16)
            link(dve.tensor_tensor(natural[:, :, :], natural[:, :, :], over(att[:, 2, :], HE), ALU.add))
            link(dve.tensor_reduce(mean[:, :], natural[:, :, :], AX_X, ALU.add))
            link(dve.tensor_scalar(mean[:, :], mean[:, :], 1.0 / HE, None, ALU.mult))
            link(dve.tensor_tensor(natural[:, :, :], natural[:, :, :],
                                   mean[:, :].rearrange("p (t o) -> p t o", o=1).to_broadcast([P, NT, HE]), ALU.subtract))
            link(dve.tensor_tensor(weighted[:, :, :], natural[:, :, :], natural[:, :, :], ALU.mult))
            link(dve.tensor_reduce(mean[:, :], weighted[:, :, :], AX_X, ALU.add))
            link(dve.tensor_scalar(mean[:, :], mean[:, :], 1.0 / HE, None, ALU.mult))
            dve.sem_inc(s_sq, 1)
            dve.wait_ge(s_sq, 2)
            link(dve.reciprocal(mean[:, :], var[:, :]))
            link(dve.tensor_tensor(natural[:, :, :], natural[:, :, :],
                                   mean[:, :].rearrange("p (t o) -> p t o", o=1).to_broadcast([P, NT, HE]), ALU.mult))
            link(dve.tensor_tensor(natural[:, :, :], natural[:, :, :], over(att[:, 3, :], HE), ALU.mult))
            link(dve.tensor_tensor(natural[:, :, :], natural[:, :, :], over(att[:, 4, :], HE), ALU.add))
            link(dve.tensor_reduce(scores[:, :, :], natural[:, :, :].rearrange("p t (h e) -> p t e h", h=HEADS), AX_X, ALU.add))
            link(dve.tensor_scalar(scores[:, :, :], scores[:, :, :], 1.0 / HEADS, None, ALU.mult))


UNIT = 2 * P


def units_most(experts):
    return (2 * N + UNIT * experts) // UNIT


def spill_row(experts):
    return (units_most(experts) + 1) * UNIT


def route(nc, const, name, logits, experts, own, sorted_x, place, gates, units, cleared):
    E = experts
    with ExitStack() as ctx:
        k = Kit(nc, ctx, name)
        full = [P, NT, E]
        best = k.sb("best", [P, 2, NT])
        pick = k.sb("pick", [P, 2, NT, E])
        work = k.sb("work", full)
        rest = k.sb("rest", full)
        index = k.sb("index", [P, NT])
        node = k.sb("node", [P, NT])
        real = k.sb("real", [P, NT])
        spill = k.sb("spill", [P, 2, NT])
        seen = k.sb("seen", [P, NT + 1, E])
        count_i = k.sb("count_i", [P, E], I32)
        n_units = k.sb("n_units", [P, E])
        first = k.sb("first", [P, E])
        spot = k.sb("spot", [P, 2, NT])
        gap = k.sb("gap", [P, NT])
        grow = k.sb("grow", [P, NT])
        denom = k.sb("denom", [P, NT])
        store_at = k.sb("store_at", [P, 2, NT], I32)
        ahead = k.ps("ahead", [P, 512])
        tile_sum = k.ps("tile_sum", [P, 512])
        s_ch, s_set, s_mm, s_pick, s_exp, s_at = (k.sem(n) for n in ("ch", "set", "mm", "pick", "exp", "at"))
        s_store = k.pool_dma_sem("store")
        block = ctx.enter_context(nc.Block())

        def over_tiles(a):
            return a.rearrange("p (o e) -> p o e", o=1).to_broadcast(full)

        def over_experts(a):
            return a.rearrange("p (t o) -> p t o", o=1).to_broadcast(full)

        @block.gpsimd
        def _(pool):
            pool.iota(node[:, :], pattern=[[P, NT]], base=0, channel_multiplier=1,
                      allow_small_or_imprecise_dtypes=True).then_inc(s_set, 1)
            pool.wait_ge(s_at, 1)
            pool.wait_ge(cleared, 16 * CLEARS)
            for c in range(2):
                for t in range(NT):
                    pool.indirect_dma_start(sorted_x[:, :], bass.IndirectOffsetOnAxis(ap=store_at[:, c, t:t + 1], axis=0),
                                            own[:, t, :], None).then_inc(s_store, 16)
            pool.wait_ge(s_store, 16 * 2 * NT)

        @block.tensor
        def _(pe):
            pe.wait_ge(s_pick, 1)
            picks = work[:, :, :].rearrange("p t e -> p (t e)")
            nc.tensor.matmul(ahead[:, 0:NT * E], const["after"][:, :], picks, start=True, stop=True).then_inc(s_mm, 1)
            nc.tensor.matmul(tile_sum[:, 0:NT * E], const["ones"][:, :], picks, start=True, stop=True).then_inc(s_mm, 1)

        @block.scalar
        def _(act):
            act.wait_ge(s_exp, 1)
            act.activation(grow[:, :], gap[:, :], ACT.Exp).then_inc(s_exp, 1)

        @block.vector
        def _(dve):
            chain = Chain(dve, s_ch)
            link = chain.link
            ramp = const["ramp"]
            left = logits
            for c in range(2):
                link(dve.tensor_reduce(best[:, c, :], left[:, :, :], AX_X, ALU.max))
                link(dve.tensor_tensor(work[:, :, :], left[:, :, :], over_experts(best[:, c, :]), ALU.is_equal))
                link(dve.scalar_tensor_tensor(out=work[:, :, :], in0=work[:, :, :], scalar=-64.0,
                                              in1=over_tiles(ramp[:, 0:E]), op0=ALU.mult, op1=ALU.add))
                link(dve.tensor_reduce(index[:, :], work[:, :, :], AX_X, ALU.min))
                link(dve.tensor_scalar(index[:, :], index[:, :], 64.0, None, ALU.add))
                link(dve.tensor_tensor(pick[:, c, :, :], over_tiles(ramp[:, 0:E]), over_experts(index[:, :]), ALU.is_equal))
                if c == 0:
                    link(dve.scalar_tensor_tensor(out=rest[:, :, :], in0=pick[:, 0, :, :], scalar=LOWEST,
                                                  in1=logits[:, :, :], op0=ALU.mult, op1=ALU.add))
                    left = rest
            link(dve.tensor_tensor(gap[:, :], best[:, 1, :], best[:, 0, :], ALU.subtract))
            dve.sem_inc(s_exp, 1)
            dve.wait_ge(s_set, 1)
            link(dve.tensor_scalar(real[:, :], node[:, :], float(N), None, ALU.is_lt))
            for c in range(2):
                chain.mark(dve.tensor_tensor(pick[:, c, :, :], pick[:, c, :, :], over_experts(real[:, :]), ALU.mult))
            chain.wait()
            link(dve.tensor_tensor(work[:, :, :], pick[:, 0, :, :], pick[:, 1, :, :], ALU.add))
            dve.sem_inc(s_pick, 1)
            dve.wait_ge(s_exp, 2)
            link(dve.tensor_scalar(denom[:, :], grow[:, :], 1.0, None, ALU.add))
            link(dve.reciprocal(gates[:, 0, :], denom[:, :]))
            link(dve.tensor_tensor(gates[:, 1, :], grow[:, :], gates[:, 0, :], ALU.mult))
            link(dve.memset(seen[:, 0, :], 0.0))
            dve.wait_ge(s_mm, 2)
            for t in range(NT):
                link(dve.tensor_tensor(seen[:, t + 1, :], seen[:, t, :], tile_sum[:, t * E:(t + 1) * E], ALU.add))
            link(dve.tensor_scalar(n_units[:, :], seen[:, NT, :], UNIT - 1.0, None, ALU.add))
            link(dve.tensor_copy(count_i[:, :], n_units[:, :]))
            link(dve.tensor_scalar(count_i[:, :], count_i[:, :], 8, None, ALU.logical_shift_right))
            link(dve.tensor_scalar(n_units[:, :], count_i[:, :], 1.0, None, ALU.max))
            chain.mark(dve.tensor_copy(units[0:1, 0:E], n_units[0:1, :]))
            link(dve.tensor_tensor_scan(first[:, :], const["ones"][:, 0:E], n_units[:, :], 0.0, ALU.mult, ALU.add))
            link(dve.tensor_tensor(first[:, :], first[:, :], n_units[:, :], ALU.subtract))
            link(dve.tensor_scalar(first[:, :], first[:, :], float(UNIT), None, ALU.mult))
            link(dve.tensor_tensor(rest[:, :, :], seen[:, 0:NT, :], over_tiles(first[:, :]), ALU.add))
            link(dve.tensor_tensor(rest[:, :, :], rest[:, :, :], ahead[:, 0:NT * E].rearrange("p (t e) -> p t e", e=E), ALU.add))
            for c in range(2):
                link(dve.tensor_tensor(work[:, :, :], rest[:, :, :], pick[:, c, :, :], ALU.mult))
                link(dve.tensor_reduce(spot[:, c, :], work[:, :, :], AX_X, ALU.add))
                chain.mark(dve.tensor_copy(place[:, c, :], spot[:, c, :]))
                link(dve.tensor_scalar(spill[:, c, :], node[:, :], float(spill_row(E) - N + UNIT * c), None, ALU.add))
                link(dve.tensor_scalar(denom[:, :], real[:, :], -1.0, 1.0, ALU.mult, ALU.add))
                link(dve.tensor_tensor(spill[:, c, :], spill[:, c, :], denom[:, :], ALU.mult))
                link(dve.tensor_tensor(spot[:, c, :], spot[:, c, :], spill[:, c, :], ALU.add))
                link(dve.tensor_copy(store_at[:, c, :], spot[:, c, :]))
            dve.sem_inc(s_at, 1)


def run_experts(nc, const, name, experts, w1, b1, w2, b2, func, sorted_x, units):
    E, F = experts, w1.shape[2]
    M = F // P
    with ExitStack() as ctx:
        k = Kit(nc, ctx, name)
        w1_sb = k.sb("w1", [P, 2, 2, F])
        w2_sb = k.sb("w2", [P, 2, M, C])
        b1_sb = k.sb("b1", [P, 2, M])
        b2_sb = k.sb("b2", [P, 2, C])
        rows = k.sb("rows", [P, 2, C])
        turned = k.sb("turned", [P, 2, UNIT])
        hidden = k.sb("hidden", [P, M, UNIT])
        y = k.sb("y", [P, 2, C])
        primed = k.sb("primed", [1, 1])
        flipped = k.ps("flipped", [P, 2, UNIT])
        up = k.ps("up", [P, M, 512])
        down = k.ps("down", [P, 2, 512])
        (s_wfree, s_x, s_flip, s_turn, s_up, s_hid, s_down, s_y, s_store, s_pp, s_ps, s_pt, s_pa, s_pv) = (
            k.sem(n) for n in ("wfree", "x", "flip", "turn", "up", "hid", "down", "y", "store", "pp", "ps", "pt", "pa", "pv"))
        s_wt = k.pool_dma_sem("wt")
        block = ctx.enter_context(nc.Block())
        most = units_most(E)

        def per_unit(eng, prepare, work):
            done = eng.alloc_register(f"{name}_{eng.engine.name}_done")
            eng.reg_mov(done, 0)
            with eng.Fori(0, E // 2) as pair:
                for b in range(2):
                    prepare(2 * pair + b, b)
                    n = eng.value_load(units[0:1, bass.ds(2 * pair + b, 1)], min_val=1, max_val=most)
                    with eng.Fori(0, n):
                        work(eng.snap(done, min_val=0, max_val=most - 1), b)
                        eng.reg_add(done, done, 1)
                    if eng is nc.vector:
                        hold(eng, s_y, 2 * eng.snap(done, min_val=0, max_val=most) + 2, s_pv)
                        eng.sem_inc(s_wfree, 1)
            return done

        @block.gpsimd
        def _(pool):
            with pool.Fori(0, E // 2) as pair:
                for b in range(2):
                    hold(pool, s_wfree, 2 * pair + b + 1, s_pp)
                    e = bass.ds(2 * pair + b, 1)
                    pool.dma_start(w1_sb[:, b, :, :], w1[e, :, :].rearrange("o (k p) n -> p (o k) n", p=P)).then_inc(s_wt, 16)
                    pool.dma_start(w2_sb[:, b, :, :], w2[e, :, :].rearrange("o (k p) n -> p (o k) n", p=P)).then_inc(s_wt, 16)
                    pool.dma_start(b1_sb[:, b, :], b1[e, :, :].rearrange("o p m -> p (o m)")).then_inc(s_wt, 16)
                    pool.dma_start(b2_sb[:, b, :], b2[e, :].to_broadcast([P, C])).then_inc(s_wt, 16)
                    hold(pool, s_wt, 128 * pair + 64 * b + 64, s_pp)

        @block.sync
        def _(sp):
            def work(u, b):
                hold(sp, s_y, 2 * u + 4, s_ps)
                sp.dma_start(sorted_x[bass.ds(u * UNIT, UNIT), :].rearrange("(h p) c -> p h c", p=P), y[:, :, :]).then_inc(s_store, 16)

            sp.dma_start(primed[:, :], b2[0:1, 0:1]).then_inc(s_store, 16)
            done = per_unit(sp, lambda e, b: None, work)
            hold(sp, s_store, 16 * sp.snap(done, min_val=1, max_val=most) + 16, s_ps)

        @block.tensor
        def _(pe):
            def turn_over(u):
                hold(pe, s_x, 16 * u + 16, s_pt)
                hold(pe, s_turn, u + 1, s_pt)
                for h in range(2):
                    for c in range(2):
                        t = nc.tensor.transpose(flipped[:, c, h * P:(h + 1) * P], rows[:, h, c * P:(c + 1) * P], ident_of(const))
                t.then_inc(s_flip, 1)

            def work(u, b):
                hold(pe, s_turn, u + 2, s_pt)
                for m in range(M):
                    hold(pe, s_hid, M * u + m + 1, s_pt)
                    for c in range(2):
                        t = nc.tensor.matmul(up[:, m, 0:UNIT], w1_sb[:, b, c, m * P:(m + 1) * P], turned[:, c, :],
                                             start=(c == 0), stop=(c == 1))
                    t.then_inc(s_up, 1)
                turn_over(u + 1)
                for h in range(2):
                    hold(pe, s_y, 2 * u + h + 1, s_pt)
                    for m in range(M):
                        if h == 0:
                            hold(pe, s_hid, M * u + m + 1 + M, s_pt)
                        t = nc.tensor.matmul(down[:, h, 0:C], hidden[:, m, h * P:(h + 1) * P], w2_sb[:, b, m, :],
                                             start=(m == 0), stop=(m == M - 1))
                    t.then_inc(s_down, 1)

            pe.sem_inc(s_down, 2)
            turn_over(0)
            per_unit(pe, lambda e, b: hold(pe, s_wt, 64 * e + 64, s_pt), work)

        @block.scalar
        def _(act):
            def load(u):
                act.dma_start(rows[:, :, :], sorted_x[bass.ds(u * UNIT, UNIT), :].rearrange("(h p) c -> p h c", p=P)).then_inc(s_x, 16)

            def copy_turned(u):
                hold(act, s_flip, u + 1, s_pa)
                load(u + 1)
                act.activation(turned[:, :, :], flipped[:, :, :], ACT.Copy).then_inc(s_turn, 1)

            def work(u, b):
                hold(act, s_down, 2 * u + 2, s_pa)
                for m in range(M):
                    hold(act, s_up, M * u + m + 1, s_pa)
                    act.activation(hidden[:, m, :], up[:, m, 0:UNIT], func, bias=b1_sb[:, b, m:m + 1]).then_inc(s_hid, 1)
                copy_turned(u + 1)

            act.sem_inc(s_turn, 1)
            act.sem_inc(s_hid, M)
            load(0)
            copy_turned(0)
            done = per_unit(act, lambda e, b: hold(act, s_wt, 64 * e + 64, s_pa), work)
            hold(act, s_x, 16 * act.snap(done, min_val=1, max_val=most) + 32, s_pa)

        @block.vector
        def _(dve):
            def work(u, b):
                hold(dve, s_store, 16 * u + 16, s_pv)
                for h in range(2):
                    hold(dve, s_down, 2 * u + h + 3, s_pv)
                    dve.tensor_tensor(y[:, h, :], down[:, h, 0:C], b2_sb[:, b, :], ALU.add).then_inc(s_y, 1)

            dve.sem_inc(s_y, 2)
            dve.sem_inc(s_wfree, 2)
            per_unit(dve, lambda e, b: hold(dve, s_wt, 64 * e + 64, s_pv), work)


def combine(nc, const, name, sorted_y, place, gates, own, x, out, table=None, gamma=None, beta=None, result=None):
    final = gamma is not None
    with ExitStack() as ctx:
        k = Kit(nc, ctx, name)
        y = k.sb("y", [P, NT, 2, C])
        gamma_sb = k.sb("gamma", [P, C])
        beta_sb = k.sb("beta", [P, C])
        zero_row = k.sb("zero_row", [1, C])
        moe = k.sb("moe", [P, GROUP, C])
        stats = k.sb("stats", [P, GROUP, 6])
        mean_var = k.sb("mean_var", [P, GROUP, 2])
        inverse = k.sb("inverse", [P, GROUP])
        s_y = [k.pool_dma_sem(f"y{i}") for i in range(2)]
        s_w, s_zero, s_got, s_sqrt_go, s_sqrt, s_out, s_store, s_ch, s_ps, s_pa, s_pv = (
            k.sem(n) for n in ("w", "zero", "got", "sqrt_go", "sqrt", "out", "store", "ch", "ps", "pa", "pv"))
        block = ctx.enter_context(nc.Block())

        @block.gpsimd
        def _(pool):
            def landed(g):
                n = GROUP if g < GROUPS else REST
                pool.wait_ge(s_y[g % 2], 32 * (GROUP * (g // 2) + n))
                pool.sem_inc(s_got, n)

            pool.memset(zero_row[:, :], 0.0).then_inc(s_zero, 1)
            for t in range(NT):
                for c in range(2):
                    pool.indirect_dma_start(y[:, t, c, :], None, sorted_y[:, :],
                                            bass.IndirectOffsetOnAxis(ap=place[:, c, t:t + 1], axis=0)
                                            ).then_inc(s_y[t // GROUP % 2], 16)
                if t % GROUP == 1 and t > GROUP:
                    landed(t // GROUP - 1)
            landed(GROUPS - 1)
            landed(GROUPS)

        @block.sync
        def _(sp):
            def store(t, n):
                hold(sp, s_out, t + n, s_ps)
                sp.dma_start(by_tile(result if final else table, t, n), tiles_of(out, t, n)).then_inc(s_store, 16)

            if final:
                sp.dma_start(gamma_sb[:, :], gamma.rearrange("(o n) -> o n", o=1).to_broadcast([P, C])).then_inc(s_w, 16)
                sp.dma_start(beta_sb[:, :], beta.rearrange("(o n) -> o n", o=1).to_broadcast([P, C])).then_inc(s_w, 16)
            with sp.Fori(0, GROUPS) as i:
                store(GROUP * i, GROUP)
            if final:
                sp.wait_ge(s_out, NT)
                sp.dma_start(result[(NT - 1) * P:N, :], out[0:LAST, NT - 1, :]).then_inc(s_store, 16)
            else:
                store(GROUP * GROUPS, REST)
                sp.wait_ge(s_zero, 1)
                sp.dma_start(table[PAD_ROW:PAD_ROW + 1, :], zero_row[:, :]).then_inc(s_w, 16)
                sp.wait_ge(s_w, 16)
            sp.wait_ge(s_store, 16 * (GROUPS + 1))

        @block.scalar
        def _(act):
            def root(t, n):
                hold(act, s_sqrt_go, t + GROUP, s_pa)
                act.activation(inverse[:, 0:n], mean_var[:, 0:n, 1], ACT.Sqrt, bias=const["eps"][:, 0:1]).then_inc(s_sqrt, GROUP)

            every_turn(act, None, root)

        @block.vector
        def _(dve):
            chain = Chain(dve, s_ch)
            if final:
                dve.wait_ge(s_w, 32)

            def mix(t, n):
                moes, moe_tile = moe[:, 0:n, :], lambda u: moe[:, u, :]
                hold(dve, s_got, t + n, s_pv)
                for c in range(2):
                    for u in range(n):
                        row = y[:, bass.ds(t + u, 1), c, :].rearrange("p o c -> p (o c)")
                        chain.mark(dve.scalar_tensor_tensor(
                            out=moe[:, u, :], in0=row, scalar=gates[:, c, bass.ds(t + u, 1)],
                            in1=tile_of(own if final else x, t + u) if c == 0 else moe[:, u, :], op0=ALU.mult, op1=ALU.add))
                    chain.wait()
                if final:
                    normalise(dve, s_sqrt_go, s_sqrt, t + GROUP, chain, n, moe_tile, moe_tile, stats, mean_var, inverse, s_pv)
                    chain.link(dve.tensor_tensor(moes, moes, same_for(gamma_sb, n), ALU.mult))
                    chain.link(dve.tensor_tensor(moes, moes, same_for(beta_sb, n), ALU.add))
                    chain.link(dve.tensor_tensor(tiles_of(out, t, n), moes, tiles_of(x, t, n), ALU.add))
                else:
                    chain.mark(dve.tensor_copy(tiles_of(x, t, n), moes))
                    normalise(dve, s_sqrt_go, s_sqrt, t + GROUP, chain, n, moe_tile, lambda u: tile_of(out, t + u),
                              stats, mean_var, inverse, s_pv)
                dve.sem_inc(s_out, n)
                chain.restart()

            every_turn(dve, None, mix)


CLEARS = 8


def build(nc, x, src, dst,
          g_wp1, g_bp1, g_wm1, g_bm1, g_wm2, g_bm2, g_wm3, g_bm3, g_ln2_g, g_ln2_b, g_ln3_g, g_ln3_b,
          f_wgat, f_att_src, f_att_dst, f_bgat, f_ln_g, f_ln_b, f_w1, f_b1, f_w2, f_b2, f_edges,
          s_w, s_bl, s_g, s_b, m_gate, m_gate_b, m_w1, m_b1, m_w2, m_b2, m_g, m_b, result):
    with ExitStack() as ctx:
        def sb(name, shape, dt=F32):
            return ctx.enter_context(nc.sbuf_tensor(name, shape, dt))

        def dram(name, shape, dt=F32):
            return nc.dram_tensor(name, shape, dt, kind="Internal").ap()

        const = {"ident": sb("ident", [P, P]), "before": sb("before", [P, P]), "after": sb("after", [P, P]),
                 "ones": sb("ones", [P, P]), "ramp": sb("ramp", [P, P]), "row": sb("row", [P, 1]),
                 "zero16": sb("zero16", [P, P], BF16), "eps": sb("eps", [P, 1]), "zeros": sb("zeros", [P, C])}
        state = sb("state", [P, NT, C])
        ping = sb("ping", [P, NT, C])
        pong = sb("pong", [P, NT, C])
        narrow = sb("narrow", [P, NT, HE])
        scores = sb("scores", [P, NT, EXPERTS0])
        place = sb("place", [P, 2, NT], I32)
        gates = sb("gates", [P, 2, NT])
        units = sb("units", [1, HE], I32)
        perm = sb("perm", [P, NT], I32)
        degree = sb("degree", [P, NT])
        weight = sb("weight", [P, NT])
        turns = sb("turns", [1, 2], I32)
        perm_f = sb("perm_f", [P, NT], I32)
        degree_f = sb("degree_f", [P, NT])
        turns_f = sb("turns_f", [1, 2], I32)

        edges, f_n = dst.shape[0], f_edges.shape[1]
        cap, cap_f = slot_capacity(edges, POOL_SLOTS), slot_capacity(f_n, SLOTS)
        slot_table, slot_table_f = dram("slot_table", [P, cap * POOL_SLOTS], I32), dram("slot_table_f", [P, cap_f * SLOTS], I32)
        block_tile, block_tile_f = dram("block_tile", [cap], I32), dram("block_tile_f", [cap_f], I32)
        ranked, ranked_f = dram("ranked", [NP, 3], I32), dram("ranked_f", [NP, 2], I32)
        segments = dram("segments", [edges // STEP, SPAN + STEP], I32)
        tables = [dram(f"table{i}", [PAD_ROW + 1, C]) for i in range(5)]
        gat_table = dram("gat_table", [PAD_ROW + 1, GROW])
        pooled = [dram(f"pooled{i}", [NP, C]) for i in range(2)]
        agg = dram("agg", [NP, HE])
        most_rows = spill_row(HE) + 2 * UNIT
        sorted_x = dram("sorted_x", [-(-most_rows // (CLEARS * P)) * CLEARS * P, C])
        cleared = ctx.enter_context(nc.semaphore("cleared"))

        build_constants(nc, const, sorted_x, cleared)
        build_slots(nc, const, "A", dst, src, edges, 125, slot_table, block_tile, ranked, perm, degree, turns,
                    POOL_SLOTS, segments)
        build_slots(nc, const, "B", f_edges[1, :], f_edges[0, :], f_n, P, slot_table_f, block_tile_f, ranked_f,
                    perm_f, degree_f, turns_f, SLOTS)

        def pool_nodes(name, table, factor, into, op, init):
            gather_pass(nc, const, name, table, slot_table, block_tile, turns, perm, factor, into, op, init)

        node_layer(nc, const, "embed", "embed", None, None, g_wp1, g_bp1, None, None, state, ping, tables[0], x, pong)
        pool_nodes("p1", tables[0], None, pooled[0], ALU.max, 0.0)
        node_layer(nc, const, "mix1", "mix", ping, pooled[0], g_wm1, g_bm1, None, None, state, pong, tables[1])
        pool_nodes("p2", tables[1], None, pooled[1], ALU.max, 0.0)
        node_layer(nc, const, "mix2", "mixnorm", pong, pooled[1], g_wm2, g_bm2, g_ln2_g, g_ln2_b, state, ping, tables[2])
        has_edges(nc, degree, weight)
        pool_nodes("p3", tables[2], weight, pooled[0], ALU.max, LOWEST)
        node_layer(nc, const, "mix3", "enter", ping, pooled[0], g_wm3, g_bm3, g_ln3_g, g_ln3_b, state, pong, tables[3])
        project(nc, const, "gat", pong, f_wgat, HE, narrow)
        attention(nc, const, "att", narrow, f_att_src, f_att_dst, f_bgat, f_ln_g, f_ln_b, slot_table_f, block_tile_f,
                  turns_f, perm_f, gat_table, agg, scores)
        route(nc, const, "r0", scores, EXPERTS0, pong, sorted_x, place, gates, units, cleared)
        run_experts(nc, const, "e0", EXPERTS0, f_w1, f_b1, f_w2, f_b2, ACT.Gelu, sorted_x, units)
        combine(nc, const, "c0", sorted_x, place, gates, pong, state, ping, tables[4])
        one_over_degree(nc, degree, weight)
        pool_nodes("p4", tables[4], weight, pooled[1], ALU.add, 0.0)
        node_layer(nc, const, "sage", "sage", ping, pooled[1], s_w, s_bl, s_g, s_b, state, pong, tables[3])
        project(nc, const, "gate", pong, m_gate, HE, narrow)
        add_bias(nc, narrow, m_gate_b)
        route(nc, const, "r1", narrow, HE, pong, sorted_x, place, gates, units, cleared)
        run_experts(nc, const, "e1", HE, m_w1, m_b1, m_w2, m_b2, ACT.Relu, sorted_x, units)
        combine(nc, const, "c1", sorted_x, place, gates, pong, state, ping, None, m_g, m_b, result)


def has_edges(nc, degree, weight):
    with ExitStack() as ctx:
        k = Kit(nc, ctx, "has")
        s_v = k.sem("v")
        block = ctx.enter_context(nc.Block())

        @block.vector
        def _(dve):
            dve.tensor_scalar(weight[:, :], degree[:, :], 0.5, None, ALU.is_gt).then_inc(s_v, 1)
            dve.wait_ge(s_v, 1)


def one_over_degree(nc, degree, weight):
    with ExitStack() as ctx:
        k = Kit(nc, ctx, "inv")
        s_v = k.sem("v")
        block = ctx.enter_context(nc.Block())

        @block.vector
        def _(dve):
            dve.tensor_scalar(weight[:, :], degree[:, :], 1.0, None, ALU.max).then_inc(s_v, 1)
            dve.wait_ge(s_v, 1)
            dve.reciprocal(weight[:, :], weight[:, :]).then_inc(s_v, 1)
            dve.wait_ge(s_v, 2)


def add_bias(nc, narrow, bias):
    with ExitStack() as ctx:
        k = Kit(nc, ctx, "bias")
        b_sb = k.sb("b", [P, HE])
        s_b, s_v = k.sem("b"), k.sem("v")
        block = ctx.enter_context(nc.Block())

        @block.sync
        def _(sp):
            sp.dma_start(b_sb[:, :], bias.rearrange("(o n) -> o n", o=1).to_broadcast([P, HE])).then_inc(s_b, 16)

        @block.vector
        def _(dve):
            dve.wait_ge(s_b, 16)
            dve.tensor_tensor(narrow[:, :, :], narrow[:, :, :],
                              b_sb[:, :].rearrange("p (o n) -> p o n", o=1).to_broadcast([P, NT, HE]), ALU.add).then_inc(s_v, 1)
            dve.wait_ge(s_v, 1)


_INS = [
    "x", "src", "dst", "L0_gnn_Wp1", "L0_gnn_bp1", "L0_gnn_Wm1", "L0_gnn_bm1", "L0_gnn_Wm2", "L0_gnn_bm2", "L0_gnn_Wm3",
    "L0_gnn_bm3", "L0_gnn_ln2_g", "L0_gnn_ln2_b", "L0_gnn_ln3_g", "L0_gnn_ln3_b", "L0_ffn_W_gat", "L0_ffn_att_src",
    "L0_ffn_att_dst", "L0_ffn_b_gat", "L0_ffn_ln_gamma", "L0_ffn_ln_beta", "L0_ffn_W1", "L0_ffn_b1", "L0_ffn_W2",
    "L0_ffn_b2", "L0_ffn_edge_index", "L1_gnn_W", "L1_gnn_b_l", "L1_gnn_gamma", "L1_gnn_beta", "L1_ffn_gate_w",
    "L1_ffn_gate_b", "L1_ffn_w1", "L1_ffn_b1", "L1_ffn_w2", "L1_ffn_b2", "L1_ffn_gamma", "L1_ffn_beta",
]


def kernel(**inputs):
    import numpy as _np
    import concourse.bacc as _bacc
    from concourse import mybir as _mybir
    from concourse.bass_utils import run_bass_kernel_spmd as _run

    given = {n: _np.asarray(a) for n, a in inputs.items()}
    for n in ("Wp1", "Wm1", "Wm2", "Wm3"):
        given[f"L0_gnn_{n}"] = given[f"L0_gnn_{n}"].T
    given["L1_gnn_W"] = _np.concatenate([given["L1_gnn_W_r"].T, given["L1_gnn_W_l"].T])
    for n in ("L0_ffn_b1", "L1_ffn_b1"):
        e, f = given[n].shape
        given[n] = given[n].reshape(e, f // 128, 128).transpose(0, 2, 1)
    nc = _bacc.Bacc("TRN2", target_bir_lowering=False, num_devices=1)
    arrays, args = {}, []
    for name in _INS:
        a = _np.ascontiguousarray(given[name])
        arrays[f"in_{name}_dram"] = a
        args.append(nc.dram_tensor(f"in_{name}_dram", a.shape, _mybir.dt.from_np(a.dtype), kind="ExternalInput").ap())
    args.append(nc.dram_tensor("out_0_dram", (3125, 256), _mybir.dt.float32, kind="ExternalOutput").ap())
    build(nc, *args)
    r = _run(nc, [arrays], core_ids=[0])
    return r.results[0]["out_0_dram"]
```

```python
import concourse.bass as bass
from concourse import mybir
from contextlib import ExitStack

ALU = mybir.AluOpType
ACT = mybir.ActivationFunctionType
AX_X = mybir.AxisListType.X
F32 = mybir.dt.float32
I32 = mybir.dt.int32
BF16 = mybir.dt.bfloat16

P = 128
N = 3125
C = 256
NT = (N + P - 1) // P
NP = NT * P
LAST = N - (NT - 1) * P
GROUP = 4
GROUPS = NT // GROUP
REST = NT - GROUP * GROUPS
PAD_ROW = NP
POOL_SLOTS = 2
SLOTS = 4
TURN = 16
SPAN = 64
STEP = 4
EPS = 1e-5
LOWEST = -3.0e38


class Chain:

    def __init__(self, eng, sem):
        self.eng, self.sem, self.n = eng, sem, 0

    def mark(self, ins):
        self.n += 1
        return ins.then_inc(self.sem, 1)

    def wait(self):
        self.eng.wait_ge(self.sem, self.n)

    def link(self, ins):
        self.mark(ins)
        self.wait()

    def restart(self):
        self.wait()
        self.eng.sem_clear(self.sem)
        self.n = 0


def hold(eng, sem, value, passed):
    eng.wait_ge(sem, value)
    eng.sem_inc(passed, 1)


class Kit:

    def __init__(self, nc, ctx, stage):
        self.nc, self.ctx, self.stage = nc, ctx, stage
        self.sems = []
        ctx.callback(self.clear)

    def clear(self):
        if self.sems:
            self.nc.clear_and_free_semaphores(self.sems)
            self.nc.all_engine_barrier(sem_only=True)

    def sb(self, name, shape, dt=F32):
        return self.ctx.enter_context(self.nc.sbuf_tensor(f"{self.stage}_{name}", shape, dt))

    def ps(self, name, shape, dt=F32):
        return self.ctx.enter_context(self.nc.psum_tensor(f"{self.stage}_{name}", shape, dt))

    def sem(self, name):
        self.sems.append(self.nc.alloc_semaphore(f"{self.stage}_{name}"))
        return self.sems[-1]

    def pool_dma_sem(self, name):
        return self.nc.alloc_semaphore(f"{self.stage}_{name}")


def slot_capacity(edges, slots):
    most = (edges + edges // P) // slots + 2 * NT
    return -(-most // 640) * 640


def start_transfers(nc, const, sorted_x, cleared, x_dram, x, x_loaded):
    with ExitStack() as ctx:
        block = ctx.enter_context(nc.Block())
        per = sorted_x.shape[0] // CLEARS // P

        @block.sync
        def _(sp):
            sp.dma_start(x[:, 0:NT - 1, :], x_dram[0:(NT - 1) * P, :].rearrange("(t p) c -> p t c", p=P)).then_inc(x_loaded, 16)
            sp.dma_start(x[0:LAST, NT - 1, :], x_dram[(NT - 1) * P:N, :]).then_inc(x_loaded, 16)
            for c in range(CLEARS):
                sp.dma_start(sorted_x[c * per * P:(c + 1) * per * P, :].rearrange("(p r) c -> p r c", p=P),
                             const["zeros"][:, 0:C].rearrange("p (o c) -> p o c", o=1).to_broadcast([P, per, C])
                             ).then_inc(cleared, 16)


def build_constants(nc, const, x):
    with ExitStack() as ctx:
        k = Kit(nc, ctx, "const")
        s_set = k.sem("set")
        zeros = const["zeros"]
        block = ctx.enter_context(nc.Block())

        @block.gpsimd
        def _(pool):
            pool.memset(zeros[:, :], 0.0).then_inc(s_set, 1)
            pool.memset(x[:, NT - 1, :], 0.0).then_inc(s_set, 1)
            pool.memset(const["ident"][:, :], 0.0).then_inc(s_set, 1)
            pool.memset(const["before"][:, :], 1.0).then_inc(s_set, 1)
            pool.memset(const["after"][:, :], 1.0).then_inc(s_set, 1)
            pool.memset(const["ones"][:, :], 1.0).then_inc(s_set, 1)
            pool.memset(const["zero16"][:, :], 0.0).then_inc(s_set, 1)
            pool.memset(const["eps"][:, :], EPS).then_inc(s_set, 1)
            pool.wait_ge(s_set, 8)
            pool.affine_select(out=const["ident"][:, :], in_=const["ident"][:, :], compare_op=ALU.not_equal,
                               fill=1.0, base=0, pattern=[[-1, P]], channel_multiplier=1).then_inc(s_set, 1)
            pool.affine_select(out=const["before"][:, :], in_=const["before"][:, :], compare_op=ALU.is_gt,
                               fill=0.0, base=0, pattern=[[-1, P]], channel_multiplier=1).then_inc(s_set, 1)
            pool.affine_select(out=const["after"][:, :], in_=const["after"][:, :], compare_op=ALU.is_gt,
                               fill=0.0, base=0, pattern=[[1, P]], channel_multiplier=-1).then_inc(s_set, 1)
            pool.iota(const["ramp"][:, :], pattern=[[1, P]], base=0, channel_multiplier=0,
                      allow_small_or_imprecise_dtypes=True).then_inc(s_set, 1)
            pool.iota(const["row"][:, :], pattern=[[0, 1]], base=0, channel_multiplier=1,
                      allow_small_or_imprecise_dtypes=True).then_inc(s_set, 1)
            pool.wait_ge(s_set, 13)


class EdgeList:

    def __init__(self, name, dst, src, edges, rows, slot_table, tile_of_block, ranked, perm, degree, turns, slots,
                 segments=None, has_edges=None, over_degree=None):
        self.name, self.dst, self.src, self.edges, self.rows = name, dst, src, edges, rows
        self.slot_table, self.tile_of_block, self.ranked, self.perm, self.degree, self.turns = (
            slot_table, tile_of_block, ranked, perm, degree, turns)
        self.slots, self.segments, self.has_edges, self.over_degree = slots, segments, has_edges, over_degree
        self.T = edges // rows
        self.CH = 20 if self.T % 20 == 0 else 16
        self.HALF = self.CH // 2
        self.NCH = self.T // self.CH
        assert self.T * rows == edges and self.NCH * self.CH == self.T
        self.cap = slot_capacity(edges, slots)
        self.per_turn = TURN // slots
        self.TURN0 = 640 // slots
        self.halves = segments is not None
        self.META = 3 if segments is not None else 2

    def keep(self, nc, ctx):
        k, T = Kit(nc, ctx, self.name), self.T
        self.dst_col = k.sb("dst_col", [P, T])
        self.src_col = k.sb("src_col", [P, T], I32)
        self.hi_col = k.sb("hi_col", [P, T])
        self.lo_col = k.sb("lo_col", [P, T])
        self.base = k.sb("base", [P, NT])
        self.start = k.sb("start", [P, NT], I32)
        self.ends_i = k.sb("ends_i", [P, NT + 1], I32)
        self.unsorted = k.sb("unsorted", [P, 1])
        self.general = k.sb("general", [P, 1], I32)


def sort_lists(nc, const, lists, transfers):
    with ExitStack() as ctx:
        for L in lists:
            L.keep(nc, ctx)
        for L in lists:
            list_columns(nc, const, L)
        transfers()
        for L in lists:
            count_degrees(nc, const, L)
        rank_nodes(nc, const, lists)
        for L in lists:
            fill_slots(nc, const, L)


def list_columns(nc, const, L):
    name, rows, T, dst_col, src_col, hi_col, lo_col = L.name, L.rows, L.T, L.dst_col, L.src_col, L.hi_col, L.lo_col
    ident = const["ident"]
    STRIPE = 100 if T % 100 == 0 else P
    NS = T // STRIPE
    dst_rows = L.dst.rearrange("(t e) -> t e", e=rows)
    src_rows = L.src.rearrange("(t e) -> t e", e=rows)
    with ExitStack() as ctx:
        k = Kit(nc, ctx, name + "c")
        raw = k.sb("raw", [P, 2, NS, rows], I32)
        rawf = k.sb("rawf", [P, 2, NS, rows])
        hi_i = k.sb("hi_i", [P, T], I32)
        dst_i = k.sb("dst_i", [P, T], I32)
        turned = k.ps("turned", [P, 2, 512])
        s_raw, s_f, s_t, s_c, s_v = (k.sem(n) for n in ("raw", "f", "t", "c", "v"))
        block = ctx.enter_context(nc.Block())

        @block.sync
        def _(sp):
            for w, list_rows in enumerate((dst_rows, src_rows)):
                sp.dma_start(raw[0:STRIPE, w, :, :], list_rows.rearrange("(s t) e -> t s e", t=STRIPE)).then_inc(s_raw, 16)
            sp.wait_ge(s_raw, 32)

        @block.tensor
        def _(pe):
            pe.wait_ge(s_f, 1)
            for w in range(2):
                for s in range(NS):
                    nc.tensor.transpose(turned[0:rows, w, STRIPE * s:STRIPE * s + STRIPE], rawf[0:STRIPE, w, s, :],
                                        ident[0:STRIPE, 0:STRIPE]).then_inc(s_t, 1)

        @block.vector
        def _(dve):
            chain = Chain(dve, s_v)
            dve.wait_ge(s_raw, 32)
            dve.tensor_copy(rawf[0:STRIPE, :, :, :], raw[0:STRIPE, :, :, :]).then_inc(s_f, 1)
            dve.wait_ge(s_t, 2 * NS)
            chain.mark(dve.tensor_copy(dst_col[0:rows, :], turned[0:rows, 0, 0:T]))
            chain.mark(dve.tensor_copy(dst_i[0:rows, :], turned[0:rows, 0, 0:T]))
            chain.link(dve.tensor_copy(src_col[0:rows, :], turned[0:rows, 1, 0:T]))
            chain.link(dve.tensor_scalar(hi_i[0:rows, :], dst_i[0:rows, :], 7, None, ALU.logical_shift_right))
            chain.link(dve.tensor_copy(hi_col[0:rows, :], hi_i[0:rows, :]))
            chain.link(dve.scalar_tensor_tensor(out=lo_col[0:rows, :], in0=hi_col[0:rows, :], scalar=-float(P),
                                                in1=dst_col[0:rows, :], op0=ALU.mult, op1=ALU.add))


def count_degrees(nc, const, L):
    name, rows, edges, dst, src, segments = L.name, L.rows, L.edges, L.dst, L.src, L.segments
    CH, HALF, NCH, hi_col, lo_col, degree, unsorted = L.CH, L.HALF, L.NCH, L.hi_col, L.lo_col, L.degree, L.unsorted
    ramp, ones, zero16 = const["ramp"], const["ones"], const["zero16"]
    with ExitStack() as ctx:
        k = Kit(nc, ctx, name + "h")
        oh_lo = k.sb("oh_lo", [P, 2, HALF, P], BF16)
        oh_hi = k.sb("oh_hi", [P, 2, HALF, NT], BF16)
        counts = k.ps("counts", [P, NT])
        wrong_total = k.ps("wrong_total", [P, 1])
        s_oh, s_used, s_done, s_pass, s_list, s_seg, s_ch, s_big, s_wrong, s_tail = (
            k.sem(n) for n in ("oh", "used", "done", "pass", "list", "seg", "ch", "big", "wrong", "tail"))
        if segments is not None:
            per = edges // rows
            here = k.sb("here", [P, per], I32)
            next_ = k.sb("next_", [P, per], I32)
            out_of_order = k.sb("out_of_order", [P, per])
            wrong = k.sb("wrong", [P, 1])
            part = edges // STEP // 100
            wide = k.sb("wide", [P, part * STEP + SPAN], I32)
        block = ctx.enter_context(nc.Block())

        if segments is not None:
            @block.sync
            def _(sp):
                sp.dma_start(here[0:rows, :], dst.rearrange("(p n) -> p n", p=rows)).then_inc(s_list, 16)
                sp.wait_ge(s_big, 1)
                whole = (rows - 1) * per
                sp.dma_start(next_[0:rows - 1, :], dst[1:1 + whole].rearrange("(p n) -> p n", n=per)).then_inc(s_list, 16)
                sp.dma_start(next_[rows - 1:rows, 0:per - 1], dst[1 + whole:edges].rearrange("(o n) -> o n", o=1)
                             ).then_inc(s_list, 16)
                width = part * STEP
                sp.wait_ge(s_big, 2)
                sp.dma_start(wide[0:100, 0:width], src.rearrange("(p n) -> p n", n=width)).then_inc(s_tail, 16)
                sp.dma_start(wide[0:99, width:width + SPAN],
                             src[width:edges].rearrange("(p n) -> p n", n=width)[:, 0:SPAN]).then_inc(s_tail, 16)
                sp.wait_ge(s_tail, 32)
                begin = wide[0:100, 0:1]
                sp.dma_start(segments.rearrange("(p r) n -> p r n", p=100),
                             bass.AP(begin.tensor, begin.offset, [begin.ap[0], [STEP, part], [1, SPAN + STEP]])
                             ).then_inc(s_seg, 16)
                sp.wait_ge(s_list, 48)
                sp.wait_ge(s_seg, 16)

            @block.gpsimd
            def _(pool):
                pool.memset(next_[:, :], 1 << 20).then_inc(s_big, 1)
                pool.memset(wide[:, :], 0).then_inc(s_big, 1)
                pool.memset(wrong[:, :], 0.0).then_inc(s_big, 1)

        @block.vector
        def _(dve):
            with dve.Fori(0, NCH) as c:
                for h in range(2):
                    hold(dve, s_used, 2 * c + h + 1, s_pass)
                    at = bass.ds(c * CH + h * HALF, HALF)
                    dve.tensor_tensor(oh_lo[0:rows, h, :, :],
                                      lo_col[0:rows, at].rearrange("p (t o) -> p t o", o=1).to_broadcast([rows, HALF, P]),
                                      ramp[0:rows, :].rearrange("p (o n) -> p o n", o=1).to_broadcast([rows, HALF, P]),
                                      ALU.is_equal).then_inc(s_oh, 1)
                    dve.tensor_tensor(oh_hi[0:rows, h, :, :],
                                      hi_col[0:rows, at].rearrange("p (t o) -> p t o", o=1).to_broadcast([rows, HALF, NT]),
                                      ramp[0:rows, 0:NT].rearrange("p (o n) -> p o n", o=1).to_broadcast([rows, HALF, NT]),
                                      ALU.is_equal).then_inc(s_oh, 1)
            dve.wait_ge(s_done, 1)
            dve.tensor_copy(degree[:, :], counts[:, :]).then_inc(s_done, 1)
            if segments is not None:
                chain = Chain(dve, s_ch)
                dve.wait_ge(s_list, 48)
                dve.wait_ge(s_big, 3)
                chain.link(dve.tensor_tensor(out_of_order[0:rows, :], here[0:rows, :], next_[0:rows, :], ALU.is_gt))
                chain.link(dve.tensor_reduce(wrong[0:rows, :], out_of_order[0:rows, :], AX_X, ALU.add))
                dve.sem_inc(s_wrong, 1)
                dve.wait_ge(s_wrong, 2)
                dve.tensor_copy(unsorted[:, :], wrong_total[:, :]).then_inc(s_wrong, 1)

        @block.tensor
        def _(pe):
            pe.sem_inc(s_used, 2)
            nc.tensor.matmul(counts[:, :], zero16[:, 0:P], zero16[:, 0:NT], start=True, stop=False,
                             skip_group_check=True)
            with pe.Fori(0, NCH) as c:
                for h in range(2):
                    pe.wait_ge(s_oh, 4 * c + 2 * h + 2)
                    for j in range(HALF):
                        last = nc.tensor.matmul(counts[:, :], oh_lo[0:rows, h, j, :], oh_hi[0:rows, h, j, :],
                                                start=False, stop=False, skip_group_check=True)
                    last.then_inc(s_used, 1)
            nc.tensor.matmul(counts[:, :], zero16[:, 0:P], zero16[:, 0:NT], start=False, stop=True,
                             skip_group_check=True).then_inc(s_done, 1)
            if segments is not None:
                pe.wait_ge(s_wrong, 1)
                nc.tensor.matmul(wrong_total[:, :], ones[:, :], wrong[:, :], start=True, stop=True).then_inc(s_wrong, 1)


def rank_nodes(nc, const, lists):
    ident, ones = const["ident"], const["ones"]
    with ExitStack() as ctx:
        k = Kit(nc, ctx, "rank")
        node = k.sb("node", [P, NT])
        limits = k.sb("limits", [P, NT])
        larger = k.sb("larger", [P, NP])
        signs = k.sb("signs", [P, NP])
        empty = k.sb("empty", [P, 640], I32)
        s_node = k.sem("node")
        DVE_TILES = 12
        for L in lists:
            k = Kit(nc, ctx, L.name + "r")
            META, CB = L.META, L.cap // P
            L.key = k.sb("key", [P, NT])
            L.key_rows = k.sb("key_rows", [NT, P])
            L.key_less = k.sb("key_less", [P, NT])
            L.all_keys = k.sb("all_keys", [P, NP])
            L.rank = k.sb("rank", [P, NT])
            L.rank_i = k.sb("rank_i", [P, NT], I32)
            L.meta = k.sb("meta", [P, NT, META], I32)
            L.ranked_in = k.sb("ranked_in", [P, NT, META], I32)
            L.deg_rows = k.sb("deg_rows", [NT, P, META], I32)
            L.deg_rows_f = k.sb("deg_rows_f", [NT, P])
            L.most = k.sb("most", [NT, 1])
            L.most_i = k.sb("most_i", [NT, 1], I32)
            L.blocks = k.sb("blocks", [NT, 1])
            L.diag = k.sb("diag", [NT, NT])
            L.tile_blocks = k.sb("tile_blocks", [P, NT])
            L.ends = k.sb("ends", [P, NT + 1])
            L.turn_i = k.sb("turn_i", [P, 2], I32)
            L.past = k.sb("past", [P, NT, NT])
            L.tile_i = k.sb("tile_i", [P, NT], I32)
            L.tile_f = k.sb("tile_f", [P, NT])
            L.block_no = k.sb("block_no", [P, CB])
            L.block_past = k.sb("block_past", [P, CB])
            L.block_i = k.sb("block_i", [P, CB], I32)
            L.before_tile = k.sb("before_tile", [P, NT])
            L.too_many = k.sb("too_many", [P, 1])
            L.keys_t = k.ps("keys_t", [P, 512])
            L.blocks_t = k.ps("blocks_t", [P, 512])
            if L.segments is not None:
                L.sums = k.ps("sums", [P, 2, 256])
            (L.s_v, L.s_iota, L.s_key, L.s_kt, L.s_kr, L.s_kd, L.s_ka, L.s_ranked, L.s_rk, L.s_rd, L.s_bt, L.s_bo, L.s_em,
             L.s_tn, L.s_start, L.s_pass) = (
                k.sem(n) for n in ("v", "iota", "key", "kt", "kr", "kd", "ka", "ranked", "rk", "rd", "bt", "bo", "em", "tn",
                                   "start", "pass"))
            L.s_scat = k.pool_dma_sem("scat")
            L.key_dram = nc.dram_tensor(f"{L.name}_keys", [NP], F32, kind="Internal").ap()
        block = ctx.enter_context(nc.Block())

        @block.gpsimd
        def _(pool):
            pool.iota(node[:, :], pattern=[[P, NT]], base=0, channel_multiplier=1,
                      allow_small_or_imprecise_dtypes=True).then_inc(s_node, 1)
            pool.iota(limits[:, :], pattern=[[P, NT]], base=P, channel_multiplier=0,
                      allow_small_or_imprecise_dtypes=True).then_inc(s_node, 1)
            pool.memset(empty[:, :], PAD_ROW).then_inc(s_node, 1)
            for L in lists:
                CB = L.cap // P
                pool.iota(L.block_no[:, :], pattern=[[1, CB]], base=0, channel_multiplier=CB,
                          allow_small_or_imprecise_dtypes=True).then_inc(L.s_iota, 1)
            for L in lists:
                pool.wait_ge(L.s_rk, 1)
                for t in range(NT):
                    pool.indirect_dma_start(L.ranked[:, :], bass.IndirectOffsetOnAxis(ap=L.rank_i[:, t:t + 1], axis=0),
                                            L.meta[:, t, :], None).then_inc(L.s_scat, 16)

        @block.tensor
        def _(pe):
            for L in lists:
                pe.wait_ge(L.s_key, 1)
                nc.tensor.transpose(L.keys_t[0:NT, 0:P], L.key[:, :], ident[:, :]).then_inc(L.s_kt, 1)
                if L.segments is not None:
                    nc.tensor.matmul(L.sums[:, 0, 0:NT], const["after"][:, :], L.degree[:, :], start=True, stop=True)
                    nc.tensor.matmul(L.sums[:, 1, 0:NT], ones[:, :], L.degree[:, :], start=True, stop=True).then_inc(L.s_start, 1)
            for L in lists:
                pe.wait_ge(L.s_bt, 1)
                nc.tensor.matmul(L.blocks_t[:, 0:NT], ones[0:NT, :], L.diag[:, :], start=True, stop=True).then_inc(L.s_bt, 1)

        @block.scalar
        def _(act):
            for L in lists:
                act.wait_ge(L.s_ka, 16)
                for t in range(DVE_TILES, NT):
                    act.activation(signs[:, :], L.all_keys[:, :], ACT.Sign, bias=L.key_less[:, t:t + 1],
                                   accum_out=L.rank[:, t:t + 1]).then_inc(L.s_ranked, 1)
                    act.wait_ge(L.s_ranked, t - DVE_TILES + 1)

        @block.sync
        def _(sp):
            for L in lists:
                sp.wait_ge(L.s_kr, 1)
                sp.dma_start(L.key_dram.rearrange("(t p) -> t p", p=P), L.key_rows[:, :]).then_inc(L.s_kd, 16)
                sp.wait_ge(L.s_kd, 16)
                sp.dma_start(L.all_keys[:, :], L.key_dram.rearrange("(o n) -> o n", o=1).to_broadcast([P, NP])).then_inc(L.s_ka, 16)
            for L in lists:
                sp.wait_ge(L.s_scat, 16 * NT)
                sp.dma_start(L.deg_rows[:, :, :], L.ranked.rearrange("(t p) w -> t p w", p=P)).then_inc(L.s_rd, 16)
                sp.dma_start(L.ranked_in[:, :, :], L.ranked.rearrange("(t p) w -> p t w", p=P)).then_inc(L.s_rd, 16)
            for L in lists:
                sp.wait_ge(L.s_tn, 1)
                sp.wait_ge(s_node, 3)
                n_clear = sp.value_load(L.turn_i[0:1, 1:2], min_val=1, max_val=L.cap // L.TURN0)
                with sp.Fori(0, n_clear) as c:
                    sp.dma_start(L.slot_table[:, bass.ds(c * 640, 640)], empty[:, :]).then_inc(L.s_em, 16)
                    hold(sp, L.s_em, c * 16 + 16, L.s_pass)
            for L in lists:
                sp.wait_ge(L.s_bo, 1)
                sp.dma_start(L.tile_of_block.rearrange("(p n) -> p n", p=P), L.block_i[:, :]).then_inc(L.s_bo, 16)
                sp.wait_ge(L.s_bo, 17)
                sp.wait_ge(L.s_rd, 32)

        @block.vector
        def _(dve):
            for L in lists:
                chain = L.chain = Chain(dve, L.s_v)
                dve.wait_ge(s_node, 3)
                chain.link(dve.tensor_scalar(L.key[:, :], L.degree[:, :], 4095.0, 4096.0, ALU.min, ALU.mult))
                chain.link(dve.tensor_tensor(L.key[:, :], L.key[:, :], node[:, :], ALU.subtract))
                chain.link(dve.tensor_scalar(L.key[:, :], L.key[:, :], 4095.0, None, ALU.add))
                chain.mark(dve.tensor_scalar(L.key_less[:, :], L.key[:, :], -1.0, None, ALU.mult))
                chain.mark(dve.tensor_copy(L.meta[:, :, 0], L.degree[:, :]))
                chain.mark(dve.tensor_copy(L.meta[:, :, 1], node[:, :]))
                chain.wait()
                dve.sem_inc(L.s_key, 1)
            for L in lists:
                chain = L.chain
                dve.wait_ge(L.s_kt, 1)
                dve.tensor_copy(L.key_rows[:, :], L.keys_t[0:NT, 0:P]).then_inc(L.s_kr, 1)
                if L.segments is not None:
                    dve.wait_ge(L.s_start, 1)
                    chain.link(dve.tensor_tensor_scan(L.before_tile[:, :], ones[:, 0:NT], L.sums[:, 1, 0:NT], 0.0, ALU.mult, ALU.add))
                    chain.link(dve.tensor_tensor(L.before_tile[:, :], L.before_tile[:, :], L.sums[:, 1, 0:NT], ALU.subtract))
                    chain.link(dve.tensor_tensor(L.before_tile[:, :], L.before_tile[:, :], L.sums[:, 0, 0:NT], ALU.add))
                    chain.link(dve.tensor_copy(L.meta[:, :, 2], L.before_tile[:, :]))
            for L in lists:
                chain = L.chain
                dve.wait_ge(L.s_ka, 16)
                for t in range(DVE_TILES):
                    chain.mark(dve.tensor_scalar(larger[:, :], L.all_keys[:, :], L.key[:, t:t + 1], 0.0, ALU.is_gt, ALU.add,
                                                 accum_out=L.rank[:, t:t + 1]))
                    chain.wait()
                dve.wait_ge(L.s_ranked, NT - DVE_TILES)
                chain.link(dve.tensor_scalar(L.rank[:, DVE_TILES:NT], L.rank[:, DVE_TILES:NT], NP - 1.0, 0.5, ALU.add, ALU.mult))
                dve.tensor_copy(L.rank_i[:, :], L.rank[:, :]).then_inc(L.s_rk, 1)
                dve.wait_ge(L.s_rk, 1)
            for L in lists:
                chain = L.chain
                dve.wait_ge(L.s_iota, 1)
                chain.link(dve.tensor_scalar(L.tile_i[:, :], L.rank_i[:, :], 7, None, ALU.logical_shift_right))
                chain.link(dve.tensor_copy(L.tile_f[:, :], L.tile_i[:, :]))
                dve.wait_ge(L.s_rd, 32)
                chain.mark(dve.tensor_copy(L.perm[:, :], L.ranked_in[:, :, 1]))
                chain.mark(dve.tensor_copy(L.degree[:, :], L.ranked_in[:, :, 0]))
                if L.segments is not None:
                    chain.mark(dve.tensor_copy(L.start[:, :], L.ranked_in[:, :, 2]))
                    chain.wait()
                    chain.mark(dve.tensor_scalar(L.has_edges[:, :], L.degree[:, :], 0.5, None, ALU.is_gt))
                    chain.link(dve.tensor_scalar(L.over_degree[:, :], L.degree[:, :], 1.0, None, ALU.max))
                    chain.link(dve.reciprocal(L.over_degree[:, :], L.over_degree[:, :]))
                chain.link(dve.tensor_copy(L.deg_rows_f[:, :], L.deg_rows[:, :, 0]))
                chain.link(dve.tensor_reduce(L.most[:, :], L.deg_rows_f[:, :], AX_X, ALU.max))
                chain.link(dve.tensor_scalar(L.most[:, :], L.most[:, :], L.slots - 1.0, None, ALU.add))
                chain.link(dve.tensor_copy(L.most_i[:, :], L.most[:, :]))
                chain.link(dve.tensor_scalar(L.most_i[:, :], L.most_i[:, :], L.slots.bit_length() - 1, None, ALU.logical_shift_right))
                chain.link(dve.tensor_copy(L.blocks[:, :], L.most_i[:, :]))
                chain.mark(dve.tensor_scalar(L.diag[:, :], ident[0:NT, 0:NT], L.blocks[:, 0:1], None, ALU.mult))
                chain.wait()
                dve.sem_inc(L.s_bt, 1)
                dve.wait_ge(L.s_bt, 2)
                chain.link(dve.tensor_copy(L.tile_blocks[:, :], L.blocks_t[:, 0:NT]))
                chain.link(dve.tensor_tensor_scan(L.ends[:, 0:NT], ones[:, 0:NT], L.tile_blocks[:, :], 0.0, ALU.mult, ALU.add))
                if L.segments is not None:
                    chain.link(dve.tensor_scalar(L.too_many[:, :], L.tile_blocks[:, 0:1], float(SPAN // L.slots), None, ALU.is_gt))
                    chain.link(dve.tensor_tensor(L.too_many[:, :], L.too_many[:, :], L.unsorted[:, :], ALU.add))
                    chain.link(dve.tensor_scalar(L.too_many[:, :], L.too_many[:, :], 1.0, None, ALU.min))
                    chain.mark(dve.tensor_copy(L.general[:, :], L.too_many[:, :]))
                    chain.mark(dve.memset(L.ends_i[:, 0:1], 0))
                    chain.mark(dve.tensor_copy(L.ends_i[:, 1:NT + 1], L.ends[:, 0:NT]))
                unit = L.per_turn // 2 if L.halves else L.per_turn
                chain.link(dve.tensor_scalar(L.ends[:, NT:NT + 1], L.ends[:, NT - 1:NT], unit - 1.0, float(L.per_turn), ALU.add, ALU.max))
                chain.link(dve.tensor_copy(L.turn_i[:, 0:1], L.ends[:, NT:NT + 1]))
                chain.mark(dve.tensor_scalar(L.turns[0:1, 0:1], L.turn_i[0:1, 0:1], L.per_turn.bit_length() - 1, None, ALU.logical_shift_right))
                chain.link(dve.tensor_scalar(L.turns[0:1, 1:2], L.turn_i[0:1, 0:1], unit.bit_length() - 1, 1,
                                             ALU.logical_shift_right, ALU.bitwise_and))
                chain.link(dve.tensor_scalar(L.ends[:, NT:NT + 1], L.ends[:, NT - 1:NT], L.TURN0 + L.per_turn - 1.0, 1.0 / L.TURN0, ALU.add, ALU.mult))
                chain.link(dve.tensor_scalar(L.ends[:, NT:NT + 1], L.ends[:, NT:NT + 1], 1.0, float(L.cap // L.TURN0), ALU.max, ALU.min))
                chain.link(dve.tensor_copy(L.turn_i[:, 1:2], L.ends[:, NT:NT + 1]))
                dve.sem_inc(L.s_tn, 1)
                chain.link(dve.tensor_tensor(
                    L.past[:, :, :], L.rank[:, :].rearrange("p (t o) -> p t o", o=1).to_broadcast([P, NT, NT]),
                    limits[:, :].rearrange("p (o j) -> p o j", o=1).to_broadcast([P, NT, NT]), ALU.is_ge))
                chain.link(dve.tensor_tensor(
                    L.past[:, :, :], L.past[:, :, :],
                    L.tile_blocks[:, :].rearrange("p (o j) -> p o j", o=1).to_broadcast([P, NT, NT]), ALU.mult))
                chain.link(dve.tensor_reduce(L.base[:, :], L.past[:, :, :], AX_X, ALU.add))
                chain.link(dve.tensor_scalar(L.base[:, :], L.base[:, :], float(L.slots), None, ALU.mult))
                chain.link(dve.scalar_tensor_tensor(out=L.tile_f[:, :], in0=L.tile_f[:, :], scalar=-float(P), in1=L.rank[:, :],
                                                    op0=ALU.mult, op1=ALU.add))
                chain.link(dve.scalar_tensor_tensor(out=L.base[:, :], in0=L.tile_f[:, :], scalar=float(L.cap * L.slots), in1=L.base[:, :],
                                                    op0=ALU.mult, op1=ALU.add))
                chain.link(dve.tensor_scalar(L.block_past[:, :], L.block_no[:, :], L.ends[:, 0:1], None, ALU.is_ge))
                for t in range(1, NT):
                    chain.link(dve.scalar_tensor_tensor(out=L.block_past[:, :], in0=L.block_no[:, :], scalar=L.ends[:, t:t + 1],
                                                        in1=L.block_past[:, :], op0=ALU.is_ge, op1=ALU.add))
                chain.link(dve.tensor_copy(L.block_i[:, :], L.block_past[:, :]))
                dve.sem_inc(L.s_bo, 1)


def fill_slots(nc, const, L):
    name, rows, edges, dst, src, segments, slots = L.name, L.rows, L.edges, L.dst, L.src, L.segments, L.slots
    CH, HALF, NCH, degree, base, start, slot_table = L.CH, L.HALF, L.NCH, L.degree, L.base, L.start, L.slot_table
    dst_col, src_col, hi_col, lo_col, ends_i, general = L.dst_col, L.src_col, L.hi_col, L.lo_col, L.ends_i, L.general
    before, ramp, row, ident = const["before"], const["ramp"], const["row"], const["ident"]
    with ExitStack() as ctx:
        k = Kit(nc, ctx, name + "s")
        dst_bc = k.sb("dst_bc", [P, 2, HALF * rows], I32)
        dst_lo = k.sb("dst_lo", [P, 2, HALF * rows], I32)
        oh_lo = k.sb("oh_lo", [P, 2, HALF, P], BF16)
        oh_hi = k.sb("oh_hi", [P, 2, HALF, NT], BF16)
        oh_lo_t = k.sb("oh_lo_t", [P, 2, HALF * rows])
        same = k.sb("same", [P, 2, P])
        in_tile = k.sb("in_tile", [P, 2, HALF])
        lookup = k.sb("lookup", [P, 2, NT])
        picked = k.sb("picked", [P, HALF, NT])
        found = k.sb("found", [P, HALF])
        slot_i = k.sb("slot_i", [P, 2, HALF], I32)
        src_i = k.sb("src_i", [P, 2, HALF], I32)
        primed = k.sb("primed", [1, 2], I32)
        counts = k.ps("counts", [P, NT])
        got = k.ps("got", [P, 2, 512])
        (s_bc, s_oh, s_lt, s_cnt, s_snap, s_got, s_slot, s_looked, s_ch, s_pass, s_pass2, s_pass3,
         s_pass4, s_free, s_base, s_blank, s_idx, s_packed) = (
            k.sem(n) for n in ("bc", "oh", "lt", "cnt", "snap", "got", "slot", "looked", "ch", "pass", "pass2",
                               "pass3", "pass4", "free", "base", "blank", "idx", "packed"))
        s_st = (k.pool_dma_sem("st0"), k.pool_dma_sem("st1"))
        if segments is not None:
            W = NT * SPAN + SPAN
            pieces = k.sb("pieces", [P, NT, SPAN + STEP], I32)
            piecef = k.sb("piecef", [P, NT, SPAN + STEP])
            moved = k.sb("moved", [P, NT, SPAN + STEP])
            valid = k.sb("valid", [P, NT, SPAN])
            packed = k.sb("packed", [P, W], I32)
            piece_row = k.sb("piece_row", [P, NT], I32)
            bit_i = k.sb("bit_i", [P, 2, NT], I32)
            bit = k.sb("bit", [P, 2, NT])
            s_piece = k.pool_dma_sem("piece")
        block = ctx.enter_context(nc.Block())

        def ways(eng, short, long):
            if segments is None:
                long()
            else:
                way = eng.value_load(general[0:1, 0:1], min_val=0, max_val=1)
                with eng.If(way == 0):
                    short()
                with eng.Else():
                    long()

        @block.sync
        def _(sp):
            def long():
                with sp.Fori(0, NCH) as c:
                    for h in range(2):
                        hold(sp, s_free, 2 * c + h + 1, s_pass4)
                        sp.dma_start(dst_bc[:, h, :],
                                     dst[bass.ds((c * CH + h * HALF) * rows, HALF * rows)]
                                     .rearrange("(o n) -> o n", o=1).to_broadcast([P, HALF * rows])).then_inc(s_bc, 16)
                        hold(sp, s_bc, (2 * c + h + 1) * 16, s_pass4)

            def short():
                sp.wait_ge(s_packed, 1)
                sp.dma_start(slot_table[:, 0:W], packed[:, :]).then_inc(s_packed, 16)
                sp.wait_ge(s_packed, 17)

            ways(sp, short, long)

        @block.vector
        def _(dve):
            def short():
                chain = Chain(dve, s_ch)
                chain.link(dve.tensor_scalar(piece_row[:, :], start[:, :], 2, None, ALU.logical_shift_right))
                chain.link(dve.tensor_scalar(piece_row[:, :], piece_row[:, :], edges / STEP - 1, None, ALU.min))
                dve.sem_inc(s_idx, 1)
                chain.mark(dve.tensor_scalar(bit_i[:, 0, :], start[:, :], 1, None, ALU.bitwise_and))
                chain.link(dve.tensor_scalar(bit_i[:, 1, :], start[:, :], 1, 1, ALU.logical_shift_right, ALU.bitwise_and))
                chain.mark(dve.tensor_copy(bit[:, :, :], bit_i[:, :, :]))
                chain.link(dve.tensor_tensor(
                    valid[:, :, :], ramp[:, 0:SPAN].rearrange("p (o n) -> p o n", o=1).to_broadcast([P, NT, SPAN]),
                    degree[:, :].rearrange("p (t o) -> p t o", o=1).to_broadcast([P, NT, SPAN]), ALU.is_lt))
                dve.wait_ge(s_piece, 16 * NT)
                chain.link(dve.tensor_copy(piecef[:, :, :], pieces[:, :, :]))
                for b, width in ((1, SPAN + 2), (0, SPAN)):
                    by = b + 1
                    chain.link(dve.tensor_tensor(moved[:, :, 0:width], piecef[:, :, by:by + width], piecef[:, :, 0:width],
                                                 ALU.subtract))
                    chain.link(dve.tensor_tensor(
                        moved[:, :, 0:width], moved[:, :, 0:width],
                        bit[:, b, :].rearrange("p (t o) -> p t o", o=1).to_broadcast([P, NT, width]), ALU.mult))
                    chain.link(dve.tensor_tensor(piecef[:, :, 0:width], piecef[:, :, 0:width], moved[:, :, 0:width], ALU.add))
                chain.link(dve.scalar_tensor_tensor(out=valid[:, :, :], in0=piecef[:, :, 0:SPAN], scalar=-float(PAD_ROW),
                                                    in1=valid[:, :, :], op0=ALU.add, op1=ALU.mult))
                dve.wait_ge(s_blank, 1)
                chain.restart()
                with dve.Fori(0, NT // 5) as fives:
                    for i in range(5):
                        t = fives * 5 + i
                        at = dve.value_load(ends_i[0:1, bass.ds(t, 1)], min_val=0, max_val=NT * SPAN // slots)
                        chain.link(dve.tensor_scalar(packed[:, bass.ds(at * slots, SPAN)],
                                                     valid[:, bass.ds(t, 1), :].rearrange("p o n -> p (o n)"), float(PAD_ROW), None,
                                                     ALU.add))
                    chain.restart()
                dve.sem_inc(s_packed, 1)

            def long():
                chain = Chain(dve, s_ch)
                dve.sem_inc(s_free, 2)
                with dve.Fori(0, NCH) as c:
                    for h in range(2):
                        at = bass.ds(c * CH + h * HALF, HALF)
                        hold(dve, s_got, 2 * c + h + 1, s_pass)
                        dve.tensor_tensor(oh_lo[0:rows, h, :, :],
                                          lo_col[0:rows, at].rearrange("p (t o) -> p t o", o=1).to_broadcast([rows, HALF, P]),
                                          ramp[0:rows, :].rearrange("p (o n) -> p o n", o=1).to_broadcast([rows, HALF, P]),
                                          ALU.is_equal).then_inc(s_oh, 1)
                        dve.tensor_tensor(oh_hi[0:rows, h, :, :],
                                          hi_col[0:rows, at].rearrange("p (t o) -> p t o", o=1).to_broadcast([rows, HALF, NT]),
                                          ramp[0:rows, 0:NT].rearrange("p (o n) -> p o n", o=1).to_broadcast([rows, HALF, NT]),
                                          ALU.is_equal).then_inc(s_oh, 1)
                        hold(dve, s_bc, (2 * c + h + 1) * 16, s_pass)
                        chain.link(dve.tensor_scalar(dst_lo[:, h, :], dst_bc[:, h, :], P - 1, None, ALU.bitwise_and))
                        dve.tensor_scalar(oh_lo_t[:, h, :], dst_lo[:, h, :], row[:, 0:1], None, ALU.is_equal).then_inc(s_lt, 1)
                        for j in range(HALF):
                            col = dst_col[0:rows, bass.ds(c * CH + h * HALF + j, 1)]
                            chain.mark(dve.scalar_tensor_tensor(
                                out=same[0:rows, j % 2, 0:rows], in0=dst_bc[0:rows, h, j * rows:(j + 1) * rows], scalar=col,
                                in1=before[0:rows, 0:rows], op0=ALU.is_equal, op1=ALU.mult,
                                accum_out=in_tile[0:rows, h, j:j + 1]))
                            if j % 2 == 1 or j == HALF - 1:
                                chain.wait()
                        dve.sem_inc(s_free, 1)
                        hold(dve, s_got, 2 * c + h + 3, s_pass)
                        chain.link(dve.tensor_tensor(
                            picked[0:rows, :, :], got[0:rows, h, 0:HALF * NT].rearrange("p (t n) -> p t n", n=NT),
                            oh_hi[0:rows, h, :, :], ALU.mult))
                        chain.link(dve.tensor_reduce(found[0:rows, :], picked[0:rows, :, :], AX_X, ALU.add))
                        hold(dve, s_st[h], 16 * HALF * c + 16, s_pass)
                        chain.mark(dve.tensor_tensor(slot_i[0:rows, h, :], found[0:rows, :], in_tile[0:rows, h, :], ALU.add))
                        chain.link(dve.tensor_copy(src_i[0:rows, h, :], src_col[0:rows, at]))
                        dve.sem_inc(s_slot, 1)
                    chain.restart()

            ways(dve, short, long)

        @block.tensor
        def _(pe):
            def long():
                pe.sem_inc(s_got, 2)
                nc.tensor.matmul(counts[:, :], ident[:, :], base[:, :], start=True, stop=False,
                                 skip_group_check=True).then_inc(s_cnt, 1)
                with pe.Fori(0, NCH) as c:
                    for h in range(2):
                        hold(pe, s_oh, 4 * c + 2 * h + 2, s_pass2)
                        hold(pe, s_lt, 2 * c + h + 1, s_pass2)
                        for j in range(HALF):
                            n = c * CH + h * HALF + j
                            pe.wait_ge(s_snap, n + 1)
                            nc.tensor.matmul(counts[:, :], oh_lo[0:rows, h, j, :], oh_hi[0:rows, h, j, :],
                                             start=False, stop=False, skip_group_check=True).then_inc(s_cnt, 1)
                            last = nc.tensor.matmul(got[0:rows, h, j * NT:(j + 1) * NT],
                                                    oh_lo_t[:, h, j * rows:(j + 1) * rows], lookup[:, j % 2, :],
                                                    start=True, stop=True, skip_group_check=True)
                            if j == HALF - 1:
                                last.then_inc(s_got, 1)
                            else:
                                last.then_inc(s_looked, 1)

            ways(pe, lambda: None, long)

        @block.scalar
        def _(act):
            def long():
                with act.Fori(0, NCH) as c:
                    for h in range(2):
                        for j in range(HALF):
                            n = c * CH + h * HALF + j
                            act.wait_ge(s_cnt, n + 1)
                            act.activation(lookup[:, j % 2, :], counts[:, :], ACT.Copy).then_inc(s_snap, 1)

            ways(act, lambda: None, long)

        @block.gpsimd
        def _(pool):
            def short():
                pool.memset(packed[:, :], PAD_ROW).then_inc(s_blank, 1)
                pool.wait_ge(s_idx, 1)
                for t in range(NT):
                    pool.indirect_dma_start(pieces[:, t, :], None, segments[:, :],
                                            bass.IndirectOffsetOnAxis(ap=piece_row[:, t:t + 1], axis=0)).then_inc(s_piece, 16)

            def long():
                for h in range(2):
                    pool.dma_start(primed[0:1, h:h + 1], dst[0:1].rearrange("(o n) -> o n", o=1)).then_inc(s_st[h], 16)
                with pool.Fori(0, NCH) as c:
                    for h in range(2):
                        hold(pool, s_slot, 2 * c + h + 1, s_pass3)
                        for j in range(HALF):
                            pool.indirect_dma_start(
                                slot_table.rearrange("p (n o) -> (p n) o", o=1),
                                bass.IndirectOffsetOnAxis(ap=slot_i[0:rows, h, j:j + 1], axis=0),
                                src_i[0:rows, h, j:j + 1], None).then_inc(s_st[h], 16)
                for h in range(2):
                    pool.wait_ge(s_st[h], 16 + 16 * HALF * NCH)

            ways(pool, short, long)


def gather_pass(nc, const, name, table, slot_table, tile_of_block, turns, perm, weight, pooled, op, init):
    RING = TURN // 2
    NB = RING // POOL_SLOTS
    most_turns = slot_capacity(50000, POOL_SLOTS) * POOL_SLOTS // TURN - 1
    with ExitStack() as ctx:
        k = Kit(nc, ctx, name)
        acc = k.sb("acc", [P, NT + 1, C])
        rows = k.sb("rows", [P, RING, C])
        slots = k.sb("slots", [P, 2, RING], I32)
        tiles = k.sb("tiles", [1, 2, NB], I32)
        s_row = [k.pool_dma_sem(f"row{r}") for r in range(RING)]
        s_slots, s_used, s_acc, s_init, s_fin, s_pass = (
            k.sem(n) for n in ("slots", "used", "acc", "init", "fin", "pass"))
        s_out = k.pool_dma_sem("out")
        block = ctx.enter_context(nc.Block())

        @block.sync
        def _(sp):
            n = sp.value_load(turns[0:1, 0:1], min_val=1, max_val=most_turns)
            odd = sp.value_load(turns[0:1, 1:2], min_val=0, max_val=1)

            def half(q, h):
                hold(sp, s_used, 2 * NB * q + NB * h + NB, s_pass)
                b = 2 * NB * q + NB * h
                sp.dma_start(slots[:, h, :], slot_table[:, bass.ds(q * TURN + h * RING, RING)]).then_inc(s_slots, 16)
                sp.dma_start(tiles[0:1, h, :], tile_of_block[bass.ds(b, NB)].rearrange("(o n) -> o n", o=1)
                             ).then_inc(s_slots, 16)
                hold(sp, s_slots, 64 * q + 32 * h + 32, s_pass)

            with sp.Fori(0, n) as q:
                half(q, 0)
                half(q, 1)
            with sp.If(odd == 1):
                half(n, 0)

        @block.gpsimd
        def _(pool):
            n = pool.value_load(turns[0:1, 0:1], min_val=1, max_val=most_turns)
            odd = pool.value_load(turns[0:1, 1:2], min_val=0, max_val=1)

            def half(q, h):
                hold(pool, s_slots, 64 * q + 32 * h + 32, s_pass)
                for u in range(NB):
                    hold(pool, s_used, 2 * NB * q + NB * h + u + NB + 1, s_pass)
                    for s in range(POOL_SLOTS):
                        r = u * POOL_SLOTS + s
                        pool.indirect_dma_start(rows[:, r, :], None, table[:, :],
                                                bass.IndirectOffsetOnAxis(ap=slots[:, h, r:r + 1], axis=0)
                                                ).then_inc(s_row[r], 16)

            with pool.Fori(0, n) as q:
                half(q, 0)
                half(q, 1)
            with pool.If(odd == 1):
                half(n, 0)
            for t in range(NT):
                pool.wait_ge(s_fin, t + 1)
                pool.indirect_dma_start(pooled[:, :], bass.IndirectOffsetOnAxis(ap=perm[:, t:t + 1], axis=0),
                                        acc[:, t, :], None).then_inc(s_out, 16)
            pool.wait_ge(s_out, 16 * NT)

        @block.vector
        def _(dve):
            chain = Chain(dve, s_acc)
            dve.memset(acc[:, :, :], init).then_inc(s_init, 1)
            dve.wait_ge(s_init, 1)
            dve.sem_inc(s_used, 2 * NB)
            n = dve.value_load(turns[0:1, 0:1], min_val=1, max_val=most_turns)
            odd = dve.value_load(turns[0:1, 1:2], min_val=0, max_val=1)

            def half(q, h):
                hold(dve, s_slots, 64 * q + 32 * h + 32, s_pass)
                for u in range(NB):
                    t = dve.value_load(tiles[0:1, h, u:u + 1], min_val=0, max_val=NT)
                    into = acc[:, bass.ds(t, 1), :].rearrange("p o c -> p (o c)")
                    for s in range(POOL_SLOTS):
                        r = u * POOL_SLOTS + s
                        dve.wait_ge(s_row[r], 32 * q + 16 * h + 16)
                        chain.link(dve.tensor_tensor(into, into, rows[:, r, :], op))
                    dve.sem_inc(s_used, 1)

            with dve.Fori(0, n) as q:
                half(q, 0)
                half(q, 1)
                chain.restart()
            with dve.If(odd == 1):
                half(n, 0)
                chain.restart()
            for t in range(NT):
                if weight is None:
                    dve.sem_inc(s_fin, 1)
                else:
                    dve.tensor_scalar(acc[:, t, :], acc[:, t, :], weight[:, t:t + 1], None, ALU.mult).then_inc(s_fin, 1)


def row_norms(dve, act_go, act_done, count, chain, n, source, stats, mean_var, inverse, passed):
    for u in range(n):
        chain.mark(dve.bn_stats(stats[:, u, :], source(u)))
    chain.wait()
    for u in range(n):
        chain.mark(dve.bn_aggr(mean_var[:, u, :], stats[:, u, :]))
    chain.wait()
    dve.sem_inc(act_go, GROUP)
    hold(dve, act_done, count, passed)
    chain.link(dve.reciprocal(inverse[:, 0:n], inverse[:, 0:n]))


def normalise(dve, act_go, act_done, count, chain, n, source, into, stats, mean_var, inverse, passed):
    row_norms(dve, act_go, act_done, count, chain, n, source, stats, mean_var, inverse, passed)
    for u in range(n):
        chain.mark(dve.tensor_scalar(into(u), source(u), mean_var[:, u, 0:1], inverse[:, u:u + 1], ALU.subtract, ALU.mult))
    chain.wait()


def hand_norm(dve, act_go, act_done, count, chain, n, source, stats, mean_var, inverse, shift, apply_go, passed):
    row_norms(dve, act_go, act_done, count, chain, n, source, stats, mean_var, inverse, passed)
    chain.link(dve.scalar_tensor_tensor(out=shift[:, 0:n], in0=mean_var[:, 0:n, 0], scalar=-1.0, in1=inverse[:, 0:n],
                                        op0=ALU.mult, op1=ALU.mult))
    dve.sem_inc(apply_go, GROUP)


def apply_norm(act, apply_go, t, n, source, into, inverse, shift, done, passed):
    hold(act, apply_go, t + GROUP, passed)
    for u in range(n):
        act.activation(tile_of(into, t + u), tile_of(source, t + u), ACT.Identity, bias=shift[:, u:u + 1],
                       scale=inverse[:, u:u + 1]).then_inc(done, 1)
    hold(act, done, t + n, passed)


def every_turn(eng, first, then):
    if first:
        first(0, GROUP)
    with eng.Fori(0, GROUPS - 1) as i:
        if first:
            first(GROUP * i + GROUP, GROUP)
        then(GROUP * i, GROUP)
    if first:
        first(GROUP * GROUPS, REST)
    then(GROUP * (GROUPS - 1), GROUP)
    then(GROUP * GROUPS, REST)


def tiles_of(a, t, n=1):
    return a[:, bass.ds(t, n), :]


def tile_of(a, t):
    return tiles_of(a, t).rearrange("p o c -> p (o c)")


def same_for(a, n):
    return a[:, :].rearrange("p (o c) -> p o c", o=1).to_broadcast([P, n, a.shape[1]])


def by_tile(dram, t, n):
    return dram[bass.ds(t * P, n * P), :].rearrange("(t p) c -> p t c", p=P)


def node_layer(nc, const, name, kind, own, pooled, w, bias, gamma, beta, x, out, table=None, x_loaded=None,
               embedded=None):
    embed = kind == "embed"
    KC = 2 if embed else 4
    normed = kind in ("mixnorm", "enter", "sage")
    renormed = kind in ("enter", "sage")
    per_turn = {"embed": 1, "mix": 0, "mixnorm": 1, "enter": 2, "sage": 2}[kind]
    if embed:
        own = out
    ident, eps = const["ident"], const["eps"]
    with ExitStack() as ctx:
        k = Kit(nc, ctx, name)
        w_sb = k.sb("w", [P, KC, C])
        bias_sb = k.sb("bias", [P, C])
        gamma_sb = k.sb("gamma", [P, C])
        beta_sb = k.sb("beta", [P, C])
        zero_row = k.sb("zero_row", [1, C])
        staged = k.sb("staged", [P, GROUP, KC * P])
        turned = k.sb("turned", [P, GROUP, KC * P])
        y = k.sb("y", [P, GROUP, C])
        stats = k.sb("stats", [P, GROUP, 6])
        mean_var = k.sb("mean_var", [P, GROUP, 2])
        inverse = k.sb("inverse", [P, GROUP])
        shift = k.sb("shift", [P, GROUP])
        flipped = k.ps("flipped", [P, GROUP, 512])
        product = k.ps("product", [P, GROUP, C])
        (s_w, s_zero, s_load, s_stage, s_flip, s_turn, s_mm, s_evac, s_sqrt_go, s_sqrt, s_normed, s_out, s_store,
         s_ch, s_pd, s_pp, s_pa, s_pv, s_ps, s_pad, s_apply) = (
            k.sem(n) for n in ("w", "zero", "load", "stage", "flip", "turn", "mm", "evac", "sqrt_go", "sqrt",
                               "normed", "out", "store", "ch", "pd", "pp", "pa", "pv", "ps", "pad", "apply"))
        params = 2 + 2 * normed
        block = ctx.enter_context(nc.Block())

        @block.sync
        def _(sp):
            def parameters():
                sp.dma_start(w_sb[:, :, :], w.rearrange("(k p) n -> p k n", p=P)).then_inc(s_w, 16)
                for to, v in ((bias_sb, bias), (gamma_sb, gamma), (beta_sb, beta))[0:params - 1]:
                    sp.dma_start(to[:, :], v.rearrange("(o n) -> o n", o=1).to_broadcast([P, C])).then_inc(s_w, 16)

            parameters()
            def load(t, n):
                hold(sp, s_flip, t + GROUP, s_ps)
                sp.dma_start(staged[:, 0:n, 2 * P:4 * P], by_tile(pooled, t, n)).then_inc(s_load, 16)

            def store(t, n):
                hold(sp, s_out, t + n, s_ps)
                sp.dma_start(by_tile(table, t, n), tiles_of(embedded if embed else out, t, n)).then_inc(s_store, 16)

            if embed:
                every_turn(sp, None, store)
            elif table is None:
                every_turn(sp, None, load)
            else:
                load(0, GROUP)
                load(GROUP, GROUP)
                with sp.Fori(0, GROUPS - 2) as i:
                    load(GROUP * i + 2 * GROUP, GROUP)
                    store(GROUP * i, GROUP)
                load(GROUP * GROUPS, REST)
                store(GROUP * (GROUPS - 2), GROUP)
                store(GROUP * (GROUPS - 1), GROUP)
                store(GROUP * GROUPS, REST)
            if table is not None:
                sp.wait_ge(s_zero, 1)
                sp.dma_start(table[PAD_ROW:PAD_ROW + 1, :], zero_row[:, :]).then_inc(s_pad, 16)
                sp.wait_ge(s_store, 16 * (GROUPS + 1))
                sp.wait_ge(s_pad, 16)

        @block.gpsimd
        def _(pool):
            def stage(t, n):
                for u in range(n):
                    if embed:
                        hold(pool, s_normed, t + u + 1, s_pp)
                    hold(pool, s_flip, t + u + 1, s_pp)
                    pool.tensor_copy(staged[:, u, 0:2 * P], tile_of(own, t + u)).then_inc(s_stage, 1)

            pool.memset(zero_row[:, :], LOWEST if kind == "mixnorm" else 0.0).then_inc(s_zero, 1)
            every_turn(pool, None, stage)

        @block.tensor
        def _(pe):
            def turn_over(t, n):
                if not embed:
                    hold(pe, s_load, 4 * t + 16, s_pd)
                for u in range(n):
                    hold(pe, s_stage, t + u + 1, s_pd)
                    hold(pe, s_turn, t + u + 1, s_pd)
                    for c in range(KC):
                        last = nc.tensor.transpose(flipped[:, u, c * P:(c + 1) * P], staged[:, u, c * P:(c + 1) * P], ident[:, :])
                    last.then_inc(s_flip, 1)

            def multiply(t, n):
                hold(pe, s_evac, t + GROUP, s_pd)
                for u in range(n):
                    hold(pe, s_turn, t + u + 1 + GROUP, s_pd)
                    for c in range(KC):
                        last = nc.tensor.matmul(product[:, u, :], turned[:, u, c * P:(c + 1) * P], w_sb[:, c, :],
                                                start=(c == 0), stop=(c == KC - 1))
                    last.then_inc(s_mm, 1)

            pe.sem_inc(s_flip, GROUP)
            pe.sem_inc(s_mm, GROUP)
            pe.wait_ge(s_w, 16 * params)

            def both(t, n):
                turn_over(t, n)
                multiply(t, n)

            every_turn(pe, None, both)

        @block.scalar
        def _(act):
            def roots(t, n, r):
                hold(act, s_sqrt_go, per_turn * t + GROUP * (r + 1), s_pa)
                act.activation(inverse[:, 0:n], mean_var[:, 0:n, 1], ACT.Sqrt, bias=eps[:, 0:1]).then_inc(s_sqrt, GROUP)

            def copy_turned(t, n):
                for u in range(n):
                    hold(act, s_flip, t + u + 1 + GROUP, s_pa)
                    hold(act, s_mm, t + u + 1, s_pa)
                    act.activation(turned[:, u, :], flipped[:, u, 0:KC * P], ACT.Copy).then_inc(s_turn, 1)

            def all_roots(t, n):
                for r in range(per_turn):
                    roots(t, n, r)
                if renormed:
                    apply_norm(act, s_apply, t, n, x, out, inverse, shift, s_out, s_pa)

            act.sem_inc(s_turn, GROUP)
            if embed:
                every_turn(act, all_roots, copy_turned)
            else:
                every_turn(act, copy_turned, all_roots)

        @block.vector
        def _(dve):
            chain = Chain(dve, s_ch)
            dve.sem_inc(s_evac, GROUP)
            dve.wait_ge(s_w, 16 * params)
            if embed:
                dve.wait_ge(x_loaded, 32)

            def norm(t, n, r, source, into):
                normalise(dve, s_sqrt_go, s_sqrt, per_turn * t + GROUP * (r + 1), chain, n, source, into,
                          stats, mean_var, inverse, s_pv)

            def norm_input(t, n):
                norm(t, n, 0, lambda u: tile_of(x, t + u), lambda u: tile_of(out, t + u))
                dve.sem_inc(s_normed, n)
                chain.restart()

            def finish(t, n):
                ys, y_tile = y[:, 0:n, :], lambda u: y[:, u, :]
                hold(dve, s_mm, t + n + GROUP, s_pv)
                dve.tensor_tensor(ys, product[:, 0:n, :], same_for(bias_sb, n), ALU.add).then_inc(s_evac, n)
                hold(dve, s_evac, t + n + GROUP, s_pv)
                if not normed:
                    chain.link(dve.tensor_scalar(tiles_of(embedded if embed else out, t, n), ys, 0.0, None, ALU.max))
                else:
                    if kind != "sage":
                        chain.link(dve.scalar_tensor_tensor(out=ys, in0=ys, scalar=0.0, in1=tiles_of(own, t, n),
                                                            op0=ALU.max, op1=ALU.add))
                    norm(t, n, 0, y_tile, y_tile)
                    chain.link(dve.tensor_tensor(ys, ys, same_for(gamma_sb, n), ALU.mult))
                    chain.link(dve.tensor_tensor(ys if renormed else tiles_of(out, t, n), ys, same_for(beta_sb, n), ALU.add))
                if renormed:
                    if kind == "sage":
                        chain.link(dve.scalar_tensor_tensor(out=ys, in0=ys, scalar=0.0, in1=tiles_of(own, t, n),
                                                            op0=ALU.max, op1=ALU.add))
                    chain.link(dve.tensor_tensor(tiles_of(x, t, n), ys, tiles_of(x, t, n), ALU.add))
                    hand_norm(dve, s_sqrt_go, s_sqrt, per_turn * t + GROUP * 2, chain, n, lambda u: tile_of(x, t + u),
                              stats, mean_var, inverse, shift, s_apply, s_pv)
                else:
                    dve.sem_inc(s_out, n)
                chain.restart()

            every_turn(dve, norm_input if embed else None, finish)




def project(nc, const, name, own, w, width, out, bias=None):
    with ExitStack() as ctx:
        k = Kit(nc, ctx, name)
        w_sb = k.sb("w", [P, 2, width])
        bias_sb = k.sb("bias", [P, width])
        staged = k.sb("staged", [P, GROUP, C])
        turned = k.sb("turned", [P, GROUP, C])
        flipped = k.ps("flipped", [P, GROUP, 512])
        product = k.ps("product", [P, GROUP, width])
        s_w, s_b, s_stage, s_flip, s_turn, s_mm, s_evac, s_pp, s_pt, s_pa, s_pv = (
            k.sem(n) for n in ("w", "b", "stage", "flip", "turn", "mm", "evac", "pp", "pt", "pa", "pv"))
        block = ctx.enter_context(nc.Block())

        @block.sync
        def _(sp):
            sp.dma_start(w_sb[:, :, :], w.rearrange("(k p) n -> p k n", p=P)).then_inc(s_w, 16)
            if bias is not None:
                sp.dma_start(bias_sb[:, :], bias.rearrange("(o n) -> o n", o=1).to_broadcast([P, width])).then_inc(s_b, 16)

        @block.gpsimd
        def _(pool):
            def stage(t, n):
                for u in range(n):
                    hold(pool, s_flip, t + u + 1, s_pp)
                    pool.tensor_copy(staged[:, u, :], tile_of(own, t + u)).then_inc(s_stage, 1)

            every_turn(pool, None, stage)

        @block.tensor
        def _(pe):
            def turn_over(t, n):
                for u in range(n):
                    hold(pe, s_stage, t + u + 1, s_pt)
                    hold(pe, s_turn, t + u + 1, s_pt)
                    for c in range(2):
                        last = nc.tensor.transpose(flipped[:, u, c * P:(c + 1) * P], staged[:, u, c * P:(c + 1) * P], ident_of(const))
                    last.then_inc(s_flip, 1)

            def multiply(t, n):
                hold(pe, s_evac, t + GROUP, s_pt)
                for u in range(n):
                    hold(pe, s_turn, t + u + 1 + GROUP, s_pt)
                    for c in range(2):
                        last = nc.tensor.matmul(product[:, u, :], turned[:, u, c * P:(c + 1) * P], w_sb[:, c, :],
                                                start=(c == 0), stop=(c == 1))
                    last.then_inc(s_mm, 1)

            pe.sem_inc(s_flip, GROUP)
            pe.sem_inc(s_mm, GROUP)
            pe.wait_ge(s_w, 16)

            def both(t, n):
                turn_over(t, n)
                multiply(t, n)

            every_turn(pe, None, both)

        @block.scalar
        def _(act):
            def copy_turned(t, n):
                for u in range(n):
                    hold(act, s_flip, t + u + 1 + GROUP, s_pa)
                    hold(act, s_mm, t + u + 1, s_pa)
                    act.activation(turned[:, u, :], flipped[:, u, 0:C], ACT.Copy).then_inc(s_turn, 1)

            act.sem_inc(s_turn, GROUP)
            every_turn(act, None, copy_turned)

        @block.vector
        def _(dve):
            def take(t, n):
                hold(dve, s_mm, t + n + GROUP, s_pv)
                if bias is None:
                    dve.tensor_copy(out[:, bass.ds(t, n), :], product[:, 0:n, :]).then_inc(s_evac, n)
                else:
                    dve.tensor_tensor(out[:, bass.ds(t, n), :], product[:, 0:n, :], same_for(bias_sb, n), ALU.add).then_inc(s_evac, n)

            if bias is not None:
                dve.wait_ge(s_b, 16)
            dve.sem_inc(s_evac, GROUP)
            every_turn(dve, None, take)


def ident_of(const):
    return const["ident"][:, :]


HEADS, EXPERTS0 = 4, 4
HE = HEADS * EXPERTS0
GROW = HE + 2 * HEADS


def attention(nc, const, name, h, att_src, att_dst, b_gat, ln_gamma, ln_beta, slot_table, tile_of_block, turns, perm,
              gat_table, agg, scores):
    QUARTERS = TURN // SLOTS
    most_turns = slot_capacity(32768, SLOTS) * SLOTS // TURN

    def over(ap, n):
        return ap.rearrange("p (o n) -> p o n", o=1).to_broadcast([P, NT, n])

    with ExitStack() as ctx:
        k = Kit(nc, ctx, name)
        att = k.sb("att", [P, 5, HE])
        table_rows = k.sb("table_rows", [P, NT, GROW])
        weighted = k.sb("weighted", [P, NT, HE])
        blank = k.sb("blank", [1, GROW])
        own = k.sb("own", [P, NT + 1, GROW])
        peak = k.sb("peak", [P, NT + 1, HEADS])
        total = k.sb("total", [P, NT + 1, HEADS])
        mixed = k.sb("mixed", [P, NT + 1, HE])
        inv = k.sb("inv", [P, NT + 1, HEADS])
        rows = k.sb("rows", [P, TURN, GROW])
        slots = k.sb("slots", [P, QUARTERS, SLOTS], I32)
        tiles = k.sb("tiles", [1, QUARTERS], I32)
        e = k.sb("e", [P, SLOTS, HEADS])
        e2 = k.sb("e2", [P, SLOTS, HEADS])
        top = k.sb("top", [P, HEADS])
        grown = k.sb("grown", [P, HEADS])
        below = k.sb("below", [P, SLOTS + 1, HEADS])
        p = k.sb("p", [P, SLOTS + 1, HEADS])
        psum_ = k.sb("psum_", [P, HEADS])
        ph = k.sb("ph", [P, SLOTS, HE])
        phsum = k.sb("phsum", [P, HE])
        natural = k.sb("natural", [P, NT, HE])
        mean = k.sb("mean", [P, NT])
        var = k.sb("var", [P, NT])
        s_row = [k.pool_dma_sem(f"row{r}") for r in range(TURN)]
        s_slots = [k.sem(f"slots{h}") for h in range(QUARTERS)]
        (s_att, s_rows, s_tab, s_used, s_ch, s_exp_go, s_exp, s_fin, s_nat, s_sq, s_set, s_pass,
         s_pa, s_pp, s_pv) = (
            k.sem(n) for n in ("att", "rows", "tab", "used", "ch", "exp_go", "exp", "fin", "nat",
                               "sq", "set", "pass", "pa", "pp", "pv"))
        s_own, s_out = k.pool_dma_sem("own"), k.pool_dma_sem("out")
        block = ctx.enter_context(nc.Block())

        @block.sync
        def _(sp):
            vectors = (att_src.rearrange("h e -> (h e)"), att_dst.rearrange("h e -> (h e)"), b_gat, ln_gamma, ln_beta)
            for j, v in enumerate(vectors):
                sp.dma_start(att[:, j, :], v.rearrange("(o n) -> o n", o=1).to_broadcast([P, HE])).then_inc(s_att, 16)
            sp.wait_ge(s_rows, 1)
            sp.dma_start(gat_table[0:NP, :].rearrange("(t p) c -> p t c", p=P), table_rows[:, :, :]).then_inc(s_tab, 16)
            sp.wait_ge(s_set, 2)
            sp.dma_start(gat_table[PAD_ROW:PAD_ROW + 1, :], blank[:, :]).then_inc(s_tab, 16)
            sp.wait_ge(s_tab, 32)
            n = sp.value_load(turns[0:1, 0:1], min_val=1, max_val=most_turns)
            with sp.Fori(0, n) as q:
                for quarter in range(QUARTERS):
                    b = QUARTERS * q + quarter
                    hold(sp, s_used, b + 1, s_pass)
                    sp.dma_start(slots[:, quarter, :], slot_table[:, bass.ds(b * SLOTS, SLOTS)]).then_inc(s_slots[quarter], 16)
                    sp.dma_start(tiles[0:1, quarter:quarter + 1], tile_of_block[bass.ds(b, 1)].rearrange("(o n) -> o n", o=1)
                                 ).then_inc(s_slots[quarter], 16)
            sp.wait_ge(s_out, 16 * NT)
            sp.dma_start(natural[:, :, :], agg.rearrange("(t p) c -> p t c", p=P)).then_inc(s_nat, 16)

        @block.gpsimd
        def _(pool):
            pool.memset(blank[:, :], 0.0).then_inc(s_set, 1)
            pool.wait_ge(s_set, 1)
            pool.memset(blank[:, HE:HE + HEADS], -1e30).then_inc(s_set, 1)
            pool.memset(own[:, NT, :], 0.0).then_inc(s_set, 1)
            pool.wait_ge(s_tab, 32)
            for t in range(NT):
                pool.indirect_dma_start(own[:, t, :], None, gat_table[:, :],
                                        bass.IndirectOffsetOnAxis(ap=perm[:, t:t + 1], axis=0)).then_inc(s_own, 16)
            n = pool.value_load(turns[0:1, 0:1], min_val=1, max_val=most_turns)
            with pool.Fori(0, n) as q:
                for quarter in range(QUARTERS):
                    hold(pool, s_slots[quarter], 32 * q + 32, s_pp)
                    hold(pool, s_used, QUARTERS * q + quarter + 1, s_pp)
                    for s in range(SLOTS):
                        r = quarter * SLOTS + s
                        pool.indirect_dma_start(rows[:, r, :], None, gat_table[:, :],
                                                bass.IndirectOffsetOnAxis(ap=slots[:, quarter, s:s + 1], axis=0)
                                                ).then_inc(s_row[r], 16)
            pool.wait_ge(s_fin, 1)
            for t in range(NT):
                pool.indirect_dma_start(agg[:, :], bass.IndirectOffsetOnAxis(ap=perm[:, t:t + 1], axis=0),
                                        mixed[:, t, :], None).then_inc(s_out, 16)

        @block.scalar
        def _(act):
            n = act.value_load(turns[0:1, 0:1], min_val=1, max_val=most_turns)
            with act.Fori(0, n) as q:
                for b in range(QUARTERS):
                    hold(act, s_exp_go, QUARTERS * q + b + 1, s_pa)
                    act.activation(p[:, :, :], below[:, :, :], ACT.Exp).then_inc(s_exp, 1)
            act.wait_ge(s_sq, 1)
            act.activation(var[:, :], mean[:, :], ACT.Sqrt, bias=const["eps"][:, 0:1]).then_inc(s_sq, 1)

        @block.vector
        def _(dve):
            chain = Chain(dve, s_ch)
            link = chain.link
            dve.wait_ge(s_att, 80)
            chain.mark(dve.tensor_copy(table_rows[:, :, 0:HE], h[:, :, :]))
            for j in range(2):
                link(dve.tensor_tensor(weighted[:, :, :], h[:, :, :], over(att[:, j, :], HE), ALU.mult))
                link(dve.tensor_reduce(table_rows[:, :, HE + j * HEADS:HE + (j + 1) * HEADS],
                                       weighted[:, :, :].rearrange("p t (h e) -> p t h e", h=HEADS), AX_X, ALU.add))
            dve.sem_inc(s_rows, 1)
            dve.wait_ge(s_own, 16 * NT)
            dve.wait_ge(s_set, 3)
            link(dve.tensor_tensor(inv[:, :, :], own[:, :, HE:HE + HEADS], own[:, :, HE + HEADS:GROW], ALU.add))
            link(dve.scalar_tensor_tensor(out=peak[:, :, :], in0=inv[:, :, :], scalar=0.2, in1=inv[:, :, :],
                                          op0=ALU.mult, op1=ALU.max))
            chain.mark(dve.memset(total[:, :, :], 1.0))
            link(dve.tensor_copy(mixed[:, :, :], own[:, :, 0:HE]))
            chain.restart()
            dve.sem_inc(s_used, QUARTERS)
            n = dve.value_load(turns[0:1, 0:1], min_val=1, max_val=most_turns)
            with dve.Fori(0, n) as q:
                for quarter in range(QUARTERS):
                    hold(dve, s_slots[quarter], 32 * q + 32, s_pv)
                    t = dve.value_load(tiles[0:1, quarter:quarter + 1], min_val=0, max_val=NT)

                    def flat(a):
                        return a[:, bass.ds(t, 1), :].rearrange("p o c -> p (o c)")

                    a_dst = own[:, bass.ds(t, 1), HE + HEADS:GROW].to_broadcast([P, SLOTS, HEADS])
                    r0 = quarter * SLOTS
                    for s in range(SLOTS):
                        hold(dve, s_row[r0 + s], 16 * q + 16, s_pv)
                    link(dve.tensor_tensor(e[:, :, :], rows[:, r0:r0 + SLOTS, HE:HE + HEADS], a_dst, ALU.add))
                    link(dve.scalar_tensor_tensor(out=e2[:, :, :], in0=e[:, :, :], scalar=0.2, in1=e[:, :, :],
                                                  op0=ALU.mult, op1=ALU.max))
                    link(dve.tensor_reduce(top[:, :], e2[:, :, :].rearrange("p s h -> p h s"), AX_X, ALU.max))
                    link(dve.tensor_tensor(grown[:, :], top[:, :], flat(peak), ALU.max))
                    chain.mark(dve.tensor_tensor(
                        below[:, 0:SLOTS, :], e2[:, :, :],
                        grown[:, :].rearrange("p (o h) -> p o h", o=1).to_broadcast([P, SLOTS, HEADS]), ALU.subtract))
                    link(dve.tensor_tensor(below[:, SLOTS, :], flat(peak), grown[:, :], ALU.subtract))
                    dve.sem_inc(s_exp_go, 1)
                    chain.mark(dve.tensor_copy(flat(peak), grown[:, :]))
                    hold(dve, s_exp, QUARTERS * q + quarter + 1, s_pv)
                    chain.mark(dve.tensor_tensor(
                        ph[:, :, :].rearrange("p s (h e) -> p s h e", h=HEADS),
                        rows[:, r0:r0 + SLOTS, 0:HE].rearrange("p s (h e) -> p s h e", h=HEADS),
                        p[:, 0:SLOTS, :].rearrange("p s (h o) -> p s h o", o=1).to_broadcast([P, SLOTS, HEADS, EXPERTS0]),
                        ALU.mult))
                    chain.mark(dve.tensor_reduce(psum_[:, :], p[:, 0:SLOTS, :].rearrange("p s h -> p h s"), AX_X, ALU.add))
                    chain.mark(dve.tensor_tensor(flat(total), flat(total), p[:, SLOTS, :], ALU.mult))
                    chain.mark(dve.tensor_tensor(
                        flat(mixed).rearrange("p (h e) -> p h e", h=HEADS), flat(mixed).rearrange("p (h e) -> p h e", h=HEADS),
                        p[:, SLOTS, :].rearrange("p (h o) -> p h o", o=1).to_broadcast([P, HEADS, EXPERTS0]), ALU.mult))
                    chain.wait()
                    chain.mark(dve.tensor_tensor(flat(total), flat(total), psum_[:, :], ALU.add))
                    link(dve.tensor_reduce(phsum[:, :], ph[:, :, :].rearrange("p s c -> p c s"), AX_X, ALU.add))
                    link(dve.tensor_tensor(flat(mixed), flat(mixed), phsum[:, :], ALU.add))
                    dve.sem_inc(s_used, 1)
                chain.restart()
            link(dve.tensor_scalar(total[:, :, :], total[:, :, :], 1e-16, None, ALU.add))
            link(dve.reciprocal(inv[:, :, :], total[:, :, :]))
            link(dve.tensor_tensor(mixed[:, :, :].rearrange("p t (h e) -> p (t h) e", h=HEADS),
                                   mixed[:, :, :].rearrange("p t (h e) -> p (t h) e", h=HEADS),
                                   inv[:, :, :].rearrange("p t (h o) -> p (t h) o", o=1).to_broadcast([P, (NT + 1) * HEADS, EXPERTS0]),
                                   ALU.mult))
            dve.sem_inc(s_fin, 1)
            dve.wait_ge(s_nat, 16)
            link(dve.tensor_tensor(natural[:, :, :], natural[:, :, :], over(att[:, 2, :], HE), ALU.add))
            link(dve.tensor_reduce(mean[:, :], natural[:, :, :], AX_X, ALU.add))
            link(dve.tensor_scalar(mean[:, :], mean[:, :], 1.0 / HE, None, ALU.mult))
            link(dve.tensor_tensor(natural[:, :, :], natural[:, :, :],
                                   mean[:, :].rearrange("p (t o) -> p t o", o=1).to_broadcast([P, NT, HE]), ALU.subtract))
            link(dve.tensor_tensor(weighted[:, :, :], natural[:, :, :], natural[:, :, :], ALU.mult))
            link(dve.tensor_reduce(mean[:, :], weighted[:, :, :], AX_X, ALU.add))
            link(dve.tensor_scalar(mean[:, :], mean[:, :], 1.0 / HE, None, ALU.mult))
            dve.sem_inc(s_sq, 1)
            dve.wait_ge(s_sq, 2)
            link(dve.reciprocal(mean[:, :], var[:, :]))
            link(dve.tensor_tensor(natural[:, :, :], natural[:, :, :],
                                   mean[:, :].rearrange("p (t o) -> p t o", o=1).to_broadcast([P, NT, HE]), ALU.mult))
            link(dve.tensor_tensor(natural[:, :, :], natural[:, :, :], over(att[:, 3, :], HE), ALU.mult))
            link(dve.tensor_tensor(natural[:, :, :], natural[:, :, :], over(att[:, 4, :], HE), ALU.add))
            link(dve.tensor_reduce(scores[:, :, :], natural[:, :, :].rearrange("p t (h e) -> p t e h", h=HEADS), AX_X, ALU.add))
            link(dve.tensor_scalar(scores[:, :, :], scores[:, :, :], 1.0 / HEADS, None, ALU.mult))


UNIT = 2 * P


def units_most(experts):
    return (2 * N + UNIT * experts) // UNIT


def spill_row(experts):
    return (units_most(experts) + 1) * UNIT


def route(nc, const, name, logits, experts, place, store_at, gates, units):
    E = experts
    with ExitStack() as ctx:
        k = Kit(nc, ctx, name)
        full = [P, NT, E]
        best = k.sb("best", [P, 2, NT])
        pick = k.sb("pick", [P, 2, NT, E])
        work = k.sb("work", full)
        rest = k.sb("rest", full)
        index = k.sb("index", [P, NT])
        node = k.sb("node", [P, NT])
        real = k.sb("real", [P, NT])
        spill = k.sb("spill", [P, 2, NT])
        seen = k.sb("seen", [P, NT + 1, E])
        count_i = k.sb("count_i", [P, E], I32)
        n_units = k.sb("n_units", [P, E])
        first = k.sb("first", [P, E])
        spot = k.sb("spot", [P, 2, NT])
        gap = k.sb("gap", [P, NT])
        grow = k.sb("grow", [P, NT])
        denom = k.sb("denom", [P, NT])
        ahead = k.ps("ahead", [P, 512])
        tile_sum = k.ps("tile_sum", [P, 512])
        s_ch, s_set, s_mm, s_pick, s_exp = (k.sem(n) for n in ("ch", "set", "mm", "pick", "exp"))
        block = ctx.enter_context(nc.Block())

        def over_tiles(a):
            return a.rearrange("p (o e) -> p o e", o=1).to_broadcast(full)

        def over_experts(a):
            return a.rearrange("p (t o) -> p t o", o=1).to_broadcast(full)

        @block.gpsimd
        def _(pool):
            pool.iota(node[:, :], pattern=[[P, NT]], base=0, channel_multiplier=1,
                      allow_small_or_imprecise_dtypes=True).then_inc(s_set, 1)

        @block.tensor
        def _(pe):
            pe.wait_ge(s_pick, 1)
            picks = work[:, :, :].rearrange("p t e -> p (t e)")
            nc.tensor.matmul(ahead[:, 0:NT * E], const["after"][:, :], picks, start=True, stop=True).then_inc(s_mm, 1)
            nc.tensor.matmul(tile_sum[:, 0:NT * E], const["ones"][:, :], picks, start=True, stop=True).then_inc(s_mm, 1)

        @block.scalar
        def _(act):
            act.wait_ge(s_exp, 1)
            act.activation(grow[:, :], gap[:, :], ACT.Exp).then_inc(s_exp, 1)

        @block.vector
        def _(dve):
            chain = Chain(dve, s_ch)
            link = chain.link
            ramp = const["ramp"]
            left = logits
            for c in range(2):
                link(dve.tensor_reduce(best[:, c, :], left[:, :, :], AX_X, ALU.max))
                link(dve.tensor_tensor(work[:, :, :], left[:, :, :], over_experts(best[:, c, :]), ALU.is_equal))
                link(dve.scalar_tensor_tensor(out=work[:, :, :], in0=work[:, :, :], scalar=-64.0,
                                              in1=over_tiles(ramp[:, 0:E]), op0=ALU.mult, op1=ALU.add))
                link(dve.tensor_reduce(index[:, :], work[:, :, :], AX_X, ALU.min))
                link(dve.tensor_scalar(index[:, :], index[:, :], 64.0, None, ALU.add))
                link(dve.tensor_tensor(pick[:, c, :, :], over_tiles(ramp[:, 0:E]), over_experts(index[:, :]), ALU.is_equal))
                if c == 0:
                    link(dve.scalar_tensor_tensor(out=rest[:, :, :], in0=pick[:, 0, :, :], scalar=LOWEST,
                                                  in1=logits[:, :, :], op0=ALU.mult, op1=ALU.add))
                    left = rest
            link(dve.tensor_tensor(gap[:, :], best[:, 1, :], best[:, 0, :], ALU.subtract))
            dve.sem_inc(s_exp, 1)
            dve.wait_ge(s_set, 1)
            link(dve.tensor_scalar(real[:, :], node[:, :], float(N), None, ALU.is_lt))
            for c in range(2):
                chain.mark(dve.tensor_tensor(pick[:, c, :, :], pick[:, c, :, :], over_experts(real[:, :]), ALU.mult))
            chain.wait()
            link(dve.tensor_tensor(work[:, :, :], pick[:, 0, :, :], pick[:, 1, :, :], ALU.add))
            dve.sem_inc(s_pick, 1)
            dve.wait_ge(s_exp, 2)
            link(dve.tensor_scalar(denom[:, :], grow[:, :], 1.0, None, ALU.add))
            link(dve.reciprocal(gates[:, 0, :], denom[:, :]))
            link(dve.tensor_tensor(gates[:, 1, :], grow[:, :], gates[:, 0, :], ALU.mult))
            link(dve.memset(seen[:, 0, :], 0.0))
            dve.wait_ge(s_mm, 2)
            for t in range(NT):
                link(dve.tensor_tensor(seen[:, t + 1, :], seen[:, t, :], tile_sum[:, t * E:(t + 1) * E], ALU.add))
            link(dve.tensor_scalar(n_units[:, :], seen[:, NT, :], UNIT - 1.0, None, ALU.add))
            link(dve.tensor_copy(count_i[:, :], n_units[:, :]))
            link(dve.tensor_scalar(count_i[:, :], count_i[:, :], 8, None, ALU.logical_shift_right))
            link(dve.tensor_scalar(n_units[:, :], count_i[:, :], 1.0, None, ALU.max))
            chain.mark(dve.tensor_copy(units[0:1, 0:E], n_units[0:1, :]))
            link(dve.tensor_tensor_scan(first[:, :], const["ones"][:, 0:E], n_units[:, :], 0.0, ALU.mult, ALU.add))
            link(dve.tensor_tensor(first[:, :], first[:, :], n_units[:, :], ALU.subtract))
            link(dve.tensor_scalar(first[:, :], first[:, :], float(UNIT), None, ALU.mult))
            link(dve.tensor_tensor(rest[:, :, :], seen[:, 0:NT, :], over_tiles(first[:, :]), ALU.add))
            link(dve.tensor_tensor(rest[:, :, :], rest[:, :, :], ahead[:, 0:NT * E].rearrange("p (t e) -> p t e", e=E), ALU.add))
            for c in range(2):
                link(dve.tensor_tensor(work[:, :, :], rest[:, :, :], pick[:, c, :, :], ALU.mult))
                link(dve.tensor_reduce(spot[:, c, :], work[:, :, :], AX_X, ALU.add))
                chain.mark(dve.tensor_copy(place[:, c, :], spot[:, c, :]))
                link(dve.tensor_scalar(spill[:, c, :], node[:, :], float(spill_row(E) - N + UNIT * c), None, ALU.add))
                link(dve.tensor_scalar(denom[:, :], real[:, :], -1.0, 1.0, ALU.mult, ALU.add))
                link(dve.tensor_tensor(spill[:, c, :], spill[:, c, :], denom[:, :], ALU.mult))
                link(dve.tensor_tensor(spot[:, c, :], spot[:, c, :], spill[:, c, :], ALU.add))
                link(dve.tensor_copy(store_at[:, c, :], spot[:, c, :]))


def run_experts(nc, const, name, experts, w1, b1, w2, b2, func, own, store_at, sorted_x, cleared, units):
    E, F = experts, w1.shape[2]
    M = F // P
    with ExitStack() as ctx:
        k = Kit(nc, ctx, name)
        w1_sb = k.sb("w1", [P, 2, 2, F])
        w2_sb = k.sb("w2", [P, 2, M, C])
        b1_sb = k.sb("b1", [P, 2, M])
        b2_sb = k.sb("b2", [P, 2, C])
        rows = k.sb("rows", [P, 2, C])
        turned = k.sb("turned", [P, 2, UNIT])
        hidden = k.sb("hidden", [P, M, UNIT])
        y = k.sb("y", [P, 2, C])
        primed = k.sb("primed", [1, 1])
        flipped = k.ps("flipped", [P, 2, UNIT])
        up = k.ps("up", [P, M, 512])
        down = k.ps("down", [P, 2, 512])
        (s_wfree, s_x, s_flip, s_turn, s_up, s_hid, s_down, s_y, s_store, s_ps, s_pt, s_pa, s_pv) = (
            k.sem(n) for n in ("wfree", "x", "flip", "turn", "up", "hid", "down", "y", "store", "ps", "pt", "pa", "pv"))
        s_wt, s_sorted = k.sem("wt"), k.pool_dma_sem("sorted")
        block = ctx.enter_context(nc.Block())
        most = units_most(E)

        def per_unit(eng, prepare, work):
            done = eng.alloc_register(f"{name}_{eng.engine.name}_done")
            eng.reg_mov(done, 0)
            with eng.Fori(0, E // 2) as pair:
                for b in range(2):
                    prepare(2 * pair + b, b)
                    n = eng.value_load(units[0:1, bass.ds(2 * pair + b, 1)], min_val=1, max_val=most)
                    with eng.Fori(0, n):
                        work(eng.snap(done, min_val=0, max_val=most - 1), b)
                        eng.reg_add(done, done, 1)
                    if eng is nc.vector:
                        hold(eng, s_y, 2 * eng.snap(done, min_val=0, max_val=most) + 2, s_pv)
                        eng.sem_inc(s_wfree, 1)
            return done

        @block.gpsimd
        def _(pool):
            pool.wait_ge(cleared, 16 * CLEARS)
            for c in range(2):
                for t in range(NT):
                    pool.indirect_dma_start(sorted_x[:, :], bass.IndirectOffsetOnAxis(ap=store_at[:, c, t:t + 1], axis=0),
                                            own[:, t, :], None).then_inc(s_sorted, 16)
            pool.wait_ge(s_sorted, 16 * 2 * NT)

        @block.sync
        def _(sp):
            def weights(e, b):
                at = bass.ds(e, 1)
                sp.dma_start(w1_sb[:, b, :, :], w1[at, :, :].rearrange("o (k p) n -> p (o k) n", p=P)).then_inc(s_wt, 16)
                sp.dma_start(w2_sb[:, b, :, :], w2[at, :, :].rearrange("o (k p) n -> p (o k) n", p=P)).then_inc(s_wt, 16)
                sp.dma_start(b1_sb[:, b, :], b1[at, :, :].rearrange("o p m -> p (o m)")).then_inc(s_wt, 16)
                sp.dma_start(b2_sb[:, b, :], b2[at, :].to_broadcast([P, C])).then_inc(s_wt, 16)

            def next_weights(e, b):
                hold(sp, s_wt, 64 * e + 64, s_ps)
                hold(sp, s_wfree, e + 2, s_ps)
                if b == 0:
                    weights(e + 1, 1)
                else:
                    with sp.If(e < E - 1):
                        weights(sp.snap(even, min_val=2, max_val=E - 2), 0)
                    sp.reg_add(even, even, 2)

            def work(u, b):
                hold(sp, s_y, 2 * u + 4, s_ps)
                sp.dma_start(sorted_x[bass.ds(u * UNIT, UNIT), :].rearrange("(h p) c -> p h c", p=P), y[:, :, :]).then_inc(s_store, 16)

            sp.dma_start(primed[:, :], b2[0:1, 0:1]).then_inc(s_store, 16)
            even = sp.alloc_register(f"{name}_even")
            sp.reg_mov(even, 2)
            weights(0, 0)
            done = per_unit(sp, next_weights, work)
            hold(sp, s_store, 16 * sp.snap(done, min_val=1, max_val=most) + 16, s_ps)

        @block.tensor
        def _(pe):
            def turn_over(u):
                hold(pe, s_x, 16 * u + 16, s_pt)
                hold(pe, s_turn, u + 1, s_pt)
                for h in range(2):
                    for c in range(2):
                        t = nc.tensor.transpose(flipped[:, c, h * P:(h + 1) * P], rows[:, h, c * P:(c + 1) * P], ident_of(const))
                t.then_inc(s_flip, 1)

            def work(u, b):
                hold(pe, s_turn, u + 2, s_pt)
                for m in range(M):
                    hold(pe, s_hid, M * u + m + 1, s_pt)
                    for c in range(2):
                        t = nc.tensor.matmul(up[:, m, 0:UNIT], w1_sb[:, b, c, m * P:(m + 1) * P], turned[:, c, :],
                                             start=(c == 0), stop=(c == 1))
                    t.then_inc(s_up, 1)
                turn_over(u + 1)
                for h in range(2):
                    hold(pe, s_y, 2 * u + h + 1, s_pt)
                    for m in range(M):
                        if h == 0:
                            hold(pe, s_hid, M * u + m + 1 + M, s_pt)
                        t = nc.tensor.matmul(down[:, h, 0:C], hidden[:, m, h * P:(h + 1) * P], w2_sb[:, b, m, :],
                                             start=(m == 0), stop=(m == M - 1))
                    t.then_inc(s_down, 1)

            pe.sem_inc(s_down, 2)
            turn_over(0)
            per_unit(pe, lambda e, b: hold(pe, s_wt, 64 * e + 64, s_pt), work)

        @block.scalar
        def _(act):
            def load(u):
                act.dma_start(rows[:, :, :], sorted_x[bass.ds(u * UNIT, UNIT), :].rearrange("(h p) c -> p h c", p=P)).then_inc(s_x, 16)

            def copy_turned(u):
                hold(act, s_flip, u + 1, s_pa)
                load(u + 1)
                act.activation(turned[:, :, :], flipped[:, :, :], ACT.Copy).then_inc(s_turn, 1)

            def work(u, b):
                hold(act, s_down, 2 * u + 2, s_pa)
                for m in range(M):
                    hold(act, s_up, M * u + m + 1, s_pa)
                    act.activation(hidden[:, m, :], up[:, m, 0:UNIT], func, bias=b1_sb[:, b, m:m + 1]).then_inc(s_hid, 1)
                copy_turned(u + 1)

            act.sem_inc(s_turn, 1)
            act.sem_inc(s_hid, M)
            act.wait_ge(s_sorted, 16 * 2 * NT)
            load(0)
            copy_turned(0)
            done = per_unit(act, lambda e, b: hold(act, s_wt, 64 * e + 64, s_pa), work)
            hold(act, s_x, 16 * act.snap(done, min_val=1, max_val=most) + 32, s_pa)

        @block.vector
        def _(dve):
            def work(u, b):
                hold(dve, s_store, 16 * u + 16, s_pv)
                for h in range(2):
                    hold(dve, s_down, 2 * u + h + 3, s_pv)
                    dve.tensor_tensor(y[:, h, :], down[:, h, 0:C], b2_sb[:, b, :], ALU.add).then_inc(s_y, 1)

            dve.sem_inc(s_y, 2)
            dve.sem_inc(s_wfree, 2)
            per_unit(dve, lambda e, b: hold(dve, s_wt, 64 * e + 64, s_pv), work)


def combine(nc, const, name, sorted_y, place, gates, own, x, out, table=None, gamma=None, beta=None, result=None):
    final = gamma is not None
    with ExitStack() as ctx:
        k = Kit(nc, ctx, name)
        y = k.sb("y", [P, NT, 2, C])
        gamma_sb = k.sb("gamma", [P, C])
        beta_sb = k.sb("beta", [P, C])
        zero_row = k.sb("zero_row", [1, C])
        moe = k.sb("moe", [P, GROUP, C])
        stats = k.sb("stats", [P, GROUP, 6])
        mean_var = k.sb("mean_var", [P, GROUP, 2])
        inverse = k.sb("inverse", [P, GROUP])
        shift = k.sb("shift", [P, GROUP])
        s_y = [k.pool_dma_sem(f"y{i}") for i in range(2)]
        s_w, s_zero, s_got, s_sqrt_go, s_sqrt, s_out, s_store, s_ch, s_ps, s_pa, s_pv, s_apply = (
            k.sem(n) for n in ("w", "zero", "got", "sqrt_go", "sqrt", "out", "store", "ch", "ps", "pa", "pv", "apply"))
        block = ctx.enter_context(nc.Block())

        @block.gpsimd
        def _(pool):
            def landed(g):
                n = GROUP if g < GROUPS else REST
                pool.wait_ge(s_y[g % 2], 32 * (GROUP * (g // 2) + n))
                pool.sem_inc(s_got, n)

            pool.memset(zero_row[:, :], 0.0).then_inc(s_zero, 1)
            for t in range(NT):
                for c in range(2):
                    pool.indirect_dma_start(y[:, t, c, :], None, sorted_y[:, :],
                                            bass.IndirectOffsetOnAxis(ap=place[:, c, t:t + 1], axis=0)
                                            ).then_inc(s_y[t // GROUP % 2], 16)
                if t % GROUP == 1 and t > GROUP:
                    landed(t // GROUP - 1)
            landed(GROUPS - 1)
            landed(GROUPS)

        @block.sync
        def _(sp):
            def store(t, n):
                hold(sp, s_out, t + n, s_ps)
                sp.dma_start(by_tile(result if final else table, t, n), tiles_of(out, t, n)).then_inc(s_store, 16)

            if final:
                sp.dma_start(gamma_sb[:, :], gamma.rearrange("(o n) -> o n", o=1).to_broadcast([P, C])).then_inc(s_w, 16)
                sp.dma_start(beta_sb[:, :], beta.rearrange("(o n) -> o n", o=1).to_broadcast([P, C])).then_inc(s_w, 16)
            with sp.Fori(0, GROUPS) as i:
                store(GROUP * i, GROUP)
            if final:
                sp.wait_ge(s_out, NT)
                sp.dma_start(result[(NT - 1) * P:N, :], out[0:LAST, NT - 1, :]).then_inc(s_store, 16)
            else:
                store(GROUP * GROUPS, REST)
                sp.wait_ge(s_zero, 1)
                sp.dma_start(table[PAD_ROW:PAD_ROW + 1, :], zero_row[:, :]).then_inc(s_w, 16)
                sp.wait_ge(s_w, 16)
            sp.wait_ge(s_store, 16 * (GROUPS + 1))

        @block.scalar
        def _(act):
            def root(t, n):
                hold(act, s_sqrt_go, t + GROUP, s_pa)
                act.activation(inverse[:, 0:n], mean_var[:, 0:n, 1], ACT.Sqrt, bias=const["eps"][:, 0:1]).then_inc(s_sqrt, GROUP)
                if not final:
                    apply_norm(act, s_apply, t, n, x, out, inverse, shift, s_out, s_pa)

            every_turn(act, None, root)

        @block.vector
        def _(dve):
            chain = Chain(dve, s_ch)
            if final:
                dve.wait_ge(s_w, 32)
                chain.link(dve.tensor_tensor(x[:, :, :], x[:, :, :], same_for(beta_sb, NT), ALU.add))
                chain.restart()

            def mix(t, n):
                moes, moe_tile = moe[:, 0:n, :], lambda u: moe[:, u, :]
                hold(dve, s_got, t + n, s_pv)
                for c in range(2):
                    for u in range(n):
                        row = y[:, bass.ds(t + u, 1), c, :].rearrange("p o c -> p (o c)")
                        chain.mark(dve.scalar_tensor_tensor(
                            out=moe[:, u, :] if final or c == 0 else tile_of(x, t + u), in0=row, scalar=gates[:, c, bass.ds(t + u, 1)],
                            in1=tile_of(own if final else x, t + u) if c == 0 else moe[:, u, :], op0=ALU.mult, op1=ALU.add))
                    chain.wait()
                if final:
                    normalise(dve, s_sqrt_go, s_sqrt, t + GROUP, chain, n, moe_tile, moe_tile, stats, mean_var, inverse, s_pv)
                    chain.link(dve.tensor_tensor(moes, moes, same_for(gamma_sb, n), ALU.mult))
                    chain.link(dve.tensor_tensor(tiles_of(out, t, n), moes, tiles_of(x, t, n), ALU.add))
                    dve.sem_inc(s_out, n)
                else:
                    hand_norm(dve, s_sqrt_go, s_sqrt, t + GROUP, chain, n, lambda u: tile_of(x, t + u),
                              stats, mean_var, inverse, shift, s_apply, s_pv)
                chain.restart()

            every_turn(dve, None, mix)


CLEARS = 8


def build(nc, x, src, dst,
          g_wp1, g_bp1, g_wm1, g_bm1, g_wm2, g_bm2, g_wm3, g_bm3, g_ln2_g, g_ln2_b, g_ln3_g, g_ln3_b,
          f_wgat, f_att_src, f_att_dst, f_bgat, f_ln_g, f_ln_b, f_w1, f_b1, f_w2, f_b2, f_edges,
          s_w, s_bl, s_g, s_b, m_gate, m_gate_b, m_w1, m_b1, m_w2, m_b2, m_g, m_b, result):
    with ExitStack() as ctx:
        def sb(name, shape, dt=F32):
            return ctx.enter_context(nc.sbuf_tensor(name, shape, dt))

        def dram(name, shape, dt=F32):
            return nc.dram_tensor(name, shape, dt, kind="Internal").ap()

        const = {"ident": sb("ident", [P, P]), "before": sb("before", [P, P]), "after": sb("after", [P, P]),
                 "ones": sb("ones", [P, P]), "ramp": sb("ramp", [P, P]), "row": sb("row", [P, 1]),
                 "zero16": sb("zero16", [P, P], BF16), "eps": sb("eps", [P, 1]), "zeros": sb("zeros", [P, C])}
        state = sb("state", [P, NT, C])
        ping = sb("ping", [P, NT, C])
        pong = sb("pong", [P, NT, C])
        narrow = sb("narrow", [P, NT, HE])
        scores = sb("scores", [P, NT, EXPERTS0])
        place = sb("place", [P, 2, NT], I32)
        gates = sb("gates", [P, 2, NT])
        store_at = sb("store_at", [P, 2, NT], I32)
        units = sb("units", [1, HE], I32)
        perm = sb("perm", [P, NT], I32)
        degree = sb("degree", [P, NT])
        has_edges, over_degree = sb("has_edges", [P, NT]), sb("over_degree", [P, NT])
        turns = sb("turns", [1, 2], I32)
        perm_f = sb("perm_f", [P, NT], I32)
        degree_f = sb("degree_f", [P, NT])
        turns_f = sb("turns_f", [1, 2], I32)

        edges, f_n = dst.shape[0], f_edges.shape[1]
        cap, cap_f = slot_capacity(edges, POOL_SLOTS), slot_capacity(f_n, SLOTS)
        slot_table, slot_table_f = dram("slot_table", [P, cap * POOL_SLOTS], I32), dram("slot_table_f", [P, cap_f * SLOTS], I32)
        block_tile, block_tile_f = dram("block_tile", [cap], I32), dram("block_tile_f", [cap_f], I32)
        ranked, ranked_f = dram("ranked", [NP, 3], I32), dram("ranked_f", [NP, 2], I32)
        segments = dram("segments", [edges // STEP, SPAN + STEP], I32)
        tables = [dram(f"table{i}", [PAD_ROW + 1, C]) for i in range(4)]
        gat_table = dram("gat_table", [PAD_ROW + 1, GROW])
        pooled = [dram(f"pooled{i}", [NP, C]) for i in range(2)]
        agg = dram("agg", [NP, HE])
        most_rows = spill_row(HE) + 2 * UNIT
        sorted_x = dram("sorted_x", [-(-most_rows // (CLEARS * P)) * CLEARS * P, C])
        cleared = ctx.enter_context(nc.semaphore("cleared"))
        x_loaded = ctx.enter_context(nc.semaphore("x_loaded"))

        build_constants(nc, const, state)
        sort_lists(nc, const, [
            EdgeList("A", dst, src, edges, 125, slot_table, block_tile, ranked, perm, degree, turns, POOL_SLOTS, segments,
                     has_edges, over_degree),
            EdgeList("B", f_edges[1, :], f_edges[0, :], f_n, P, slot_table_f, block_tile_f, ranked_f, perm_f, degree_f,
                     turns_f, SLOTS)],
                   lambda: start_transfers(nc, const, sorted_x, cleared, x, state, x_loaded))

        def pool_nodes(name, table, factor, into, op, init):
            gather_pass(nc, const, name, table, slot_table, block_tile, turns, perm, factor, into, op, init)

        node_layer(nc, const, "embed", "embed", None, None, g_wp1, g_bp1, None, None, state, ping, tables[0], x_loaded, pong)
        pool_nodes("p1", tables[0], None, pooled[0], ALU.max, 0.0)
        node_layer(nc, const, "mix1", "mix", ping, pooled[0], g_wm1, g_bm1, None, None, state, pong, tables[1])
        pool_nodes("p2", tables[1], None, pooled[1], ALU.max, 0.0)
        node_layer(nc, const, "mix2", "mixnorm", pong, pooled[1], g_wm2, g_bm2, g_ln2_g, g_ln2_b, state, ping, tables[2])
        pool_nodes("p3", tables[2], has_edges, pooled[0], ALU.max, LOWEST)
        node_layer(nc, const, "mix3", "enter", ping, pooled[0], g_wm3, g_bm3, g_ln3_g, g_ln3_b, state, pong)
        project(nc, const, "gat", pong, f_wgat, HE, narrow)
        attention(nc, const, "att", narrow, f_att_src, f_att_dst, f_bgat, f_ln_g, f_ln_b, slot_table_f, block_tile_f,
                  turns_f, perm_f, gat_table, agg, scores)
        route(nc, const, "r0", scores, EXPERTS0, place, store_at, gates, units)
        run_experts(nc, const, "e0", EXPERTS0, f_w1, f_b1, f_w2, f_b2, ACT.Gelu, pong, store_at, sorted_x, cleared, units)
        combine(nc, const, "c0", sorted_x, place, gates, pong, state, ping, tables[3])
        pool_nodes("p4", tables[3], over_degree, pooled[1], ALU.add, 0.0)
        node_layer(nc, const, "sage", "sage", ping, pooled[1], s_w, s_bl, s_g, s_b, state, pong)
        project(nc, const, "gate", pong, m_gate, HE, narrow, m_gate_b)
        route(nc, const, "r1", narrow, HE, place, store_at, gates, units)
        run_experts(nc, const, "e1", HE, m_w1, m_b1, m_w2, m_b2, ACT.Relu, pong, store_at, sorted_x, cleared, units)
        combine(nc, const, "c1", sorted_x, place, gates, pong, state, ping, None, m_g, m_b, result)


_INS = [
    "x", "src", "dst", "L0_gnn_Wp1", "L0_gnn_bp1", "L0_gnn_Wm1", "L0_gnn_bm1", "L0_gnn_Wm2", "L0_gnn_bm2", "L0_gnn_Wm3",
    "L0_gnn_bm3", "L0_gnn_ln2_g", "L0_gnn_ln2_b", "L0_gnn_ln3_g", "L0_gnn_ln3_b", "L0_ffn_W_gat", "L0_ffn_att_src",
    "L0_ffn_att_dst", "L0_ffn_b_gat", "L0_ffn_ln_gamma", "L0_ffn_ln_beta", "L0_ffn_W1", "L0_ffn_b1", "L0_ffn_W2",
    "L0_ffn_b2", "L0_ffn_edge_index", "L1_gnn_W", "L1_gnn_b_l", "L1_gnn_gamma", "L1_gnn_beta", "L1_ffn_gate_w",
    "L1_ffn_gate_b", "L1_ffn_w1", "L1_ffn_b1", "L1_ffn_w2", "L1_ffn_b2", "L1_ffn_gamma", "L1_ffn_beta",
]


def kernel(**inputs):
    import numpy as _np
    import concourse.bacc as _bacc
    from concourse import mybir as _mybir
    from concourse.bass_utils import run_bass_kernel_spmd as _run

    given = {n: _np.asarray(a) for n, a in inputs.items()}
    for n in ("Wp1", "Wm1", "Wm2", "Wm3"):
        given[f"L0_gnn_{n}"] = given[f"L0_gnn_{n}"].T
    given["L1_gnn_W"] = _np.concatenate([given["L1_gnn_W_r"].T, given["L1_gnn_W_l"].T])
    for n in ("L0_ffn_b1", "L1_ffn_b1"):
        e, f = given[n].shape
        given[n] = given[n].reshape(e, f // 128, 128).transpose(0, 2, 1)
    nc = _bacc.Bacc("TRN2", target_bir_lowering=False, num_devices=1)
    arrays, args = {}, []
    for name in _INS:
        a = _np.ascontiguousarray(given[name])
        arrays[f"in_{name}_dram"] = a
        args.append(nc.dram_tensor(f"in_{name}_dram", a.shape, _mybir.dt.from_np(a.dtype), kind="ExternalInput").ap())
    args.append(nc.dram_tensor("out_0_dram", (3125, 256), _mybir.dt.float32, kind="ExternalOutput").ap())
    build(nc, *args)
    r = _run(nc, [arrays], core_ids=[0])
    return r.results[0]["out_0_dram"]
```
